# Optimizing a Trainium2 kernel written in Bass

```python
import numpy as np
import jax
import jax.numpy as jnp

def _softmax(x, axis=-1):
    return jax.nn.softmax(x, axis=axis)

def _gelu(x):
    return jax.nn.gelu(x, approximate=True)

def _silu(x):
    return jax.nn.silu(x)

def _sigmoid(x):
    return jax.nn.sigmoid(x)

def _layernorm(x, axis=-1, eps=1e-05):
    m = jnp.mean(x, axis=axis, keepdims=True)
    v = jnp.var(x, axis=axis, keepdims=True)
    return (x - m) / jnp.sqrt(v + eps)

def _scatter_add(tgt, idx, src, axis=0):
    return tgt.at[idx].add(src)

def _segment_sum(src, seg, n):
    return jax.ops.segment_sum(src, seg, n)
kernel_name = 'mk_xattn_ffn_d1_seqx_r2_897636'

def setup_inputs(seed: int=0):
    np.random.seed(seed)
    _w = jnp.asarray

    def _rec_inputs():
        import jax
        import jax.numpy as jnp
        _rk = jax.random.key(seed)
        x = 7.22e-05 + 1 * jax.random.normal(jax.random.fold_in(_rk, 1), (4, 1024, 1024), jnp.float32)
        _lenS = 1024 - jax.random.randint(jax.random.fold_in(_rk, 7), (4,), 0, max(1, 1024 // 4) + 1, jnp.int32)
        _lenS2 = 1024 - jax.random.randint(jax.random.fold_in(_rk, 8), (4,), 0, max(1, 1024 // 4) + 1, jnp.int32)
        _ctx_1024P = jax.random.normal(jax.random.fold_in(_rk, 11), (4, 16, 512), jnp.float32)
        _ctx_1024c = jax.random.dirichlet(jax.random.fold_in(_rk, 511), 0.3 * jnp.ones((16,), jnp.float32), (4, 1024))
        _ctx_1024t = jnp.einsum('bsk,bkd->bsd', _ctx_1024c, _ctx_1024P)
        _ctx_1024t = _ctx_1024t * jax.lax.rsqrt(jnp.mean(jnp.square(_ctx_1024t)) + 1e-12) * 0.953939
        ctx_1024 = 2.81802e-05 + 1.00001 * (_ctx_1024t + 0.3 * jax.random.normal(jax.random.fold_in(_rk, 611), (4, 1024, 512), jnp.float32))
        return (x, ctx_1024)
    x, ctx_1024 = _rec_inputs()

    def _L0_xattn_setup():
        import jax, jax.numpy as jnp
        import numpy as np
        key = jax.random.key(seed)
        ks = jax.random.split(key, 6)
        B, L, N, C, D = (8, 256, 1024, 512, 128)
        return {'teacher_logits': jax.random.normal(ks[0], (B, L, N), dtype=jnp.float32), 'teacher_features': jax.random.normal(ks[1], (B, N, C), dtype=jnp.float32), 'Wq': jax.random.normal(ks[2], (D, C), dtype=jnp.float32) * (1.0 / np.sqrt(C)), 'bq': jnp.zeros((D,), dtype=jnp.float32), 'Wk': jax.random.normal(ks[3], (D, C), dtype=jnp.float32) * (1.0 / np.sqrt(C)), 'bk': jnp.zeros((D,), dtype=jnp.float32)}
    _L0_xattn_all = _L0_xattn_setup()
    _L0_xattn_in = {k: v for k, v in _L0_xattn_all.items() if k in ('Wq', 'bq', 'Wk', 'bk')}
    del _L0_xattn_all

    def _L0_ffn_setup():
        import jax, jax.numpy as jnp
        import numpy as np
        BS, SLEN, DIM = (2, 1024, 1024)
        HIDDEN = 704
        E = 8
        TOP_K = 2
        ROUTE_SCALE = 1.0

        def _grouped_swiglu(xr, w1, w2, w3, group_sizes):
            xb = xr.astype(jnp.bfloat16)
            w1t = jnp.swapaxes(w1, 1, 2).astype(jnp.bfloat16)
            w3t = jnp.swapaxes(w3, 1, 2).astype(jnp.bfloat16)
            w2t = jnp.swapaxes(w2, 1, 2).astype(jnp.bfloat16)
            h = jax.nn.silu(jax.lax.ragged_dot(xb, w1t, group_sizes))
            h = h * jax.lax.ragged_dot(xb, w3t, group_sizes)
            return jax.lax.ragged_dot(h, w2t, group_sizes).astype(xr.dtype)
        key = jax.random.key(seed)
        ks = jax.random.split(key, 9)
        s = 0.02
        return {'x': jax.random.normal(ks[0], (BS, SLEN, DIM), jnp.float32), 'gate_w': jax.random.normal(ks[1], (E, DIM), jnp.float32) * s, 'w1': jax.random.normal(ks[2], (E, HIDDEN, DIM), jnp.float32) * s, 'w2': jax.random.normal(ks[3], (E, DIM, HIDDEN), jnp.float32) * s, 'w3': jax.random.normal(ks[4], (E, HIDDEN, DIM), jnp.float32) * s, 'sw1': jax.random.normal(ks[5], (HIDDEN, DIM), jnp.float32) * s, 'sw2': jax.random.normal(ks[6], (DIM, HIDDEN), jnp.float32) * s, 'sw3': jax.random.normal(ks[7], (HIDDEN, DIM), jnp.float32) * s, 'expert_bias': jnp.zeros((E,), jnp.float32)}
    _L0_ffn_all = _L0_ffn_setup()
    _L0_ffn_in = {k: v for k, v in _L0_ffn_all.items() if k in ('gate_w', 'w1', 'w2', 'w3', 'sw1', 'sw2', 'sw3', 'expert_bias')}
    del _L0_ffn_all
    return {'x': x, 'ctx_1024': ctx_1024, 'L0_xattn_Wq': _L0_xattn_in['Wq'], 'L0_xattn_bq': _L0_xattn_in['bq'], 'L0_xattn_Wk': _L0_xattn_in['Wk'], 'L0_xattn_bk': _L0_xattn_in['bk'], 'L0_ffn_gate_w': _L0_ffn_in['gate_w'], 'L0_ffn_w1': _L0_ffn_in['w1'], 'L0_ffn_w2': _L0_ffn_in['w2'], 'L0_ffn_w3': _L0_ffn_in['w3'], 'L0_ffn_sw1': _L0_ffn_in['sw1'], 'L0_ffn_sw2': _L0_ffn_in['sw2'], 'L0_ffn_sw3': _L0_ffn_in['sw3'], 'L0_ffn_expert_bias': _L0_ffn_in['expert_bias']}

def reference(x, ctx_1024, L0_xattn_Wq, L0_xattn_bq, L0_xattn_Wk, L0_xattn_bk, L0_ffn_gate_w, L0_ffn_w1, L0_ffn_w2, L0_ffn_w3, L0_ffn_sw1, L0_ffn_sw2, L0_ffn_sw3, L0_ffn_expert_bias):
    import jax
    import jax.numpy as jnp

    def _L0_xattn_ref(teacher_logits, teacher_features, Wq, bq, Wk, bk):
        import jax, jax.numpy as jnp
        import numpy as np
        query = jnp.einsum('bnc,dc->bnd', teacher_features, Wq) + bq
        key = jnp.einsum('bnc,dc->bnd', teacher_features, Wk) + bk
        energy = jnp.einsum('bnd,bmd->bnm', query, key)
        attention = jax.nn.softmax(energy, axis=-1)
        x_m = jnp.einsum('bln,bmn->blm', teacher_logits, attention)
        return x_m

    def _L0_ffn_ref(x, gate_w, w1, w2, w3, sw1, sw2, sw3, expert_bias):
        import jax, jax.numpy as jnp
        import numpy as np
        BS, SLEN, DIM = (2, 1024, 1024)
        HIDDEN = 704
        E = 8
        TOP_K = 2
        ROUTE_SCALE = 1.0

        def _grouped_swiglu(xr, w1, w2, w3, group_sizes):
            xb = xr.astype(jnp.bfloat16)
            w1t = jnp.swapaxes(w1, 1, 2).astype(jnp.bfloat16)
            w3t = jnp.swapaxes(w3, 1, 2).astype(jnp.bfloat16)
            w2t = jnp.swapaxes(w2, 1, 2).astype(jnp.bfloat16)
            h = jax.nn.silu(jax.lax.ragged_dot(xb, w1t, group_sizes))
            h = h * jax.lax.ragged_dot(xb, w3t, group_sizes)
            return jax.lax.ragged_dot(h, w2t, group_sizes).astype(xr.dtype)
        bs, slen, dim = x.shape
        xt = x.reshape(bs * slen, dim)
        scores = jax.nn.sigmoid((xt @ gate_w.T).astype(jnp.float32))
        _, sel = jax.lax.top_k(scores + expert_bias[None, :], TOP_K)
        top_scores = jnp.take_along_axis(scores, sel, axis=1) * ROUTE_SCALE
        sel_flat = sel.reshape(-1)
        num_tokens_per_expert = jnp.zeros((E,), jnp.int32).at[sel_flat].add(1)
        order = jnp.argsort(sel_flat, stable=True)
        scores_sorted = top_scores.reshape(-1)[order].astype(x.dtype)
        tok_idx = order // TOP_K
        routed_in = xt[tok_idx] * scores_sorted[:, None]
        routed_out = _grouped_swiglu(routed_in, w1, w2, w3, num_tokens_per_expert)
        shared = jax.nn.silu(xt @ sw1.T) * (xt @ sw3.T) @ sw2.T
        out = shared.at[tok_idx].add(routed_out)
        return out.reshape(bs, slen, dim)
    x = x + _L0_xattn_ref(_layernorm(x, axis=-1), ctx_1024, L0_xattn_Wq, L0_xattn_bq, L0_xattn_Wk, L0_xattn_bk)
    x = x + _L0_ffn_ref(_layernorm(x, axis=-1), L0_ffn_gate_w, L0_ffn_w1, L0_ffn_w2, L0_ffn_w3, L0_ffn_sw1, L0_ffn_sw2, L0_ffn_sw3, L0_ffn_expert_bias)
    return x

_drawn_inputs = setup_inputs


def setup_inputs(seed=0):
    import zlib

    import numpy as np

    out = dict(_drawn_inputs(seed))
    spreads = {'L0_xattn_bq': (0.0, 0.1), 'L0_xattn_bk': (0.0, 0.1), 'L0_ffn_expert_bias': (0.0, 0.1)}
    factors = {}
    for name, (base, spread) in spreads.items():
        noise = np.random.default_rng([zlib.crc32(name.encode()), seed]).standard_normal(out[name].shape)
        drawn = base * np.exp(spread * noise) if base else spread * noise
        out[name] = jnp.asarray(drawn.astype(out[name].dtype))
    for name, factor in factors.items():
        out[name] = (out[name] * factor).astype(out[name].dtype)
    return out
```

```python
from contextlib import ExitStack

import numpy as np

import concourse.bass as bass
import concourse.mybir as mybir
from concourse.alu_op_type import AluOpType as ALU

F32 = mybir.dt.float32
F32R = mybir.dt.float32r
BF16 = mybir.dt.bfloat16
I32 = mybir.dt.int32
ACT = mybir.ActivationFunctionType
AX = mybir.AxisListType.X

P = 128
B, L, D = 4, 1024, 1024
TOK = B * L
NT = TOK // P
C, DH = 512, 128
CC = C // P
DC = D // P
BT = L // P
E, HID = 8, 704
HALF = HID // 2
HC = -(-HID // P)
HTAIL = HID - (HC - 1) * P
TOPK = 2
REG = TOK + P
ET = TOPK * TOK // P + E - 1
IDLE = E - 1
GROWS = E * REG + IDLE * P
EPS = 1e-5
DMA_RING = 8192
GROUP = 512
LOW = -1e30


class Count:

    def __init__(self, ctx, nc, name, per=1, first=0, lead=24):
        self.sem = ctx.enter_context(nc.semaphore(name))
        self.per, self.first, self.lead = per, first, lead

    def prime(self, eng):
        eng.sem_inc(self.sem, self.per * self.lead)

    def wait(self, eng, tile, k=None):
        k = self.per if k is None else k
        eng.wait_ge(self.sem, (tile - self.first + self.lead) * self.per + k)

    def inc(self, ins):
        ins.then_inc(self.sem, 1)


class Loads:

    def __init__(self, ctx, nc, name, n=1, first=0, lead=4):
        self.sems = [ctx.enter_context(nc.semaphore(f"{name}{p}")) for p in (0, 1)]
        self.n, self.first, self.lead = n, first // 2, lead

    def prime(self, eng):
        for s in self.sems:
            eng.sem_inc(s, 16 * self.n * self.lead)

    def wait(self, eng, tile):
        eng.wait_ge(self.sems[tile.par], (tile.half - self.first + 1 + self.lead) * 16 * self.n)

    def inc(self, ins, tile):
        ins.then_inc(self.sems[tile.par], 16)


class Tile:

    def __init__(self, half, par):
        self.half, self.par = half, par
        self.at = half * 2 + par

    def __add__(self, n):
        q, par = divmod(self.par + n, 2)
        return Tile(self.half + q, par)

    def __sub__(self, n):
        return self + (-n)


def settled(eng, spare):
    eng.sem_inc(spare, 1)


def pipeline(eng, stages, body):
    lo = min(a - o for o, a, b in stages.values())
    hi = max(b - o for o, a, b in stages.values())
    lo -= lo % 2
    shift = -lo // 2

    def on(s):
        return frozenset(n for n, (o, a, b) in stages.items() if a <= s + o < b)

    pairs = [(on(s), on(s + 1)) for s in range(lo, hi, 2)]
    at = 0
    while at < len(pairs):
        end = at
        while end < len(pairs) and pairs[end] == pairs[at]:
            end += 1

        def both(half):
            for par in (0, 1):
                if pairs[at][par]:
                    body(Tile(half - shift, par), pairs[at][par])

        if end - at == 1:
            both(at)
        else:
            with eng.Fori(at, end) as half:
                both(half)
        at = end


def build(nc, x, ctxt, wq, wk, bq, bk, gate_w, ebias, w13, w2, sw13, sw2, out):
    x1_d = nc.dram_tensor("x1_d", [TOK, D], F32, kind="Internal").ap()
    rows_d = nc.dram_tensor("rows_d", [GROWS, D], BF16, kind="Internal").ap()
    y_d = nc.dram_tensor("y_d", [ET * P, D], BF16, kind="Internal").ap()
    q_d, k_d = (nc.dram_tensor(n, [NT, P, P], F32, kind="Internal").ap() for n in ("q_d", "k_d"))
    with ExitStack() as ctx:
        def keep(name, shape, dt):
            return ctx.enter_context(nc.sbuf_tensor(name, shape, dt))

        kept = {
            "ident_f": keep("ident_f", [P, P], F32),
            "ident_b": keep("ident_b", [P, P], BF16),
            "ones_b": keep("ones_b", [P, P], BF16),
            "dest_all": keep("dest_all", [P, NT, TOPK], F32),
            "slot_all": keep("slot_all", [P, NT, TOPK], I32),
            "stat_all": keep("stat_all", [P, NT, 2], F32),
            "ends": keep("ends_i", [1, E], I32),
            "spare": ctx.enter_context(nc.semaphore("spare")),
            "seen": [keep(f"seen{p}", [P, E], BF16) for p in (0, 1)],
        }
        project(nc, ctx, ctxt, (wq, wk), (bq, bk), (q_d, k_d))
        attention(nc, ctx, kept, x, q_d, k_d, gate_w, ebias, x1_d, rows_d)
        table = keep("table", [1, 2, P], I32)
        plan(nc, ctx, kept, table, rows_d)
        routed(nc, ctx, kept, table, w13, w2, rows_d, y_d)
        shared(nc, ctx, kept, sw13, sw2, x1_d, y_d, out)


def project(nc, sems, ctxt, weights, biases, outs):
    with ExitStack() as ctx:
        def sb(name, shape, dt):
            return ctx.enter_context(nc.sbuf_tensor(name, shape, dt))

        def pair(name, shape, dt):
            return [sb(f"{name}{p}", shape, dt) for p in (0, 1)]

        NG = TOK // GROUP
        raw = sb("raw", [P, 2, CC, DH], F32)
        w_h, w_l = sb("w_h", [P, 2, CC, DH], F32R), sb("w_l", [P, 2, CC, DH], F32R)
        bias = sb("bias", [P, 2], F32)
        cf = pair("cf", [P, CC, GROUP], F32)
        ch, cl = pair("ch", [P, CC, GROUP], F32R), pair("cl", [P, CC, GROUP], F32R)
        res = pair("res", [P, 2, GROUP], F32)
        acc = [ctx.enter_context(nc.psum_tensor(f"acc{p}", [P, 2, GROUP], F32)) for p in (0, 1)]

        d_w = sems.enter_context(nc.semaphore("d_w"))
        c_w = sems.enter_context(nc.semaphore("c_w"))
        d_c = Loads(sems, nc, "d_c")
        d_res = Loads(sems, nc, "d_res", n=2)
        a_hi = Count(sems, nc, "a_hi")
        v_lo = Count(sems, nc, "v_lo")
        p_acc = Count(sems, nc, "p_acc")
        a_res = Count(sems, nc, "a_res")

        with nc.Block() as block:
            @block.sync
            def _(eng):
                d_c.prime(eng)
                for i in (0, 1):
                    eng.dma_start(raw[:, i], weights[i]).then_inc(d_w, 16)
                    eng.dma_start(bias[:, i:i + 1], biases[i]).then_inc(d_w, 16)

                def step(now, on):
                    if "load" in on:
                        t = now + 2
                        a_hi.wait(eng, t.at - 2)
                        v_lo.wait(eng, t.at - 2)
                        d_c.inc(eng.dma_start(cf[t.par][:], ctxt[t.at]), t)
                    if "out" in on:
                        a_res.wait(eng, now.at)
                        for i in (0, 1):
                            d_res.inc(eng.dma_start(
                                outs[i][bass.ts(now.at, GROUP // P)].rearrange("t p n -> p t n"),
                                res[now.par][:, i].rearrange("p (t n) -> p t n", n=P)), now)

                pipeline(eng, {"load": (2, 0, NG), "out": (0, 0, NG)}, step)
                for t in (NG - 2, NG - 1):
                    d_res.wait(eng, Tile(t // 2, t % 2))

            @block.scalar
            def _(eng):
                a_hi.prime(eng)
                a_res.prime(eng)
                d_res.prime(eng)
                eng.wait_ge(d_w, 16 * 4)
                eng.copy(w_h[:], raw[:]).then_inc(c_w, 1)

                def step(now, on):
                    if "hi" in on:
                        t = now + 1
                        d_c.wait(eng, t)
                        p_acc.wait(eng, t.at - 2)
                        a_hi.inc(eng.copy(ch[t.par][:], cf[t.par][:]))
                    if "res" in on:
                        p_acc.wait(eng, now.at)
                        d_res.wait(eng, now - 2)
                        eng.activation(res[now.par][:, 0], acc[now.par][:, 0], ACT.Identity, bias=bias[:, 0:1])
                        a_res.inc(eng.activation(res[now.par][:, 1], acc[now.par][:, 1], ACT.Identity,
                                                 bias=bias[:, 1:2]))

                pipeline(eng, {"hi": (1, 0, NG), "res": (0, 0, NG)}, step)

            @block.vector
            def _(eng):
                v_lo.prime(eng)
                eng.wait_ge(c_w, 1)
                eng.tensor_tensor(w_l[:], raw[:], w_h[:].bitcast(F32), ALU.subtract).then_inc(c_w, 1)

                def step(now, on):
                    a_hi.wait(eng, now.at)
                    v_lo.inc(eng.tensor_tensor(cl[now.par][:], cf[now.par][:], ch[now.par][:].bitcast(F32),
                                               ALU.subtract))

                pipeline(eng, {"lo": (0, 0, NG)}, step)

            @block.tensor
            def _(eng):
                p_acc.prime(eng)
                eng.wait_ge(c_w, 2)

                def step(now, on):
                    v_lo.wait(eng, now.at)
                    a_res.wait(eng, now.at - 2)
                    for i in (0, 1):
                        for c in range(CC):
                            for w, v in ((w_h, ch), (w_h, cl), (w_l, ch)):
                                ins = eng.matmul(acc[now.par][:, i], w[:, i, c, :], v[now.par][:, c, :],
                                                 start=(c == 0 and w is w_h and v is ch),
                                                 stop=(c == CC - 1 and w is w_l))
                    p_acc.inc(ins)

                pipeline(eng, {"mm": (0, 0, NG)}, step)


def attention(nc, sems, kept, x, q_d, k_d, gate_w, ebias, x1_d, rows_d):
    with ExitStack() as ctx:
        def sb(name, shape, dt):
            return ctx.enter_context(nc.sbuf_tensor(name, shape, dt))

        def ps(name, shape, dt):
            return ctx.enter_context(nc.psum_tensor(name, shape, dt))

        def count(name, **kw):
            return Count(sems, nc, name, **kw)

        def pair(name, shape, dt):
            return [sb(f"{name}{p}", shape, dt) for p in (0, 1)]

        ident_f, ident_b, ones_b = kept["ident_f"], kept["ident_b"], kept["ones_b"]
        dest_all, stat_all, seen = kept["dest_all"], kept["stat_all"], kept["seen"]

        before = sb("before", [P, P], BF16)
        gw = sb("gw", [P, DC, E], F32)
        eb = sb("eb", [P, E], F32)
        rank8 = sb("rank8", [P, E], F32)
        region = sb("region", [P, E], F32)
        eps = sb("eps", [P, 1], F32)
        half_neg = sb("half_neg", [P, 1], F32)

        qf, kf = pair("qf", [P, P], F32), pair("kf", [P, P], F32)
        q_h, q_l = pair("q_h", [P, P], F32R), pair("q_l", [P, P], F32R)
        k_h, k_l = sb("k_h", [P, 2 * L], F32R), sb("k_l", [P, 2 * L], F32R)
        att_h, att_l = sb("att_h", [P, 2 * BT, L], F32R), sb("att_l", [P, 2 * BT, L], F32R)
        expd, att = sb("expd", [P, L], F32), sb("att", [P, L], F32)
        nmax, rsum, rinv = (pair(n, [P, 1], F32) for n in ("nmax", "rsum", "rinv"))

        xs = pair("xs", [P, D], F32)
        xr = sb("xr", [P, D], F32)
        xn = sb("xn", [P, D], F32)
        xnt_h, xnt_l = pair("xnt_h", [P, DC, P], F32R), pair("xnt_l", [P, DC, P], F32R)
        x1 = sb("x1", [P, D], F32)
        x2 = pair("x2", [P, D], F32)
        x2t = sb("x2t", [P, DC, P], F32)
        bs = [pair("bs0", [P, 2, 6], F32), pair("bs1", [P, 2, 6], F32)]
        mv = [pair("mv0", [P, 2], F32), pair("mv1", [P, 2], F32)]
        ve = [pair("ve0", [P, 1], F32), pair("ve1", [P, 1], F32)]
        rstd = [pair("rstd0", [P, 1], F32), pair("rstd1", [P, 1], F32)]

        logit = pair("logit", [P, E], F32)
        rank = pair("rank", [P, E], F32)
        sig_e = pair("sig_e", [P, E], F32)
        score = pair("score", [P, E], F32)
        sel = pair("sel", [P, E], F32)
        top = pair("top", [P, 4], F32)
        cand = pair("cand", [P, E], F32)
        one_hot = [pair("hot0_", [P, E], F32), pair("hot1_", [P, E], F32)]
        mask = pair("mask", [P, E], BF16)
        junk = pair("junk", [P, E], F32)
        wsc = pair("wsc", [P, TOPK], F32)
        destf = pair("destf", [P, TOPK], F32)
        dest = [pair("dest0_", [P, 1], I32), pair("dest1_", [P, 1], I32)]
        disp = [sb("disp0", [P, D], BF16), sb("disp1", [P, D], BF16)]

        o_ps = [ps(f"o_ps{p}", [P, L], F32) for p in (0, 1)]
        e_ps = ps("e_ps", [P, L], F32)
        t_ps = ps("t_ps", [P, L], F32)
        gate_ps, rank_ps = t_ps[:, 0:E], t_ps[:, E:2 * E]

        d_const = sems.enter_context(nc.semaphore("d_const"))
        d_idle = sems.enter_context(nc.semaphore("d_idle"))
        d_x, d_xr = Loads(sems, nc, "d_x"), Loads(sems, nc, "d_xr")
        d_q, d_k = Loads(sems, nc, "d_q"), Loads(sems, nc, "d_k")
        d_x1 = Loads(sems, nc, "d_x1")
        d_disp = Loads(sems, nc, "d_disp", n=TOPK, lead=0)
        c_setup = sems.enter_context(nc.semaphore("c_setup"))
        spare = kept["spare"]
        v_xstat = count("v_xstat", per=3)
        g_rstd = [count("g_rstd0", per=2), count("g_rstd1", per=2)]
        v_xn = count("v_xn")
        p_xt = count("p_xt")
        a_xth = count("a_xth")
        v_xtl = count("v_xtl")
        p_mm = count("p_mm")
        v_x1 = count("v_x1", per=4)
        v_x2 = count("v_x2")
        v_keep = count("v_keep", per=2)
        p_x2t = count("p_x2t")
        a_x2t = count("a_x2t")
        p_gate = count("p_gate")
        v_gcopy = count("v_gcopy")
        a_sig = count("a_sig")
        v_route = count("v_route", per=15)
        p_rank = count("p_rank")
        v_rcopy = count("v_rcopy")
        v_dest = count("v_dest", per=6)
        a_disp = count("a_disp")
        a_qh, a_kh = count("a_qh"), count("a_kh")
        g_ql, g_kl = count("g_ql"), count("g_kl")
        p_en = count("p_en")
        v_max = count("v_max")
        a_exp = count("a_exp")
        v_inv = count("v_inv")
        a_att = count("a_att")
        p_att = count("p_att")
        a_atth = count("a_atth")
        v_attl = count("v_attl")

        K_LEAD = 2 * BT + 2
        E_LEAD = BT + 2

        def columns(half, t):
            return half[:, bass.ds(t.at & BT, BT), bass.ds((t.at & (BT - 1)) * P, P)]

        with nc.Block() as block:
            @block.sync
            def _(eng):
                for s in (d_x, d_xr, d_q, d_k):
                    s.prime(eng)
                eng.dma_start(gw[:], gate_w).then_inc(d_const, 16)
                eng.dma_start(eb[:], ebias.broadcast_to([P, E])).then_inc(d_const, 16)
                eng.wait_ge(c_setup, 3)
                for i in range(IDLE):
                    r = E * REG + i * P
                    eng.dma_start(rows_d[r:r + P, :], disp[0][:]).then_inc(d_idle, 16)

                def step(now, on):
                    if "st" in on:
                        t = now - 1
                        v_x1.wait(eng, t.at, 1)
                        d_x1.inc(eng.dma_start(x1_d[bass.ts(t.at, P), :], x1[:]), t)
                    if "xr" in on:
                        t = now
                        v_x1.wait(eng, t.at - 1, 1)
                        d_xr.inc(eng.dma_start(xr[:], x[t.at]), t)
                    if "x" in on:
                        t = now + 3
                        v_xn.wait(eng, t.at - 2)
                        d_x.inc(eng.dma_start(xs[t.par][:], x[t.at]), t)
                    for name, off, dst, src, sem, hi, lo in (("k", K_LEAD + 1, kf, k_d, d_k, a_kh, g_kl),
                                                             ("q", E_LEAD + 2, qf, q_d, d_q, a_qh, g_ql)):
                        if name in on:
                            t = now + off
                            hi.wait(eng, t.at - 2)
                            lo.wait(eng, t.at - 2)
                            sem.inc(eng.dma_start(dst[t.par][:], src[t.at]), t)

                pipeline(eng, {"k": (K_LEAD + 1, 0, NT), "q": (E_LEAD + 2, 0, NT), "x": (3, 0, NT),
                               "xr": (0, 0, NT), "st": (-1, 0, NT)}, step)
                eng.wait_ge(d_idle, 16 * IDLE)
                for t in (NT - 2, NT - 1):
                    d_x1.wait(eng, Tile(t // 2, t % 2))

            @block.gpsimd
            def _(eng):
                for s in (*g_rstd, g_ql, g_kl):
                    s.prime(eng)
                eng.memset(ident_f[:], 0.0).then_inc(c_setup, 1)
                eng.memset(ones_b[:], 1.0).then_inc(c_setup, 1)
                eng.memset(disp[0][:], 0.0).then_inc(c_setup, 1)
                eng.memset(half_neg[:], -0.5).then_inc(c_setup, 1)
                eng.memset(eps[:], EPS).then_inc(c_setup, 1)
                for p in (0, 1):
                    eng.memset(seen[p][:], 0.0).then_inc(c_setup, 1)
                eng.wait_ge(c_setup, 2)
                eng.affine_select(out=ident_f[:], in_=ident_f[:], compare_op=ALU.not_equal, fill=1.0, base=0,
                                  pattern=[[-1, P]], channel_multiplier=1).then_inc(c_setup, 1)
                eng.affine_select(out=before[:], in_=ones_b[:], compare_op=ALU.is_gt, fill=0.0, base=0,
                                  pattern=[[1, P]], channel_multiplier=-1).then_inc(c_setup, 1)
                eng.iota(rank8[:], pattern=[[1, E]], base=-E, channel_multiplier=0,
                         allow_small_or_imprecise_dtypes=True).then_inc(c_setup, 1)
                eng.iota(region[:], pattern=[[REG, E]], base=0, channel_multiplier=0,
                         allow_small_or_imprecise_dtypes=True).then_inc(c_setup, 1)
                eng.wait_ge(c_setup, 8)
                eng.tensor_copy(ident_b[:], ident_f[:]).then_inc(c_setup, 1)

                def step(now, on):
                    for i, name, off in ((1, "r1", -1), (0, "r0", 2)):
                        if name in on:
                            t = now + off
                            (v_x1 if i else v_xstat).wait(eng, t.at)
                            (v_x2 if i else v_xn).wait(eng, t.at - 2)
                            if i:
                                v_keep.wait(eng, t.at - 2)
                            g_rstd[i].inc(eng.tensor_tensor(ve[i][t.par][:], mv[i][t.par][:, 1:2], eps[:], ALU.add))
                            g_rstd[i].wait(eng, t.at, 1)
                            g_rstd[i].inc(eng.tensor_tensor(rstd[i][t.par][:], ve[i][t.par][:], half_neg[:],
                                                            ALU.pow))
                    if "disp" in on:
                        t = now - 3
                        a_disp.wait(eng, t.at)
                        v_dest.wait(eng, t.at)
                        for k in range(TOPK):
                            settled(eng, spare)
                            d_disp.inc(eng.indirect_dma_start(
                                rows_d, bass.IndirectOffsetOnAxis(ap=dest[k][t.par][:, 0:1], axis=0),
                                disp[k][:], None), t)
                    if "k" in on:
                        t = now + K_LEAD
                        at = bass.ts(t.at & (2 * BT - 1), P)
                        a_kh.wait(eng, t.at)
                        g_kl.inc(eng.tensor_tensor(k_l[:, at], kf[t.par][:], k_h[:, at].bitcast(F32), ALU.subtract))
                    if "q" in on:
                        t = now + E_LEAD + 1
                        a_qh.wait(eng, t.at)
                        g_ql.inc(eng.tensor_tensor(q_l[t.par][:], qf[t.par][:], q_h[t.par][:].bitcast(F32),
                                                   ALU.subtract))

                pipeline(eng, {"k": (K_LEAD, 0, NT), "q": (E_LEAD + 1, 0, NT), "r1": (-1, 0, NT),
                               "r0": (2, 0, NT), "disp": (-3, 0, NT)}, step)
                for t in (NT - 2, NT - 1):
                    d_disp.wait(eng, Tile(t // 2, t % 2))

            @block.scalar
            def _(eng):
                for s in (a_xth, a_x2t, a_sig, a_disp, a_qh, a_kh, a_exp, a_att, a_atth):
                    s.prime(eng)
                def step(now, on):
                    if "xt" in on:
                        t = now + 1
                        p_xt.wait(eng, t.at)
                        p_mm.wait(eng, t.at - 2)
                        a_xth.inc(eng.copy(xnt_h[t.par][:], t_ps[:]))
                    if "ta" in on:
                        t = now + E_LEAD - 2
                        p_att.wait(eng, t.at)
                        p_mm.wait(eng, t.at - BT - 1)
                        a_atth.inc(eng.copy(columns(att_h, t), t_ps[:].rearrange("p (c n) -> p c n", n=P)))
                    if "sm" in on:
                        t = now + E_LEAD - 1
                        v_max.wait(eng, t.at)
                        v_inv.wait(eng, t.at - 2)
                        a_exp.inc(eng.activation(expd[:], e_ps[:], ACT.Exp, bias=nmax[t.par][:],
                                                 accum_out=rsum[t.par][:]))
                        v_inv.wait(eng, t.at)
                        p_att.wait(eng, t.at - 1)
                        a_att.inc(eng.activation(att[:], expd[:], ACT.Copy, scale=rinv[t.par][:]))
                    if "sig" in on:
                        t = now - 2
                        v_gcopy.wait(eng, t.at)
                        v_route.wait(eng, t.at - 2)
                        a_sig.inc(eng.activation(sig_e[t.par][:], logit[t.par][:], ACT.Exp, scale=-1.0))
                    if "x2t" in on:
                        t = now - 1
                        p_x2t.wait(eng, t.at)
                        p_gate.wait(eng, t.at - 1)
                        a_x2t.inc(eng.copy(x2t[:], t_ps[:]))
                    if "disp" in on:
                        t = now - 2
                        v_route.wait(eng, t.at)
                        if "sent" in on:
                            d_disp.wait(eng, t - 1)
                        if isinstance(t.at, int):
                            eng.wait_ge(d_idle, 16 * IDLE)
                        for k in range(TOPK):
                            ins = eng.activation(disp[k][:], x2[t.par][:], ACT.Copy,
                                                 scale=wsc[t.par][:, k:k + 1])
                        a_disp.inc(ins)
                    if "k" in on:
                        t = now + K_LEAD
                        d_k.wait(eng, t)
                        p_en.wait(eng, t.at - BT - 1)
                        a_kh.inc(eng.copy(k_h[:, bass.ts(t.at & (2 * BT - 1), P)], kf[t.par][:]))
                    if "q" in on:
                        t = now + E_LEAD + 1
                        d_q.wait(eng, t)
                        p_en.wait(eng, t.at - 2)
                        a_qh.inc(eng.copy(q_h[t.par][:], qf[t.par][:]))

                pipeline(eng, {"k": (K_LEAD, 0, NT), "q": (E_LEAD + 1, 0, NT), "xt": (1, 0, NT),
                               "ta": (E_LEAD - 2, 0, NT), "sm": (E_LEAD - 1, 0, NT),
                               "sig": (-2, 0, NT), "x2t": (-1, 0, NT), "disp": (-2, 0, NT), "sent": (-3, 0, NT)}, step)

            @block.vector
            def _(eng):
                for s in (v_xstat, v_xn, v_xtl, v_x1, v_x2, v_keep, v_gcopy, v_route, v_rcopy, v_dest,
                          v_max, v_inv, v_attl, d_x1):
                    s.prime(eng)
                eng.wait_ge(d_const, 16 * 2)
                eng.wait_ge(c_setup, 12)

                def stats(src, i, t, counts, k0):
                    for h in (0, 1):
                        counts.inc(eng.bn_stats(bs[i][t.par][:, h, :], src[:, h * 512:(h + 1) * 512]))
                    counts.wait(eng, t.at, k0 + 2)
                    settled(eng, spare)
                    counts.inc(eng.bn_aggr(mv[i][t.par][:], bs[i][t.par][:].rearrange("p a b -> p (a b)")))

                def normalize(dst, src, i, t, counts):
                    counts.inc(eng.tensor_scalar(dst, src, mv[i][t.par][:, 0:1], rstd[i][t.par][:, 0:1],
                                                 ALU.subtract, ALU.mult))

                def step(now, on):
                    if "gcopy" in on:
                        t = now - 2
                        p_gate.wait(eng, t.at)
                        a_sig.wait(eng, t.at - 2)
                        v_gcopy.inc(eng.tensor_copy(logit[t.par][:], gate_ps))
                    if "rcopy" in on:
                        t = now - 3
                        p_rank.wait(eng, t.at)
                        v_rcopy.inc(eng.tensor_copy(rank[t.par][:], rank_ps))
                    if "x1" in on:
                        t = now - 1
                        p_mm.wait(eng, t.at)
                        d_x1.wait(eng, t - 1)
                        g_rstd[1].wait(eng, t.at - 2, 1)
                        d_xr.wait(eng, t)
                        v_x1.inc(eng.tensor_tensor(x1[:], o_ps[t.par][:], xr[:], ALU.add))
                        v_x1.wait(eng, t.at, 1)
                        stats(x1, 1, t, v_x1, 1)
                    if "dest" in on:
                        t = now - 3
                        p, n = t.par, 0

                        def dlink(ins):
                            nonlocal n
                            n += 1
                            v_dest.inc(ins)
                            v_dest.wait(eng, t.at, n)

                        v_rcopy.wait(eng, t.at)
                        if "sent" in on:
                            d_disp.wait(eng, t - 2)
                        dlink(eng.tensor_tensor(seen[1 - p][:], seen[p][:], mask[p][:], ALU.add))
                        dlink(eng.tensor_tensor(rank[p][:], rank[p][:], region[:], ALU.add))
                        for k in range(TOPK):
                            dlink(eng.tensor_tensor_reduce(junk[p][:, 0:E], one_hot[k][p][:], rank[p][:], 1.0,
                                                           0.0, ALU.mult, ALU.add, destf[p][:, k:k + 1]))
                        dlink(eng.tensor_copy(dest_all[:, t.at, :], destf[p][:]))
                        eng.tensor_copy(dest[0][p][:], destf[p][:, 0:1])
                        dlink(eng.tensor_copy(dest[1][p][:], destf[p][:, 1:2]))
                    if "xt" in on:
                        t = now + 1
                        a_xth.wait(eng, t.at)
                        v_xtl.inc(eng.tensor_tensor(xnt_l[t.par][:].rearrange("p c n -> p (c n)"), t_ps[:],
                                                    xnt_h[t.par][:].rearrange("p c n -> p (c n)").bitcast(F32),
                                                    ALU.subtract))
                    if "x1" in on:
                        t = now - 1
                        g_rstd[1].wait(eng, t.at)
                        p_x2t.wait(eng, t.at - 2)
                        a_disp.wait(eng, t.at - 2)
                        normalize(x2[t.par][:], x1[:], 1, t, v_x2)
                        v_keep.inc(eng.tensor_copy(stat_all[:, t.at, 0:1], mv[1][t.par][:, 0:1]))
                        v_keep.inc(eng.tensor_copy(stat_all[:, t.at, 1:2], rstd[1][t.par][:]))
                    if "sm" in on:
                        t = now + E_LEAD - 1
                        p_en.wait(eng, t.at)
                        a_exp.wait(eng, t.at - 2)
                        v_max.inc(eng.tensor_reduce(nmax[t.par][:], e_ps[:], AX, ALU.max, negate=True))
                    if "ta" in on:
                        t = now + E_LEAD - 2
                        a_atth.wait(eng, t.at)
                        v_attl.inc(eng.tensor_tensor(columns(att_l, t), t_ps[:].rearrange("p (c n) -> p c n", n=P),
                                                     columns(att_h, t).bitcast(F32), ALU.subtract))
                    if "xs" in on:
                        t = now + 2
                        d_x.wait(eng, t)
                        g_rstd[0].wait(eng, t.at - 2, 1)
                        stats(xs[t.par], 0, t, v_xstat, 0)
                    if "sm" in on:
                        t = now + E_LEAD - 1
                        a_exp.wait(eng, t.at)
                        a_att.wait(eng, t.at - 2)
                        v_inv.inc(eng.reciprocal(rinv[t.par][:], rsum[t.par][:]))
                    if "route" in on:
                        t = now - 2
                        p, n = t.par, 0

                        def link(ins):
                            nonlocal n
                            n += 1
                            v_route.inc(ins)
                            v_route.wait(eng, t.at, n)

                        a_sig.wait(eng, t.at)
                        a_disp.wait(eng, t.at - 2)
                        link(eng.tensor_scalar(score[p][:], sig_e[p][:], 1.0, None, ALU.add))
                        link(eng.reciprocal(score[p][:], score[p][:]))
                        link(eng.tensor_tensor(sel[p][:], score[p][:], eb[:], ALU.add))
                        for k in range(TOPK):
                            link(eng.tensor_reduce(top[p][:, 2 * k:2 * k + 1], sel[p][:], AX, ALU.max))
                            link(eng.scalar_tensor_tensor(cand[p][:], sel[p][:], top[p][:, 2 * k:2 * k + 1],
                                                          rank8[:], ALU.is_equal, ALU.mult))
                            link(eng.tensor_reduce(top[p][:, 2 * k + 1:2 * k + 2], cand[p][:], AX, ALU.min))
                            link(eng.tensor_scalar(one_hot[k][p][:], rank8[:], top[p][:, 2 * k + 1:2 * k + 2],
                                                   None, ALU.is_equal))
                            if k == 0:
                                link(eng.scalar_tensor_tensor(sel[p][:], one_hot[0][p][:], LOW, sel[p][:],
                                                              ALU.mult, ALU.add))
                        p_rank.wait(eng, t.at - 2)
                        link(eng.tensor_tensor(mask[p][:], one_hot[0][p][:], one_hot[1][p][:], ALU.add))
                        for k in range(TOPK):
                            ins = eng.tensor_tensor_reduce(junk[p][:, 0:E], one_hot[k][p][:], score[p][:], 1.0,
                                                           0.0, ALU.mult, ALU.add, wsc[p][:, k:k + 1])
                            link(ins)
                    if "xn" in on:
                        t = now + 2
                        g_rstd[0].wait(eng, t.at)
                        p_xt.wait(eng, t.at - 1)
                        normalize(xn[:], xs[t.par][:], 0, t, v_xn)

                pipeline(eng, {"x1": (-1, 0, NT), "gcopy": (-2, 0, NT), "rcopy": (-3, 0, NT),
                               "xt": (1, 0, NT), "ta": (E_LEAD - 2, 0, NT),
                               "sm": (E_LEAD - 1, 0, NT), "xs": (2, 0, NT), "route": (-2, 0, NT),
                               "dest": (-3, 0, NT), "sent": (-5, 0, NT), "xn": (2, 0, NT)}, step)

            @block.tensor
            def _(eng):
                for s in (p_xt, p_mm, p_x2t, p_gate, p_rank, p_en, p_att):
                    s.prime(eng)
                eng.wait_ge(d_const, 16 * 2)
                eng.wait_ge(c_setup, 12)

                def transposes(src):
                    for c in range(DC):
                        ins = eng.transpose(t_ps[:, c * P:(c + 1) * P], src[:, c * P:(c + 1) * P], ident_f[:])
                    return ins

                def sums(t, chunks):
                    parity = t.at & BT
                    for c in chunks:
                        for xt, at in ((xnt_h, att_h), (xnt_h, att_l), (xnt_l, att_h)):
                            for h in (0, 1):
                                ins = eng.matmul(o_ps[t.par][:, h * 512:(h + 1) * 512], xt[t.par][:, c, :],
                                                 at[:, parity + c, h * 512:(h + 1) * 512],
                                                 start=(c == 0 and xt is xnt_h and at is att_h),
                                                 stop=(c == DC - 1 and xt is xnt_l))
                    return ins

                def copied(now, on):
                    if "ta_last" in on:
                        v_attl.wait(eng, now.at + E_LEAD - 3)
                    if "x2t_last" in on:
                        v_gcopy.wait(eng, now.at - 2)
                    if "rank_last" in on:
                        v_rcopy.wait(eng, now.at - 3)

                def step(now, on):
                    if "xt" in on:
                        t = now + 1
                        v_xn.wait(eng, t.at)
                        copied(now, on)
                        p_xt.inc(transposes(xn))
                    if "mm" in on:
                        t = now
                        v_xtl.wait(eng, t.at)
                        v_attl.wait(eng, t.at | (BT - 1))
                        v_x1.wait(eng, t.at - 2, 1)
                        sums(t, range(0, 2))
                    if "ta" in on:
                        t = now + E_LEAD - 2
                        a_att.wait(eng, t.at)
                        if "xt" in on:
                            v_xtl.wait(eng, now.at + 1)
                        else:
                            copied(now, on)
                        p_att.inc(transposes(att))
                    if "mm" in on:
                        sums(now, range(2, 5))
                    if "x2t" in on:
                        t = now - 1
                        v_x2.wait(eng, t.at)
                        if "ta" in on:
                            v_attl.wait(eng, now.at + E_LEAD - 2)
                        elif "xt" in on:
                            v_xtl.wait(eng, now.at + 1)
                        else:
                            copied(now, on)
                        p_x2t.inc(transposes(x2[t.par]))
                    if "mm" in on:
                        p_mm.inc(sums(now, range(5, DC)))
                    if "rank" in on:
                        t = now - 2
                        v_route.wait(eng, t.at)
                        v_dest.wait(eng, t.at - 1, 1)
                        if "x2t" in on:
                            a_x2t.wait(eng, t.at + 1)
                        else:
                            copied(now, on)
                        eng.matmul(rank_ps, before[:], mask[t.par][:], start=True, stop=False)
                        p_rank.inc(eng.matmul(rank_ps, ones_b[:], seen[t.par][:], start=False, stop=True))
                    if "x2t" in on:
                        t = now - 1
                        a_x2t.wait(eng, t.at)
                        for c in range(DC):
                            ins = eng.matmul(gate_ps, x2t[:, c, :], gw[:, c, :], start=(c == 0),
                                             stop=(c == DC - 1))
                        p_gate.inc(ins)
                    if "en" in on:
                        t = now + E_LEAD
                        g_ql.wait(eng, t.at)
                        g_kl.wait(eng, t.at | (BT - 1))
                        a_exp.wait(eng, t.at - 1)
                        base = (t.at & BT) * P
                        for q, k in ((q_h, k_h), (q_h, k_l), (q_l, k_h)):
                            for h in (0, 1):
                                ins = eng.matmul(e_ps[:, h * 512:(h + 1) * 512], q[t.par][:],
                                                 k[:, bass.ds(base + h * 512, 512)],
                                                 start=(q is q_h and k is k_h), stop=(q is q_l))
                        p_en.inc(ins)

                pipeline(eng, {"xt": (1, 0, NT), "mm": (0, 0, NT), "ta": (E_LEAD - 2, 0, NT),
                               "ta_last": (E_LEAD - 3, 0, NT), "x2t": (-1, 0, NT), "x2t_last": (-2, 0, NT),
                               "rank": (-2, 0, NT), "rank_last": (-3, 0, NT),
                               "en": (E_LEAD, 0, NT)}, step)


def plan(nc, sems, kept, table, rows_d):
    with ExitStack() as ctx:
        def sb(name, shape, dt):
            return ctx.enter_context(nc.sbuf_tensor(name, shape, dt))

        zeros = sb("zeros", [P, D], BF16)
        cnt_i = sb("cnt_i", [P, E], I32)
        rows_i = sb("rows_i", [P, 2, E], I32)
        tiles = sb("tiles", [P, E], F32)
        ends = sb("ends", [P, E], F32)
        base = sb("base", [P, E], F32)
        moved = sb("moved", [P, E], F32)
        step = sb("step", [P, E], F32)
        part = sb("part", [P, NT * TOPK], F32)
        slot = [sb(f"slot{p}", [P, NT * TOPK], F32) for p in (0, 1)]
        index = sb("index", [1, P], F32)
        expert = [sb(f"expert{p}", [1, P], F32) for p in (0, 1)]
        first = [sb(f"first{p}", [1, P], F32) for p in (0, 1)]
        work = [sb(f"work{n}", [1, P], F32) for n in range(5)]
        cnt = ctx.enter_context(nc.psum_tensor("cnt", [P, E], F32))
        s_pool = sems.enter_context(nc.semaphore("s_pool"))
        s_cnt = sems.enter_context(nc.semaphore("s_cnt"))
        s_v = sems.enter_context(nc.semaphore("s_v"))
        s_tail = sems.enter_context(nc.semaphore("s_tail"))

        with nc.Block() as block:
            @block.gpsimd
            def _(eng):
                eng.iota(index[:], pattern=[[1, P]], base=0, channel_multiplier=0,
                         allow_small_or_imprecise_dtypes=True).then_inc(s_pool, 1)
                eng.iota(base[:], pattern=[[REG, E]], base=0, channel_multiplier=0,
                         allow_small_or_imprecise_dtypes=True).then_inc(s_pool, 1)
                eng.memset(zeros[:], 0.0).then_inc(s_pool, 1)

            @block.tensor
            def _(eng):
                eng.matmul(cnt[:], kept["ones_b"][:], kept["seen"][NT % 2][:], start=True,
                           stop=True).then_inc(s_cnt, 1)

            @block.vector
            def _(eng):
                n = 0

                def link(ins):
                    nonlocal n
                    n += 1
                    ins.then_inc(s_v, 1)
                    eng.wait_ge(s_v, n)

                eng.wait_ge(s_cnt, 1)
                eng.wait_ge(s_pool, 3)
                link(eng.tensor_scalar(cnt_i[:], cnt[:], float(P - 1), None, ALU.add))
                link(eng.tensor_tensor(rows_i[:, 1, :], cnt[:], base[:], ALU.add))
                link(eng.tensor_scalar(rows_i[:, 0, :], cnt_i[:], P.bit_length() - 1, None,
                                       ALU.arith_shift_right))
                link(eng.tensor_copy(tiles[:], rows_i[:, 0, :]))
                link(eng.tensor_copy(ends[:, 0:1], tiles[:, 0:1]))
                for e in range(1, E):
                    link(eng.tensor_tensor(ends[:, e:e + 1], ends[:, e - 1:e], tiles[:, e:e + 1], ALU.add))
                link(eng.tensor_scalar(expert[0][:], index[:], 0.0, None, ALU.mult))
                link(eng.tensor_scalar(first[0][:], index[:], 0.0, None, ALU.mult))
                for e in range(E):
                    a, b = e % 2, 1 - e % 2
                    link(eng.scalar_tensor_tensor(expert[b][:], index[:], ends[0:1, e:e + 1], expert[a][:],
                                                  ALU.is_ge, ALU.add))
                    link(eng.tensor_scalar(work[0][:], index[:], ends[0:1, e:e + 1], tiles[0:1, e:e + 1],
                                           ALU.is_ge, ALU.mult))
                    link(eng.tensor_tensor(first[b][:], first[a][:], work[0][:], ALU.add))
                link(eng.tensor_tensor(work[0][:], index[:], first[0][:], ALU.subtract))
                link(eng.tensor_scalar(work[1][:], expert[0][:], float(REG), None, ALU.mult))
                link(eng.scalar_tensor_tensor(table[:, 0, :], work[0][:], float(P), work[1][:], ALU.mult, ALU.add))
                link(eng.tensor_scalar(work[2][:], expert[0][:], float(E - 1), None, ALU.min))
                link(eng.tensor_copy(table[:, 1, :], work[2][:]))
                link(eng.tensor_copy(kept["ends"][:], ends[0:1, :]))
                link(eng.tensor_tensor(moved[:], ends[:], tiles[:], ALU.subtract))
                link(eng.scalar_tensor_tensor(moved[:], moved[:], float(P), base[:], ALU.mult, ALU.subtract))
                link(eng.tensor_copy(step[:, 0:1], moved[:, 0:1]))
                link(eng.tensor_tensor(step[:, 1:E], moved[:, 1:E], moved[:, 0:E - 1], ALU.subtract))
                dest = kept["dest_all"][:].rearrange("p t k -> p (t k)")
                link(eng.tensor_copy(slot[0][:], dest))
                for e in range(E):
                    a, b = e % 2, 1 - e % 2
                    link(eng.tensor_scalar(part[:], dest, float(e * REG), step[:, e:e + 1], ALU.is_ge, ALU.mult))
                    link(eng.tensor_tensor(slot[b][:], slot[a][:], part[:], ALU.add))
                link(eng.tensor_copy(kept["slot_all"][:].rearrange("p t k -> p (t k)"), slot[E % 2][:]))

            @block.sync
            def _(eng):
                eng.wait_ge(s_v, 2)
                for e in range(E):
                    row = eng.value_load(rows_i[0:1, 1, e:e + 1], min_val=e * REG, max_val=e * REG + TOK)
                    eng.dma_start(rows_d[bass.ds(row, P), :], zeros[:]).then_inc(s_tail, 16)
                eng.wait_ge(s_tail, 16 * E)


def routed(nc, sems, kept, table, w13, w2, rows_d, y_d):
    with ExitStack() as ctx:
        def sb(name, shape, dt):
            return ctx.enter_context(nc.sbuf_tensor(name, shape, dt))

        def pair(name, shape, dt):
            return [sb(f"{name}{p}", shape, dt) for p in (0, 1)]

        def count(name, **kw):
            return Count(sems, nc, name, **kw)

        ident_b = kept["ident_b"]
        wu = sb("wu", [P, 2, DC, 2 * HID], BF16)
        wd = sb("wd", [P, 2, HC, D], BF16)
        g = pair("g", [P, D], BF16)
        gt = pair("gt", [P, DC, P], BF16)
        sil = sb("sil", [P, HID], F32)
        h = pair("h", [P, HID], BF16)
        ht = pair("ht", [P, HC, P], BF16)
        y = pair("y", [P, D], BF16)
        up_ps = ctx.enter_context(nc.psum_tensor("up_ps", [P, 4, 512], F32))
        down_ps = ctx.enter_context(nc.psum_tensor("down_ps", [P, D], F32))
        gt_ps = ctx.enter_context(nc.psum_tensor("gt_ps", [P, DC, P], BF16))
        ht_ps = ctx.enter_context(nc.psum_tensor("ht_ps", [P, DC, P], BF16))

        NW = 4
        d_w = [sems.enter_context(nc.semaphore(f"d_we{p}")) for p in (0, 1)]
        g_w = sems.enter_context(nc.semaphore("g_w"))
        d_g, d_y = Loads(sems, nc, "d_g"), Loads(sems, nc, "d_y")
        p_gt = count("p_gt")
        a_gt = count("a_gt")
        p_up = count("p_up")
        a_sil = count("a_sil", per=2)
        v_h = count("v_h", per=2)
        p_ht = count("p_ht")
        v_ht = count("v_ht", per=2)
        p_dn = count("p_dn")
        a_y = count("a_y")
        v_y = count("v_y")

        with nc.Block() as block:
            @block.gpsimd
            def _(eng):
                for e in range(E):
                    if e >= 1:
                        eng.wait_ge(d_w[1 - e % 2], (e + 1) // 2 * 16 * NW)
                        eng.sem_inc(g_w, 1)
                    if e >= 2:
                        last = eng.value_load(kept["ends"][0:1, e - 2:e - 1], min_val=0, max_val=ET)
                        eng.wait_ge(p_dn.sem, last + p_dn.lead)
                        settled(eng, kept["spare"])
                    for c in (0, 1):
                        cs = slice(c * DC // 2, (c + 1) * DC // 2)
                        eng.dma_start(wu[:, e % 2, cs, :], w13[e][:, cs, :]).then_inc(d_w[e % 2], 16)
                    eng.dma_start(wd[:, e % 2, 0:HC - 1, :],
                                  w2[e][0:(HC - 1) * P, :].rearrange("(c p) n -> p c n", p=P)).then_inc(d_w[e % 2], 16)
                    eng.dma_start(wd[0:HTAIL, e % 2, HC - 1, :], w2[e][(HC - 1) * P:HID, :]).then_inc(d_w[e % 2], 16)
                eng.wait_ge(d_w[1 - E % 2], (E + 1) // 2 * 16 * NW)
                eng.sem_inc(g_w, 1)

            @block.sync
            def _(eng):
                for s in (d_g,):
                    s.prime(eng)

                def step(now, on):
                    if "g" in on:
                        t = now + 3
                        p_gt.wait(eng, t.at - 2)
                        settled(eng, kept["spare"])
                        row = eng.value_load(table[0:1, 0, bass.ds(t.at, 1)], min_val=0, max_val=GROWS - P)
                        d_g.inc(eng.dma_start(g[t.par][:], rows_d[bass.ds(row, P), :]), t)
                    if "y" in on:
                        t = now - 1
                        a_y.wait(eng, t.at)
                        v_y.wait(eng, t.at)
                        d_y.inc(eng.dma_start(y_d[bass.ts(t.at, P), :], y[t.par][:]), t)

                pipeline(eng, {"g": (3, 0, ET), "y": (-1, 0, ET)}, step)
                for t in (ET - 2, ET - 1):
                    d_y.wait(eng, Tile(t // 2, t % 2))

            @block.scalar
            def _(eng):
                for s in (a_gt, a_sil, a_y):
                    s.prime(eng)

                def step(now, on):
                    if "gt" in on:
                        t = now + 1
                        p_gt.wait(eng, t.at)
                        p_up.wait(eng, t.at - 2)
                        a_gt.inc(eng.copy(gt[t.par][:], gt_ps[:]))
                    if "up" in on:
                        t = now
                        p_up.wait(eng, t.at)
                        for i in (0, 1):
                            v_h.wait(eng, t.at - 1, i + 1)
                            a_sil.inc(eng.activation(sil[:, i * HALF:(i + 1) * HALF], up_ps[:, i, 0:HALF], ACT.Silu))
                    if "y" in on:
                        t = now - 1
                        p_dn.wait(eng, t.at)
                        d_y.wait(eng, t - 2)
                        a_y.inc(eng.copy(y[t.par][:, 0:512], down_ps[:, 0:512]))

                pipeline(eng, {"gt": (1, 0, ET), "up": (0, 0, ET), "y": (-1, 0, ET)}, step)

            @block.vector
            def _(eng):
                for s in (v_h, v_ht, v_y, d_y):
                    s.prime(eng)

                def step(now, on):
                    if "ht" in on:
                        t = now - 1
                        p_ht.wait(eng, t.at)
                        p_dn.wait(eng, t.at - 2)
                        v_ht.inc(eng.tensor_copy(ht[t.par][:, 0:HC - 1, :], ht_ps[:, 0:HC - 1, :]))
                        v_ht.inc(eng.tensor_copy(ht[t.par][0:HTAIL, HC - 1, :], ht_ps[0:HTAIL, HC - 1, :]))
                    if "up" in on:
                        t = now
                        p_ht.wait(eng, t.at - 2)
                        for i in (0, 1):
                            a_sil.wait(eng, t.at, i + 1)
                            v_h.inc(eng.tensor_tensor(h[t.par][:, i * HALF:(i + 1) * HALF],
                                                      sil[:, i * HALF:(i + 1) * HALF], up_ps[:, 2 + i, 0:HALF],
                                                      ALU.mult))
                    if "y" in on:
                        t = now - 1
                        p_dn.wait(eng, t.at)
                        d_y.wait(eng, t - 2)
                        v_y.inc(eng.tensor_copy(y[t.par][:, 512:], down_ps[:, 512:]))

                pipeline(eng, {"ht": (-1, 0, ET), "up": (0, 0, ET), "y": (-1, 0, ET)}, step)

            @block.tensor
            def _(eng):
                for s in (p_gt, p_up, p_ht, p_dn):
                    s.prime(eng)

                def step(now, on):
                    if "gt" in on:
                        t = now + 1
                        d_g.wait(eng, t)
                        a_gt.wait(eng, t.at - 1)
                        for c in range(DC):
                            ins = eng.transpose(gt_ps[:, c, :], g[t.par][:, c * P:(c + 1) * P], ident_b[:])
                        p_gt.inc(ins)
                    if "up" in on:
                        t = now
                        expert = eng.value_load(table[0:1, 1, bass.ds(t.at, 1)], min_val=0, max_val=E - 1)
                        buf = expert & 1
                        eng.wait_ge(g_w, expert + 1)
                        a_gt.wait(eng, t.at)
                        v_h.wait(eng, t.at - 1)
                        for c in range(DC):
                            for i in range(4):
                                ins = eng.matmul(up_ps[:, i, 0:HALF], gt[t.par][:, c, :],
                                                 wu[:, buf, c, i * HALF:(i + 1) * HALF], start=c == 0,
                                                 stop=c == DC - 1)
                        p_up.inc(ins)
                    if "dn" in on:
                        t = now - 1
                        expert = eng.value_load(table[0:1, 1, bass.ds(t.at, 1)], min_val=0, max_val=E - 1)
                        buf = expert & 1
                        v_ht.wait(eng, t.at)
                        a_y.wait(eng, t.at - 1)
                        v_y.wait(eng, t.at - 1)
                        for c in range(HC):
                            k = P if c < HC - 1 else HTAIL
                            for i in (0, 1):
                                ins = eng.matmul(down_ps[:, i * 512:(i + 1) * 512], ht[t.par][0:k, c, :],
                                                 wd[0:k, buf, c, i * 512:(i + 1) * 512], start=c == 0,
                                                 stop=c == HC - 1)
                        p_dn.inc(ins)
                    if "up" in on:
                        t = now
                        v_h.wait(eng, t.at)
                        v_ht.wait(eng, t.at - 1)
                        for c in range(HC):
                            k = P if c < HC - 1 else HTAIL
                            ins = eng.transpose(ht_ps[0:k, c, :], h[t.par][:, c * P:c * P + k], ident_b[:])
                        p_ht.inc(ins)

                pipeline(eng, {"gt": (1, 0, ET), "up": (0, 0, ET), "dn": (-1, 0, ET)}, step)


def shared(nc, sems, kept, sw13, sw2, x1_d, y_d, out):
    with ExitStack() as ctx:
        def sb(name, shape, dt):
            return ctx.enter_context(nc.sbuf_tensor(name, shape, dt))

        def pair(name, shape, dt):
            return [sb(f"{name}{p}", shape, dt) for p in (0, 1)]

        def count(name, **kw):
            return Count(sems, nc, name, **kw)

        ident_f, slot_all, stat_all = kept["ident_f"], kept["slot_all"], kept["stat_all"]
        wu_h, wu_l = sb("wu_h", [P, DC, 2 * HID], F32R), sb("wu_l", [P, DC, 2 * HID], F32R)
        wd_h, wd_l = sb("wd_h", [P, HC, D], F32R), sb("wd_l", [P, HC, D], F32R)
        raw = pair("raw", [P, 2 * HID], F32)
        x1 = sb("sx1", [P, 4, D], F32)
        xn = sb("sxn", [P, D], F32)
        xt_h, xt_l = pair("xt_h", [P, DC, P], F32R), pair("xt_l", [P, DC, P], F32R)
        sil = sb("ssil", [P, HID], F32)
        h = sb("sh", [P, HID], F32)
        ht_h, ht_l = sb("ht_h", [P, HC, P], F32R), sb("ht_l", [P, HC, P], F32R)
        idx = [pair("idx0_", [P, 1], I32), pair("idx1_", [P, 1], I32)]
        yr = [sb("yr0", [P, D], BF16), sb("yr1", [P, D], BF16)]
        o = sb("so", [P, D], F32)
        up_ps = ctx.enter_context(nc.psum_tensor("sup_ps", [P, 4, 512], F32))
        down_ps = ctx.enter_context(nc.psum_tensor("sdown_ps", [P, D], F32))
        t_ps = ctx.enter_context(nc.psum_tensor("st_ps", [P, D], F32))

        d_raw = Loads(sems, nc, "d_raw")
        d_x1 = Loads(sems, nc, "d_sx1")
        d_yr = Loads(sems, nc, "d_yr", n=TOPK, lead=0)
        d_o = Loads(sems, nc, "d_o")
        a_wh, v_wl = count("a_wh"), count("v_wl")
        v_idx = count("v_idx", per=2)
        v_xn = count("v_sxn")
        p_xt = count("p_sxt")
        a_xt, v_xt = count("a_sxt"), count("v_sxt")
        p_up = count("p_sup")
        a_sil = count("a_ssil", per=2)
        v_h = count("v_sh", per=2)
        p_ht = count("p_sht")
        a_ht, v_ht = count("a_sht", per=2), count("v_sht", per=2)
        p_dn = count("p_sdn")
        v_o = count("v_o", per=3)

        chunks = [(sw13[:, c, :], wu_h[:, c, :], wu_l[:, c, :], P, 2 * HID) for c in range(DC)]
        for c in range(HC):
            k = P if c < HC - 1 else HTAIL
            chunks.append((sw2[c * P:c * P + k, :], wd_h[0:k, c, :], wd_l[0:k, c, :], k, D))

        with nc.Block() as block:
            @block.sync
            def _(eng):
                for s in (d_raw, d_x1):
                    s.prime(eng)
                for n, (src, _, _, k, width) in enumerate(chunks):
                    t = Tile(n // 2, n % 2)
                    a_wh.wait(eng, n - 2)
                    v_wl.wait(eng, n - 2)
                    d_raw.inc(eng.dma_start(raw[t.par][0:k, 0:width], src), t)

                def step(now, on):
                    if "x1" in on:
                        t = now + 3
                        v_xn.wait(eng, t.at - 2)
                        v_o.wait(eng, t.at - 4)
                        settled(eng, kept["spare"])
                        d_x1.inc(eng.dma_start(x1[:, t.at & 3, :], x1_d[bass.ts(t.at, P), :]), t)
                    if "o" in on:
                        t = now - 1
                        v_o.wait(eng, t.at)
                        d_o.inc(eng.dma_start(out[t.at], o[:]), t)

                pipeline(eng, {"x1": (3, 0, NT), "o": (-1, 0, NT)}, step)
                for t in (NT - 2, NT - 1):
                    d_o.wait(eng, Tile(t // 2, t % 2))

            @block.gpsimd
            def _(eng):
                def step(now, on):
                    t = now
                    v_idx.wait(eng, t.at)
                    v_o.wait(eng, t.at - 1)
                    for k in range(TOPK):
                        settled(eng, kept["spare"])
                        d_yr.inc(eng.indirect_dma_start(
                            yr[k][:], None, y_d, bass.IndirectOffsetOnAxis(ap=idx[k][t.par][:, 0:1], axis=0)), t)

                pipeline(eng, {"y": (0, 0, NT)}, step)

            @block.scalar
            def _(eng):
                for s in (a_wh, a_xt, a_sil, a_ht):
                    s.prime(eng)
                for n, (_, hi, _, k, width) in enumerate(chunks):
                    d_raw.wait(eng, Tile(n // 2, n % 2))
                    a_wh.inc(eng.copy(hi, raw[n % 2][0:k, 0:width]))

                def step(now, on):
                    if "xt" in on:
                        t = now + 1
                        p_xt.wait(eng, t.at)
                        p_up.wait(eng, t.at - 2)
                        a_xt.inc(eng.copy(xt_h[t.par][:], t_ps[:]))
                    if "up" in on:
                        t = now
                        p_up.wait(eng, t.at)
                        for i in (0, 1):
                            v_h.wait(eng, t.at - 1, i + 1)
                            a_sil.inc(eng.activation(sil[:, i * HALF:(i + 1) * HALF], up_ps[:, i, 0:HALF], ACT.Silu))
                        p_ht.wait(eng, t.at)
                        p_dn.wait(eng, t.at - 1)
                        a_ht.inc(eng.copy(ht_h[:, 0:HC - 1, :], t_ps[:, 0:(HC - 1) * P]))
                        a_ht.inc(eng.copy(ht_h[0:HTAIL, HC - 1, :], t_ps[0:HTAIL, (HC - 1) * P:HC * P]))

                pipeline(eng, {"xt": (1, 0, NT), "up": (0, 0, NT)}, step)

            @block.vector
            def _(eng):
                for s in (v_wl, v_idx, v_xn, v_xt, v_h, v_ht, v_o, d_o):
                    s.prime(eng)
                for n, (_, hi, lo, k, width) in enumerate(chunks):
                    a_wh.wait(eng, n)
                    v_wl.inc(eng.tensor_tensor(lo, raw[n % 2][0:k, 0:width], hi.bitcast(F32), ALU.subtract))

                def step(now, on):
                    if "idx" in on:
                        t = now
                        if "sent" in on:
                            d_yr.wait(eng, t - 2)
                        for k in range(TOPK):
                            v_idx.inc(eng.tensor_copy(idx[k][t.par][:], slot_all[:, bass.ds(t.at, 1), k]))
                    if "xt" in on:
                        t = now + 1
                        a_xt.wait(eng, t.at)
                        v_xt.inc(eng.tensor_tensor(xt_l[t.par][:].rearrange("p c n -> p (c n)"), t_ps[:],
                                                   xt_h[t.par][:].rearrange("p c n -> p (c n)").bitcast(F32),
                                                   ALU.subtract))
                    if "up" in on:
                        t = now
                        p_ht.wait(eng, t.at - 1)
                        for i in (0, 1):
                            a_sil.wait(eng, t.at, i + 1)
                            v_h.inc(eng.tensor_tensor(h[:, i * HALF:(i + 1) * HALF],
                                                      sil[:, i * HALF:(i + 1) * HALF], up_ps[:, 2 + i, 0:HALF],
                                                      ALU.mult))
                        a_ht.wait(eng, t.at)
                        v_ht.inc(eng.tensor_tensor(
                            ht_l[:, 0:HC - 1, :].rearrange("p c n -> p (c n)"), t_ps[:, 0:(HC - 1) * P],
                            ht_h[:, 0:HC - 1, :].rearrange("p c n -> p (c n)").bitcast(F32), ALU.subtract))
                        v_ht.inc(eng.tensor_tensor(ht_l[0:HTAIL, HC - 1, :], t_ps[0:HTAIL, (HC - 1) * P:HC * P],
                                                   ht_h[0:HTAIL, HC - 1, :].bitcast(F32), ALU.subtract))
                    if "xn" in on:
                        t = now + 2
                        d_x1.wait(eng, t)
                        p_xt.wait(eng, t.at - 1)
                        v_xn.inc(eng.tensor_scalar(xn[:], x1[:, t.at & 3, :], stat_all[:, bass.ds(t.at, 1), 0],
                                                   stat_all[:, bass.ds(t.at, 1), 1], ALU.subtract, ALU.mult))
                    if "o" in on:
                        t = now - 1
                        p_dn.wait(eng, t.at)
                        d_yr.wait(eng, t)
                        d_o.wait(eng, t - 1)
                        v_o.inc(eng.tensor_tensor(o[:], down_ps[:], yr[0][:], ALU.add))
                        v_o.wait(eng, t.at, 1)
                        v_o.inc(eng.tensor_tensor(o[:], o[:], yr[1][:], ALU.add))
                        v_o.wait(eng, t.at, 2)
                        v_o.inc(eng.tensor_tensor(o[:], o[:], x1[:, t.at & 3, :], ALU.add))

                pipeline(eng, {"idx": (0, 0, NT), "sent": (-2, 0, NT), "xn": (2, 0, NT), "xt": (1, 0, NT),
                               "o": (-1, 0, NT), "up": (0, 0, NT)}, step)

            @block.tensor
            def _(eng):
                for s in (p_xt, p_up, p_ht, p_dn):
                    s.prime(eng)

                def up(t, cs):
                    for c in cs:
                        if isinstance(t.at, int) and t.at == 0:
                            v_wl.wait(eng, c)
                        for x, w in ((xt_h, wu_h), (xt_h, wu_l), (xt_l, wu_h)):
                            for i in range(4):
                                ins = eng.matmul(up_ps[:, i, 0:HALF], x[t.par][:, c, :],
                                                 w[:, c, i * HALF:(i + 1) * HALF],
                                                 start=c == 0 and x is xt_h and w is wu_h,
                                                 stop=c == DC - 1 and x is xt_l)
                    return ins

                def step(now, on):
                    if "up" in on:
                        t = now
                        v_xt.wait(eng, t.at)
                        v_h.wait(eng, t.at - 1)
                        up(t, range(DC // 2))
                    if "xt" in on:
                        t = now + 1
                        v_xn.wait(eng, t.at)
                        v_ht.wait(eng, t.at - 2)
                        for c in range(DC):
                            ins = eng.transpose(t_ps[:, c * P:(c + 1) * P], xn[:, c * P:(c + 1) * P], ident_f[:])
                        p_xt.inc(ins)
                    if "up" in on:
                        p_up.inc(up(now, range(DC // 2, DC)))
                    if "dn" in on:
                        t = now - 1
                        if isinstance(t.at, int) and t.at == 0:
                            v_wl.wait(eng, DC + HC - 1)
                        v_ht.wait(eng, t.at)
                        v_o.wait(eng, t.at - 1, 1)
                        for c in range(HC):
                            k = P if c < HC - 1 else HTAIL
                            for x, w in ((ht_h, wd_h), (ht_h, wd_l), (ht_l, wd_h)):
                                for i in (0, 1):
                                    ins = eng.matmul(down_ps[:, i * 512:(i + 1) * 512], x[0:k, c, :],
                                                     w[0:k, c, i * 512:(i + 1) * 512],
                                                     start=c == 0 and x is ht_h and w is wd_h,
                                                     stop=c == HC - 1 and x is ht_l)
                        p_dn.inc(ins)
                    if "up" in on:
                        t = now
                        v_h.wait(eng, t.at)
                        if "xt" in on:
                            v_xt.wait(eng, t.at + 1)
                        for c in range(HC):
                            k = P if c < HC - 1 else HTAIL
                            ins = eng.transpose(t_ps[0:k, c * P:(c + 1) * P], h[:, c * P:c * P + k], ident_f[:])
                        p_ht.inc(ins)

                pipeline(eng, {"up": (0, 0, NT), "xt": (1, 0, NT), "dn": (-1, 0, NT)}, step)


def layout(a, chunk=P):
    return np.ascontiguousarray(a.reshape(-1, chunk, a.shape[-1]).transpose(1, 0, 2))


def kernel(x, ctx_1024, L0_xattn_Wq, L0_xattn_bq, L0_xattn_Wk, L0_xattn_bk, L0_ffn_gate_w, L0_ffn_w1, L0_ffn_w2,
           L0_ffn_w3, L0_ffn_sw1, L0_ffn_sw2, L0_ffn_sw3, L0_ffn_expert_bias):
    import concourse.bacc as bacc
    from concourse.bass_utils import run_bass_kernel_spmd

    up = np.concatenate([L0_ffn_w1, L0_ffn_w3], axis=1)
    sup = np.concatenate([L0_ffn_sw1, L0_ffn_sw3], axis=0)
    inputs = {
        "x": np.ascontiguousarray(x.reshape(NT, P, D)),
        "ctxt": np.ascontiguousarray(ctx_1024.reshape(TOK // GROUP, GROUP, CC, P).transpose(0, 3, 2, 1)),
        "wq": layout(L0_xattn_Wq.T), "wk": layout(L0_xattn_Wk.T),
        "bq": L0_xattn_bq.reshape(DH, 1), "bk": L0_xattn_bk.reshape(DH, 1),
        "gate_w": layout(L0_ffn_gate_w.T), "ebias": L0_ffn_expert_bias.reshape(1, E),
        "w13": np.ascontiguousarray(up.reshape(E, 2 * HID, DC, P).transpose(0, 3, 2, 1)),
        "w2": np.ascontiguousarray(L0_ffn_w2.transpose(0, 2, 1)),
        "sw13": np.ascontiguousarray(sup.reshape(2 * HID, DC, P).transpose(2, 1, 0)),
        "sw2": np.ascontiguousarray(L0_ffn_sw2.T),
    }
    nc = bacc.Bacc("TRN2", target_bir_lowering=False, num_devices=1, dynamic_dma_scratch_size=DMA_RING)
    args = []
    for name, a in inputs.items():
        args.append(nc.dram_tensor(f"in_{name}", a.shape, mybir.dt.from_np(a.dtype), kind="ExternalInput").ap())
    out = nc.dram_tensor("out", [NT, P, D], F32, kind="ExternalOutput").ap()
    build(nc, *args, out)
    r = run_bass_kernel_spmd(nc, [{f"in_{n}": a for n, a in inputs.items()}], core_ids=[0])
    return r.results[0]["out"].reshape(B, L, D)
```

```python
from contextlib import ExitStack

import numpy as np

import concourse.bass as bass
import concourse.mybir as mybir
from concourse.alu_op_type import AluOpType as ALU

F32 = mybir.dt.float32
F32R = mybir.dt.float32r
BF16 = mybir.dt.bfloat16
I32 = mybir.dt.int32
U32 = mybir.dt.uint32
ACT = mybir.ActivationFunctionType
AX = mybir.AxisListType.X

P = 128
B, L, D = 4, 1024, 1024
TOK = B * L
NT = TOK // P
C, DH = 512, 128
CC = C // P
DC = D // P
BT = L // P
E, HID = 8, 704
HALF = HID // 2
HC = -(-HID // P)
HTAIL = HID - (HC - 1) * P
TOPK = 2
REG = TOK + P
ET = TOPK * TOK // P + E - 1
IDLE = E - 1
GROWS = E * REG + IDLE * P
EPS = 1e-5
DMA_RING = 8192
GROUP = 512


class Count:

    def __init__(self, ctx, nc, name, per=1, first=0, lead=24):
        self.sem = ctx.enter_context(nc.semaphore(name))
        self.per, self.first, self.lead = per, first, lead

    def prime(self, eng):
        eng.sem_inc(self.sem, self.per * self.lead)

    def wait(self, eng, tile, k=None):
        k = self.per if k is None else k
        eng.wait_ge(self.sem, (tile - self.first + self.lead) * self.per + k)

    def inc(self, ins):
        ins.then_inc(self.sem, 1)


class Loads:

    def __init__(self, ctx, nc, name, n=1, first=0, lead=4):
        self.sems = [ctx.enter_context(nc.semaphore(f"{name}{p}")) for p in (0, 1)]
        self.n, self.first, self.lead = n, first // 2, lead

    def prime(self, eng):
        for s in self.sems:
            eng.sem_inc(s, 16 * self.n * self.lead)

    def wait(self, eng, tile):
        eng.wait_ge(self.sems[tile.par], (tile.half - self.first + 1 + self.lead) * 16 * self.n)

    def inc(self, ins, tile):
        ins.then_inc(self.sems[tile.par], 16)


class Tile:

    def __init__(self, half, par):
        self.half, self.par = half, par
        self.at = half * 2 + par

    def __add__(self, n):
        q, par = divmod(self.par + n, 2)
        return Tile(self.half + q, par)

    def __sub__(self, n):
        return self + (-n)


def settled(eng, spare):
    eng.sem_inc(spare, 1)


def pipeline(eng, stages, body):
    lo = min(a - o for o, a, b in stages.values())
    hi = max(b - o for o, a, b in stages.values())
    lo -= lo % 2
    shift = -lo // 2

    def on(s):
        return frozenset(n for n, (o, a, b) in stages.items() if a <= s + o < b)

    pairs = [(on(s), on(s + 1)) for s in range(lo, hi, 2)]
    at = 0
    while at < len(pairs):
        end = at
        while end < len(pairs) and pairs[end] == pairs[at]:
            end += 1

        def both(half):
            for par in (0, 1):
                if pairs[at][par]:
                    body(Tile(half - shift, par), pairs[at][par])

        if end - at == 1:
            both(at)
        else:
            with eng.Fori(at, end) as half:
                both(half)
        at = end


def build(nc, x, ctxt, wq, wk, bq, bk, gate_w, ebias, w13, w2, sw13, sw2, out):
    xt_d = nc.dram_tensor("xt_d", [NT, P, D], F32, kind="Internal").ap()
    x1_d = nc.dram_tensor("x1_d", [TOK, D], F32, kind="Internal").ap()
    rows_d = nc.dram_tensor("rows_d", [GROWS, D], BF16, kind="Internal").ap()
    y_d = nc.dram_tensor("y_d", [ET * P, D], BF16, kind="Internal").ap()
    q_d, k_d = (nc.dram_tensor(n, [NT, P, P], F32, kind="Internal").ap() for n in ("q_d", "k_d"))
    with ExitStack() as ctx:
        def keep(name, shape, dt):
            return ctx.enter_context(nc.sbuf_tensor(name, shape, dt))

        kept = {
            "ident_f": keep("ident_f", [P, P], F32),
            "ident_b": keep("ident_b", [P, P], BF16),
            "ones_b": keep("ones_b", [P, P], BF16),
            "dest_all": keep("dest_all", [P, NT, TOPK], F32),
            "slot_all": keep("slot_all", [P, NT, TOPK], I32),
            "before": keep("before", [P, P], BF16),
            "gw": keep("gw", [P, DC, E], F32),
            "eb": keep("eb", [P, E], F32),
            "index8": keep("index8", [P, E], F32),
            "region": keep("region", [P, E], F32),
            "eps": keep("eps", [P, 1], F32),
            "half_neg": keep("half_neg", [P, 1], F32),
            "ends": keep("ends_i", [1, E], I32),
            "spare": ctx.enter_context(nc.semaphore("spare")),
            "seen": [keep(f"seen{p}", [P, E], BF16) for p in (0, 1)],
        }
        project(nc, ctx, kept, ctxt, (wq, wk), (bq, bk), (q_d, k_d), gate_w, ebias, rows_d)
        attention(nc, ctx, kept, x, q_d, k_d, x1_d, xt_d, rows_d)
        table = keep("table", [1, 2, P], I32)
        plan(nc, ctx, kept, table, rows_d)
        routed(nc, ctx, kept, table, w13, w2, rows_d, y_d)
        shared(nc, ctx, kept, sw13, sw2, x1_d, xt_d, y_d, out)


def project(nc, sems, kept, ctxt, weights, biases, outs, gate_w, ebias, rows_d):
    with ExitStack() as ctx:
        def sb(name, shape, dt):
            return ctx.enter_context(nc.sbuf_tensor(name, shape, dt))

        def pair(name, shape, dt):
            return [sb(f"{name}{p}", shape, dt) for p in (0, 1)]

        NG = TOK // GROUP
        raw = sb("raw", [P, 2, CC, DH], F32)
        w_h, w_l = sb("w_h", [P, 2, CC, DH], F32R), sb("w_l", [P, 2, CC, DH], F32R)
        bias = sb("bias", [P, 2], F32)
        cf = pair("cf", [P, CC, GROUP], F32)
        ch, cl = pair("ch", [P, CC, GROUP], F32R), pair("cl", [P, CC, GROUP], F32R)
        res = pair("res", [P, 2, GROUP], F32)
        acc = [ctx.enter_context(nc.psum_tensor(f"acc{p}", [P, 2, GROUP], F32)) for p in (0, 1)]

        zeros = sb("idle_zeros", [P, D], BF16)

        d_const = sems.enter_context(nc.semaphore("d_const"))
        d_idle = sems.enter_context(nc.semaphore("d_idle"))
        c_const = sems.enter_context(nc.semaphore("c_const"))
        d_w = sems.enter_context(nc.semaphore("d_w"))
        c_w = sems.enter_context(nc.semaphore("c_w"))
        d_c = Loads(sems, nc, "d_c")
        d_res = Loads(sems, nc, "d_res", n=2)
        a_hi = Count(sems, nc, "a_hi")
        v_lo = Count(sems, nc, "v_lo")
        p_acc = Count(sems, nc, "p_acc")
        a_res = Count(sems, nc, "a_res")

        with nc.Block() as block:
            @block.gpsimd
            def _(eng):
                def const(ins):
                    ins.then_inc(c_const, 1)

                ident_f, ones_b = kept["ident_f"], kept["ones_b"]
                const(eng.memset(zeros[:], 0.0))
                const(eng.memset(ident_f[:], 0.0))
                const(eng.memset(ones_b[:], 1.0))
                eng.wait_ge(c_const, 3)
                const(eng.affine_select(out=ident_f[:], in_=ident_f[:], compare_op=ALU.not_equal, fill=1.0, base=0,
                                        pattern=[[-1, P]], channel_multiplier=1))
                const(eng.affine_select(out=kept["before"][:], in_=ones_b[:], compare_op=ALU.is_gt, fill=0.0,
                                        base=0, pattern=[[1, P]], channel_multiplier=-1))
                eng.wait_ge(c_const, 4)
                const(eng.tensor_copy(kept["ident_b"][:], ident_f[:]))
                const(eng.iota(kept["index8"][:], pattern=[[1, E]], base=0, channel_multiplier=0,
                               allow_small_or_imprecise_dtypes=True))
                const(eng.iota(kept["region"][:], pattern=[[REG, E]], base=0, channel_multiplier=0,
                               allow_small_or_imprecise_dtypes=True))
                const(eng.memset(kept["half_neg"][:], -0.5))
                const(eng.memset(kept["eps"][:], EPS))
                for p in (0, 1):
                    const(eng.memset(kept["seen"][p][:], 0.0))

            @block.sync
            def _(eng):
                d_c.prime(eng)
                for i in (0, 1):
                    eng.dma_start(raw[:, i], weights[i]).then_inc(d_w, 16)
                    eng.dma_start(bias[:, i:i + 1], biases[i]).then_inc(d_w, 16)

                def step(now, on):
                    if "load" in on:
                        t = now + 2
                        a_hi.wait(eng, t.at - 2)
                        v_lo.wait(eng, t.at - 2)
                        d_c.inc(eng.dma_start(cf[t.par][:], ctxt[t.at]), t)
                    if "out" in on:
                        a_res.wait(eng, now.at)
                        for i in (0, 1):
                            d_res.inc(eng.dma_start(
                                outs[i][bass.ts(now.at, GROUP // P)].rearrange("t p n -> p t n"),
                                res[now.par][:, i].rearrange("p (t n) -> p t n", n=P)), now)

                pipeline(eng, {"load": (2, 0, NG), "out": (0, 0, NG)}, step)
                eng.dma_start(kept["gw"][:], gate_w).then_inc(d_const, 16)
                eng.dma_start(kept["eb"][:], ebias.broadcast_to([P, E])).then_inc(d_const, 16)
                eng.wait_ge(c_const, 1)
                for i in range(IDLE):
                    r = E * REG + i * P
                    eng.dma_start(rows_d[r:r + P, :], zeros[:]).then_inc(d_idle, 16)
                eng.wait_ge(d_const, 16 * 2)
                eng.wait_ge(d_idle, 16 * IDLE)
                for t in (NG - 2, NG - 1):
                    d_res.wait(eng, Tile(t // 2, t % 2))

            @block.scalar
            def _(eng):
                a_hi.prime(eng)
                a_res.prime(eng)
                d_res.prime(eng)
                eng.wait_ge(d_w, 16 * 4)
                eng.copy(w_h[:], raw[:]).then_inc(c_w, 1)

                def step(now, on):
                    if "hi" in on:
                        t = now + 1
                        d_c.wait(eng, t)
                        p_acc.wait(eng, t.at - 2)
                        a_hi.inc(eng.copy(ch[t.par][:], cf[t.par][:]))
                    if "res" in on:
                        p_acc.wait(eng, now.at)
                        d_res.wait(eng, now - 2)
                        eng.activation(res[now.par][:, 0], acc[now.par][:, 0], ACT.Identity, bias=bias[:, 0:1])
                        a_res.inc(eng.activation(res[now.par][:, 1], acc[now.par][:, 1], ACT.Identity,
                                                 bias=bias[:, 1:2]))

                pipeline(eng, {"hi": (1, 0, NG), "res": (0, 0, NG)}, step)

            @block.vector
            def _(eng):
                v_lo.prime(eng)
                eng.wait_ge(c_w, 1)
                eng.tensor_tensor(w_l[:], raw[:], w_h[:].bitcast(F32), ALU.subtract).then_inc(c_w, 1)

                def step(now, on):
                    a_hi.wait(eng, now.at)
                    v_lo.inc(eng.tensor_tensor(cl[now.par][:], cf[now.par][:], ch[now.par][:].bitcast(F32),
                                               ALU.subtract))

                pipeline(eng, {"lo": (0, 0, NG)}, step)

            @block.tensor
            def _(eng):
                p_acc.prime(eng)
                eng.wait_ge(c_w, 2)

                def step(now, on):
                    v_lo.wait(eng, now.at)
                    a_res.wait(eng, now.at - 2)
                    for i in (0, 1):
                        for c in range(CC):
                            for w, v in ((w_h, ch), (w_h, cl), (w_l, ch)):
                                ins = eng.matmul(acc[now.par][:, i], w[:, i, c, :], v[now.par][:, c, :],
                                                 start=(c == 0 and w is w_h and v is ch),
                                                 stop=(c == CC - 1 and w is w_l))
                    p_acc.inc(ins)

                pipeline(eng, {"mm": (0, 0, NG)}, step)


def attention(nc, sems, kept, x, q_d, k_d, x1_d, xt_d, rows_d):
    with ExitStack() as ctx:
        def sb(name, shape, dt):
            return ctx.enter_context(nc.sbuf_tensor(name, shape, dt))

        def ps(name, shape, dt):
            return ctx.enter_context(nc.psum_tensor(name, shape, dt))

        def count(name, **kw):
            return Count(sems, nc, name, **kw)

        def pair(name, shape, dt):
            return [sb(f"{name}{p}", shape, dt) for p in (0, 1)]

        ident_f, ident_b, ones_b = kept["ident_f"], kept["ident_b"], kept["ones_b"]
        dest_all, seen = kept["dest_all"], kept["seen"]
        before, gw, eb, index8, region, eps, half_neg = (
            kept[n] for n in ("before", "gw", "eb", "index8", "region", "eps", "half_neg"))

        qf, kf = pair("qf", [P, P], F32), pair("kf", [P, P], F32)
        q_h, q_l = pair("q_h", [P, P], F32R), pair("q_l", [P, P], F32R)
        k_h, k_l = sb("k_h", [P, 2 * L], F32R), sb("k_l", [P, 2 * L], F32R)
        att_h, att_l = sb("att_h", [P, 2 * BT, L], F32R), sb("att_l", [P, 2 * BT, L], F32R)
        expd, att = sb("expd", [P, L], F32), sb("att", [P, L], F32)
        nmax, rsum, rinv = (pair(n, [P, 1], F32) for n in ("nmax", "rsum", "rinv"))

        xs = pair("xs", [P, D], F32)
        xr = sb("xr", [P, D], F32)
        xn = sb("xn", [P, D], F32)
        xnt_h, xnt_l = pair("xnt_h", [P, DC, P], F32R), pair("xnt_l", [P, DC, P], F32R)
        x1 = sb("x1", [P, D], F32)
        x2 = pair("x2", [P, D], F32)
        x2t = sb("x2t", [P, DC, P], F32)
        bs = [pair("bs0", [P, 2, 6], F32), pair("bs1", [P, 2, 6], F32)]
        mv = [pair("mv0", [P, 2], F32), pair("mv1", [P, 2], F32)]
        ve = [pair("ve0", [P, 1], F32), pair("ve1", [P, 1], F32)]
        rstd = [pair("rstd0", [P, 1], F32), pair("rstd1", [P, 1], F32)]

        logit = pair("logit", [P, E], F32)
        rank = pair("rank", [P, E], F32)
        sig_e = pair("sig_e", [P, E], F32)
        score = pair("score", [P, E], F32)
        sel = pair("sel", [P, E], F32)
        top = pair("top", [P, E], F32)
        top_i = pair("top_i", [P, E], U32)
        top_e = pair("top_e", [P, TOPK], F32)
        one_hot = [pair("hot0_", [P, E], F32), pair("hot1_", [P, E], F32)]
        mask = pair("mask", [P, E], BF16)
        junk = pair("junk", [P, E], F32)
        wsc = pair("wsc", [P, TOPK], F32)
        destf = pair("destf", [P, TOPK], F32)
        dest = [pair("dest0_", [P, 1], I32), pair("dest1_", [P, 1], I32)]
        disp = [sb("disp0", [P, D], BF16), sb("disp1", [P, D], BF16)]

        o_ps = [ps(f"o_ps{p}", [P, L], F32) for p in (0, 1)]
        e_ps = ps("e_ps", [P, L], F32)
        t_ps = ps("t_ps", [P, L], F32)
        gate_ps, rank_ps = t_ps[:, 0:E], t_ps[:, E:2 * E]

        d_first = sems.enter_context(nc.semaphore("d_first"))
        c_first = sems.enter_context(nc.semaphore("c_first"))
        d_x, d_xr = Loads(sems, nc, "d_x"), Loads(sems, nc, "d_xr")
        d_q, d_k = Loads(sems, nc, "d_q"), Loads(sems, nc, "d_k", first=BT)
        d_x1, d_x2t = Loads(sems, nc, "d_x1"), Loads(sems, nc, "d_x2t")
        d_disp = Loads(sems, nc, "d_disp", n=TOPK, lead=0)
        spare = kept["spare"]
        v_xstat = count("v_xstat", per=3)
        g_rstd = [count("g_rstd0", per=2), count("g_rstd1", per=2)]
        v_xn = count("v_xn")
        p_xt = count("p_xt")
        a_xth = count("a_xth")
        v_xtl = count("v_xtl")
        p_mm = count("p_mm")
        v_x1 = count("v_x1", per=4)
        v_x2 = count("v_x2")
        p_x2t = count("p_x2t")
        a_x2t = count("a_x2t")
        p_gate = count("p_gate")
        v_gcopy = count("v_gcopy")
        a_sig = count("a_sig")
        v_route = count("v_route", per=11)
        p_rank = count("p_rank")
        v_rcopy = count("v_rcopy")
        v_dest = count("v_dest", per=6)
        a_disp = count("a_disp")
        a_qh, a_kh = count("a_qh"), count("a_kh", first=BT)
        g_ql, g_kl = count("g_ql"), count("g_kl", first=BT)
        p_en = count("p_en")
        v_max = count("v_max")
        a_exp = count("a_exp")
        v_inv = count("v_inv")
        a_att = count("a_att")
        p_att = count("p_att")
        a_atth = count("a_atth")
        v_attl = count("v_attl")

        K_LEAD = 2 * BT + 2
        E_LEAD = BT + 2

        def columns(half, t):
            return half[:, bass.ds(t.at & BT, BT), bass.ds((t.at & (BT - 1)) * P, P)]

        with nc.Block() as block:
            @block.sync
            def _(eng):
                for s in (d_x, d_xr, d_q, d_k):
                    s.prime(eng)
                eng.dma_start(expd[:].rearrange("p (t n) -> p t n", n=P),
                              k_d[0:BT].rearrange("t p n -> p t n")).then_inc(d_first, 16)

                def step(now, on):
                    if "st" in on:
                        t = now - 1
                        v_x1.wait(eng, t.at, 1)
                        d_x1.inc(eng.dma_start(x1_d[bass.ts(t.at, P), :], x1[:]), t)
                    if "st2" in on:
                        t = now - 2
                        a_x2t.wait(eng, t.at)
                        d_x2t.inc(eng.dma_start(xt_d[t.at], x2t[:].rearrange("p c n -> p (c n)")), t)
                    if "xr" in on:
                        t = now
                        v_x1.wait(eng, t.at - 1, 1)
                        d_xr.inc(eng.dma_start(xr[:], x[t.at]), t)
                    if "x" in on:
                        t = now + 3
                        v_xn.wait(eng, t.at - 2)
                        d_x.inc(eng.dma_start(xs[t.par][:], x[t.at]), t)
                    for name, off, dst, src, sem, hi, lo in (("k", K_LEAD + 1, kf, k_d, d_k, a_kh, g_kl),
                                                             ("q", E_LEAD + 2, qf, q_d, d_q, a_qh, g_ql)):
                        if name in on:
                            t = now + off
                            hi.wait(eng, t.at - 2)
                            lo.wait(eng, t.at - 2)
                            sem.inc(eng.dma_start(dst[t.par][:], src[t.at]), t)

                pipeline(eng, {"k": (K_LEAD + 1, BT, NT), "q": (E_LEAD + 2, 0, NT), "x": (3, 0, NT),
                               "xr": (0, 0, NT), "st": (-1, 0, NT), "st2": (-2, 0, NT)}, step)
                for t in (NT - 2, NT - 1):
                    d_x1.wait(eng, Tile(t // 2, t % 2))
                    d_x2t.wait(eng, Tile(t // 2, t % 2))

            @block.gpsimd
            def _(eng):
                for s in (*g_rstd, g_ql, g_kl):
                    s.prime(eng)
                def deviation(t, i):
                    (v_x1 if i else v_xstat).wait(eng, t.at)
                    (v_x2 if i else v_xn).wait(eng, t.at - 2)
                    g_rstd[i].inc(eng.tensor_tensor(ve[i][t.par][:], mv[i][t.par][:, 1:2], eps[:], ALU.add))
                    g_rstd[i].wait(eng, t.at, 1)
                    g_rstd[i].inc(eng.tensor_tensor(rstd[i][t.par][:], ve[i][t.par][:], half_neg[:],
                                                    ALU.pow))

                def step(now, on):
                    if "r1" in on:
                        deviation(now - 1, 1)
                    if "disp" in on:
                        t = now - 3
                        a_disp.wait(eng, t.at)
                        v_dest.wait(eng, t.at)
                        for k in range(TOPK):
                            settled(eng, spare)
                            d_disp.inc(eng.indirect_dma_start(
                                rows_d, bass.IndirectOffsetOnAxis(ap=dest[k][t.par][:, 0:1], axis=0),
                                disp[k][:], None), t)
                    if "r0" in on:
                        deviation(now + 2, 0)
                    if "k" in on:
                        t = now + K_LEAD
                        at = bass.ts(t.at & (2 * BT - 1), P)
                        a_kh.wait(eng, t.at)
                        g_kl.inc(eng.tensor_tensor(k_l[:, at], kf[t.par][:], k_h[:, at].bitcast(F32), ALU.subtract))
                    if "q" in on:
                        t = now + E_LEAD + 1
                        a_qh.wait(eng, t.at)
                        g_ql.inc(eng.tensor_tensor(q_l[t.par][:], qf[t.par][:], q_h[t.par][:].bitcast(F32),
                                                   ALU.subtract))

                pipeline(eng, {"k": (K_LEAD, BT, NT), "q": (E_LEAD + 1, 0, NT), "r1": (-1, 0, NT),
                               "r0": (2, 0, NT), "disp": (-3, 0, NT)}, step)
                for t in (NT - 2, NT - 1):
                    d_disp.wait(eng, Tile(t // 2, t % 2))

            @block.scalar
            def _(eng):
                for s in (a_xth, a_x2t, a_sig, a_disp, a_qh, a_kh, a_exp, a_att, a_atth):
                    s.prime(eng)
                eng.wait_ge(d_first, 16)
                eng.copy(k_h[:, 0:L], expd[:]).then_inc(c_first, 1)

                def step(now, on):
                    if "sig" in on:
                        t = now - 2
                        v_gcopy.wait(eng, t.at)
                        v_route.wait(eng, t.at - 2)
                        a_sig.inc(eng.activation(sig_e[t.par][:], logit[t.par][:], ACT.Exp, scale=-1.0))
                    if "xt" in on:
                        t = now + 1
                        p_xt.wait(eng, t.at)
                        p_mm.wait(eng, t.at - 2)
                        a_xth.inc(eng.copy(xnt_h[t.par][:], t_ps[:]))
                    if "disp" in on:
                        t = now - 3
                        v_route.wait(eng, t.at)
                        if "sent" in on:
                            d_disp.wait(eng, t - 1)
                        for k in range(TOPK):
                            ins = eng.activation(disp[k][:], x2[t.par][:], ACT.Copy,
                                                 scale=wsc[t.par][:, k:k + 1])
                        a_disp.inc(ins)
                    if "sm" in on:
                        t = now + E_LEAD - 1
                        v_max.wait(eng, t.at)
                        v_inv.wait(eng, t.at - 2)
                        a_att.wait(eng, t.at - 1)
                        a_exp.inc(eng.activation(expd[:], e_ps[:], ACT.Exp, bias=nmax[t.par][:],
                                                 accum_out=rsum[t.par][:]))
                    if "ta" in on:
                        t = now + E_LEAD - 2
                        p_att.wait(eng, t.at)
                        p_mm.wait(eng, t.at - BT - 1)
                        a_atth.inc(eng.copy(columns(att_h, t), t_ps[:].rearrange("p (c n) -> p c n", n=P)))
                    if "x2t" in on:
                        t = now - 1
                        p_x2t.wait(eng, t.at)
                        p_gate.wait(eng, t.at - 1)
                        d_x2t.wait(eng, t - 1)
                        a_x2t.inc(eng.copy(x2t[:], t_ps[:]))
                    if "sm" in on:
                        t = now + E_LEAD - 1
                        v_inv.wait(eng, t.at)
                        p_att.wait(eng, t.at - 1)
                        a_att.inc(eng.activation(att[:], expd[:], ACT.Copy, scale=rinv[t.par][:]))
                    if "k" in on:
                        t = now + K_LEAD
                        d_k.wait(eng, t)
                        p_en.wait(eng, t.at - BT - 1)
                        a_kh.inc(eng.copy(k_h[:, bass.ts(t.at & (2 * BT - 1), P)], kf[t.par][:]))
                    if "q" in on:
                        t = now + E_LEAD + 1
                        d_q.wait(eng, t)
                        p_en.wait(eng, t.at - 2)
                        a_qh.inc(eng.copy(q_h[t.par][:], qf[t.par][:]))

                pipeline(eng, {"k": (K_LEAD, BT, NT), "q": (E_LEAD + 1, 0, NT), "xt": (1, 0, NT),
                               "ta": (E_LEAD - 2, 0, NT), "sm": (E_LEAD - 1, 0, NT),
                               "sig": (-2, 0, NT), "x2t": (-1, 0, NT), "disp": (-3, 0, NT), "sent": (-4, 0, NT)}, step)

            @block.vector
            def _(eng):
                for s in (v_xstat, v_xn, v_xtl, v_x1, v_x2, v_gcopy, v_route, v_rcopy, v_dest,
                          v_max, v_inv, v_attl, d_x1, d_x2t):
                    s.prime(eng)

                eng.wait_ge(c_first, 1)
                eng.tensor_tensor(k_l[:, 0:L], expd[:], k_h[:, 0:L].bitcast(F32), ALU.subtract).then_inc(c_first, 1)

                def stats(src, i, t, counts, k0):
                    for h in (0, 1):
                        counts.inc(eng.bn_stats(bs[i][t.par][:, h, :], src[:, h * 512:(h + 1) * 512]))
                    counts.wait(eng, t.at, k0 + 2)
                    settled(eng, spare)
                    counts.inc(eng.bn_aggr(mv[i][t.par][:], bs[i][t.par][:].rearrange("p a b -> p (a b)")))

                def normalize(dst, src, i, t, counts):
                    counts.inc(eng.tensor_scalar(dst, src, mv[i][t.par][:, 0:1], rstd[i][t.par][:, 0:1],
                                                 ALU.subtract, ALU.mult))

                def step(now, on):
                    if "gcopy" in on:
                        t = now - 2
                        p_gate.wait(eng, t.at)
                        a_sig.wait(eng, t.at - 2)
                        v_gcopy.inc(eng.tensor_copy(logit[t.par][:], gate_ps))
                    if "rcopy" in on:
                        t = now - 3
                        p_rank.wait(eng, t.at)
                        v_rcopy.inc(eng.tensor_copy(rank[t.par][:], rank_ps))
                    if "x1" in on:
                        t = now - 1
                        p_mm.wait(eng, t.at)
                        d_x1.wait(eng, t - 1)
                        g_rstd[1].wait(eng, t.at - 2, 1)
                        d_xr.wait(eng, t)
                        v_x1.inc(eng.tensor_tensor(x1[:], o_ps[t.par][:], xr[:], ALU.add))
                        v_x1.wait(eng, t.at, 1)
                        stats(x1, 1, t, v_x1, 1)
                    if "dest" in on:
                        t = now - 3
                        p, n = t.par, 0

                        def dlink(ins):
                            nonlocal n
                            n += 1
                            v_dest.inc(ins)
                            v_dest.wait(eng, t.at, n)

                        v_rcopy.wait(eng, t.at)
                        if "sent" in on:
                            d_disp.wait(eng, t - 2)
                        dlink(eng.tensor_tensor(seen[1 - p][:], seen[p][:], mask[p][:], ALU.add))
                        dlink(eng.tensor_tensor(rank[p][:], rank[p][:], region[:], ALU.add))
                        for k in range(TOPK):
                            dlink(eng.tensor_tensor_reduce(junk[p][:, 0:E], one_hot[k][p][:], rank[p][:], 1.0,
                                                           0.0, ALU.mult, ALU.add, destf[p][:, k:k + 1]))
                        dlink(eng.tensor_copy(dest_all[:, t.at, :], destf[p][:]))
                        eng.tensor_copy(dest[0][p][:], destf[p][:, 0:1])
                        dlink(eng.tensor_copy(dest[1][p][:], destf[p][:, 1:2]))
                    if "xt" in on:
                        t = now + 1
                        a_xth.wait(eng, t.at)
                        v_xtl.inc(eng.tensor_tensor(xnt_l[t.par][:].rearrange("p c n -> p (c n)"), t_ps[:],
                                                    xnt_h[t.par][:].rearrange("p c n -> p (c n)").bitcast(F32),
                                                    ALU.subtract))
                    if "sm" in on:
                        t = now + E_LEAD - 1
                        p_en.wait(eng, t.at)
                        a_exp.wait(eng, t.at - 2)
                        v_max.inc(eng.tensor_reduce(nmax[t.par][:], e_ps[:], AX, ALU.max, negate=True))
                    if "x1" in on:
                        t = now - 1
                        g_rstd[1].wait(eng, t.at)
                        p_x2t.wait(eng, t.at - 2)
                        a_disp.wait(eng, t.at - 2)
                        normalize(x2[t.par][:], x1[:], 1, t, v_x2)
                    if "xs" in on:
                        t = now + 2
                        d_x.wait(eng, t)
                        g_rstd[0].wait(eng, t.at - 2, 1)
                        stats(xs[t.par], 0, t, v_xstat, 0)
                    if "ta" in on:
                        t = now + E_LEAD - 2
                        a_atth.wait(eng, t.at)
                        v_attl.inc(eng.tensor_tensor(columns(att_l, t), t_ps[:].rearrange("p (c n) -> p c n", n=P),
                                                     columns(att_h, t).bitcast(F32), ALU.subtract))
                    if "route" in on:
                        t = now - 2
                        p, n = t.par, 0

                        def link(ins=None):
                            nonlocal n
                            if ins:
                                n += 1
                                v_route.inc(ins)
                            v_route.wait(eng, t.at, n)

                        a_sig.wait(eng, t.at)
                        a_disp.wait(eng, t.at - 2)
                        link(eng.tensor_scalar(score[p][:], sig_e[p][:], 1.0, None, ALU.add))
                        link(eng.reciprocal(score[p][:], score[p][:]))
                        link(eng.tensor_tensor(sel[p][:], score[p][:], eb[:], ALU.add))
                        settled(eng, spare)
                        link(eng.max(top[p][:], sel[p][:]))
                        settled(eng, spare)
                        link(eng.max_index(top_i[p][:], top[p][:], sel[p][:]))
                        link(eng.tensor_copy(top_e[p][:], top_i[p][:, 0:TOPK]))
                        for k in range(TOPK):
                            link(eng.tensor_scalar(one_hot[k][p][:], index8[:], top_e[p][:, k:k + 1], None,
                                                   ALU.is_equal))
                        p_rank.wait(eng, t.at - 2)
                        link(eng.tensor_tensor(mask[p][:], one_hot[0][p][:], one_hot[1][p][:], ALU.add))
                        for k in range(TOPK):
                            link(eng.tensor_tensor_reduce(junk[p][:, 0:E], one_hot[k][p][:], score[p][:], 1.0,
                                                          0.0, ALU.mult, ALU.add, wsc[p][:, k:k + 1]))
                    if "sm" in on:
                        t = now + E_LEAD - 1
                        a_exp.wait(eng, t.at)
                        a_att.wait(eng, t.at - 2)
                        v_inv.inc(eng.reciprocal(rinv[t.par][:], rsum[t.par][:]))
                    if "xn" in on:
                        t = now + 2
                        g_rstd[0].wait(eng, t.at)
                        p_xt.wait(eng, t.at - 1)
                        normalize(xn[:], xs[t.par][:], 0, t, v_xn)

                pipeline(eng, {"x1": (-1, 0, NT), "gcopy": (-2, 0, NT), "rcopy": (-3, 0, NT),
                               "xt": (1, 0, NT), "ta": (E_LEAD - 2, 0, NT),
                               "sm": (E_LEAD - 1, 0, NT), "xs": (2, 0, NT), "route": (-2, 0, NT),
                               "dest": (-3, 0, NT), "sent": (-5, 0, NT), "xn": (2, 0, NT)}, step)

            @block.tensor
            def _(eng):
                for s in (p_xt, p_mm, p_x2t, p_gate, p_rank, p_en, p_att):
                    s.prime(eng)

                eng.wait_ge(c_first, 2)

                def transposes(src):
                    for c in range(DC):
                        ins = eng.transpose(t_ps[:, c * P:(c + 1) * P], src[:, c * P:(c + 1) * P], ident_f[:])
                    return ins

                def sums(t, chunks):
                    parity = t.at & BT
                    for c in chunks:
                        for xt, at in ((xnt_h, att_h), (xnt_h, att_l), (xnt_l, att_h)):
                            for h in (0, 1):
                                ins = eng.matmul(o_ps[t.par][:, h * 512:(h + 1) * 512], xt[t.par][:, c, :],
                                                 at[:, parity + c, h * 512:(h + 1) * 512],
                                                 start=(c == 0 and xt is xnt_h and at is att_h),
                                                 stop=(c == DC - 1 and xt is xnt_l))
                    return ins

                def copied(now, on):
                    if "ta_last" in on:
                        v_attl.wait(eng, now.at + E_LEAD - 3)
                    if "x2t_last" in on:
                        v_gcopy.wait(eng, now.at - 2)
                    if "rank_last" in on:
                        v_rcopy.wait(eng, now.at - 3)

                def step(now, on):
                    if "xt" in on:
                        t = now + 1
                        v_xn.wait(eng, t.at)
                        copied(now, on)
                        p_xt.inc(transposes(xn))
                    if "mm" in on:
                        t = now
                        v_xtl.wait(eng, t.at)
                        v_attl.wait(eng, t.at | (BT - 1))
                        v_x1.wait(eng, t.at - 2, 1)
                        sums(t, range(0, 3))
                    if "ta" in on:
                        t = now + E_LEAD - 2
                        a_att.wait(eng, t.at)
                        if "xt" in on:
                            v_xtl.wait(eng, now.at + 1)
                        else:
                            copied(now, on)
                        p_att.inc(transposes(att))
                    if "mm" in on:
                        sums(now, range(3, 6))
                    if "x2t" in on:
                        t = now - 1
                        v_x2.wait(eng, t.at)
                        if "ta" in on:
                            v_attl.wait(eng, now.at + E_LEAD - 2)
                        elif "xt" in on:
                            v_xtl.wait(eng, now.at + 1)
                        else:
                            copied(now, on)
                        p_x2t.inc(transposes(x2[t.par]))
                    if "mm" in on:
                        p_mm.inc(sums(now, range(6, DC)))
                    if "rank" in on:
                        t = now - 2
                        v_route.wait(eng, t.at)
                        v_dest.wait(eng, t.at - 1, 1)
                        if "x2t" in on:
                            a_x2t.wait(eng, t.at + 1)
                        else:
                            copied(now, on)
                        eng.matmul(rank_ps, before[:], mask[t.par][:], start=True, stop=False)
                        p_rank.inc(eng.matmul(rank_ps, ones_b[:], seen[t.par][:], start=False, stop=True))
                    if "x2t" in on:
                        t = now - 1
                        a_x2t.wait(eng, t.at)
                        for c in range(DC):
                            ins = eng.matmul(gate_ps, x2t[:, c, :], gw[:, c, :], start=(c == 0),
                                             stop=(c == DC - 1))
                        p_gate.inc(ins)
                    if "en" in on:
                        t = now + E_LEAD
                        g_ql.wait(eng, t.at)
                        g_kl.wait(eng, t.at | (BT - 1))
                        a_exp.wait(eng, t.at - 1)
                        base = (t.at & BT) * P
                        for q, k in ((q_h, k_h), (q_h, k_l), (q_l, k_h)):
                            for h in (0, 1):
                                ins = eng.matmul(e_ps[:, h * 512:(h + 1) * 512], q[t.par][:],
                                                 k[:, bass.ds(base + h * 512, 512)],
                                                 start=(q is q_h and k is k_h), stop=(q is q_l))
                        p_en.inc(ins)

                pipeline(eng, {"xt": (1, 0, NT), "mm": (0, 0, NT), "ta": (E_LEAD - 2, 0, NT),
                               "ta_last": (E_LEAD - 3, 0, NT), "x2t": (-1, 0, NT), "x2t_last": (-2, 0, NT),
                               "rank": (-2, 0, NT), "rank_last": (-3, 0, NT),
                               "en": (E_LEAD, 0, NT)}, step)


def plan(nc, sems, kept, table, rows_d):
    with ExitStack() as ctx:
        def sb(name, shape, dt):
            return ctx.enter_context(nc.sbuf_tensor(name, shape, dt))

        zeros = sb("zeros", [P, D], BF16)
        cnt_i = sb("cnt_i", [P, E], I32)
        rows_i = sb("rows_i", [P, 2, E], I32)
        tiles = sb("tiles", [P, E], F32)
        ends = sb("ends", [P, E], F32)
        base = sb("base", [P, E], F32)
        moved = sb("moved", [P, E], F32)
        step = sb("step", [P, E], F32)
        part = sb("part", [P, NT * TOPK], F32)
        slot = [sb(f"slot{p}", [P, NT * TOPK], F32) for p in (0, 1)]
        index = sb("index", [1, P], F32)
        expert = [sb(f"expert{p}", [1, P], F32) for p in (0, 1)]
        first = [sb(f"first{p}", [1, P], F32) for p in (0, 1)]
        work = [sb(f"work{n}", [1, P], F32) for n in range(5)]
        cnt = ctx.enter_context(nc.psum_tensor("cnt", [P, E], F32))
        s_pool = sems.enter_context(nc.semaphore("s_pool"))
        s_cnt = sems.enter_context(nc.semaphore("s_cnt"))
        s_v = sems.enter_context(nc.semaphore("s_v"))
        s_tail = sems.enter_context(nc.semaphore("s_tail"))

        with nc.Block() as block:
            @block.gpsimd
            def _(eng):
                eng.iota(index[:], pattern=[[1, P]], base=0, channel_multiplier=0,
                         allow_small_or_imprecise_dtypes=True).then_inc(s_pool, 1)
                eng.iota(base[:], pattern=[[REG, E]], base=0, channel_multiplier=0,
                         allow_small_or_imprecise_dtypes=True).then_inc(s_pool, 1)
                eng.memset(zeros[:], 0.0).then_inc(s_pool, 1)

            @block.tensor
            def _(eng):
                eng.matmul(cnt[:], kept["ones_b"][:], kept["seen"][NT % 2][:], start=True,
                           stop=True).then_inc(s_cnt, 1)

            @block.vector
            def _(eng):
                n = 0

                def link(ins):
                    nonlocal n
                    n += 1
                    ins.then_inc(s_v, 1)
                    eng.wait_ge(s_v, n)

                eng.wait_ge(s_cnt, 1)
                eng.wait_ge(s_pool, 3)
                link(eng.tensor_scalar(cnt_i[:], cnt[:], float(P - 1), None, ALU.add))
                link(eng.tensor_tensor(rows_i[:, 1, :], cnt[:], base[:], ALU.add))
                link(eng.tensor_scalar(rows_i[:, 0, :], cnt_i[:], P.bit_length() - 1, None,
                                       ALU.arith_shift_right))
                link(eng.tensor_copy(tiles[:], rows_i[:, 0, :]))
                link(eng.tensor_copy(ends[:, 0:1], tiles[:, 0:1]))
                for e in range(1, E):
                    link(eng.tensor_tensor(ends[:, e:e + 1], ends[:, e - 1:e], tiles[:, e:e + 1], ALU.add))
                link(eng.tensor_scalar(expert[0][:], index[:], 0.0, None, ALU.mult))
                link(eng.tensor_scalar(first[0][:], index[:], 0.0, None, ALU.mult))
                for e in range(E):
                    a, b = e % 2, 1 - e % 2
                    link(eng.scalar_tensor_tensor(expert[b][:], index[:], ends[0:1, e:e + 1], expert[a][:],
                                                  ALU.is_ge, ALU.add))
                    link(eng.tensor_scalar(work[0][:], index[:], ends[0:1, e:e + 1], tiles[0:1, e:e + 1],
                                           ALU.is_ge, ALU.mult))
                    link(eng.tensor_tensor(first[b][:], first[a][:], work[0][:], ALU.add))
                link(eng.tensor_tensor(work[0][:], index[:], first[0][:], ALU.subtract))
                link(eng.tensor_scalar(work[1][:], expert[0][:], float(REG), None, ALU.mult))
                link(eng.scalar_tensor_tensor(table[:, 0, :], work[0][:], float(P), work[1][:], ALU.mult, ALU.add))
                link(eng.tensor_scalar(work[2][:], expert[0][:], float(E - 1), None, ALU.min))
                link(eng.tensor_copy(table[:, 1, :], work[2][:]))
                link(eng.tensor_copy(kept["ends"][:], ends[0:1, :]))
                link(eng.tensor_tensor(moved[:], ends[:], tiles[:], ALU.subtract))
                link(eng.scalar_tensor_tensor(moved[:], moved[:], float(P), base[:], ALU.mult, ALU.subtract))
                link(eng.tensor_copy(step[:, 0:1], moved[:, 0:1]))
                link(eng.tensor_tensor(step[:, 1:E], moved[:, 1:E], moved[:, 0:E - 1], ALU.subtract))
                dest = kept["dest_all"][:].rearrange("p t k -> p (t k)")
                link(eng.tensor_copy(slot[0][:], dest))
                for e in range(E):
                    a, b = e % 2, 1 - e % 2
                    link(eng.tensor_scalar(part[:], dest, float(e * REG), step[:, e:e + 1], ALU.is_ge, ALU.mult))
                    link(eng.tensor_tensor(slot[b][:], slot[a][:], part[:], ALU.add))
                link(eng.tensor_copy(kept["slot_all"][:].rearrange("p t k -> p (t k)"), slot[E % 2][:]))

            @block.sync
            def _(eng):
                eng.wait_ge(s_v, 2)
                for e in range(E):
                    row = eng.value_load(rows_i[0:1, 1, e:e + 1], min_val=e * REG, max_val=e * REG + TOK)
                    eng.dma_start(rows_d[bass.ds(row, P), :], zeros[:]).then_inc(s_tail, 16)
                eng.wait_ge(s_tail, 16 * E)


def routed(nc, sems, kept, table, w13, w2, rows_d, y_d):
    with ExitStack() as ctx:
        def sb(name, shape, dt):
            return ctx.enter_context(nc.sbuf_tensor(name, shape, dt))

        def pair(name, shape, dt):
            return [sb(f"{name}{p}", shape, dt) for p in (0, 1)]

        def count(name, **kw):
            return Count(sems, nc, name, **kw)

        ident_b = kept["ident_b"]
        wu = sb("wu", [P, 2, DC, 2 * HID], BF16)
        wd = sb("wd", [P, 2, HC, D], BF16)
        g = pair("g", [P, D], BF16)
        gt = pair("gt", [P, DC, P], BF16)
        sil = sb("sil", [P, HID], F32)
        h = pair("h", [P, HID], BF16)
        ht = pair("ht", [P, HC, P], BF16)
        y = pair("y", [P, D], BF16)
        up_ps = ctx.enter_context(nc.psum_tensor("up_ps", [P, 4, 512], F32))
        down_ps = ctx.enter_context(nc.psum_tensor("down_ps", [P, D], F32))
        gt_ps = ctx.enter_context(nc.psum_tensor("gt_ps", [P, DC, P], BF16))
        ht_ps = ctx.enter_context(nc.psum_tensor("ht_ps", [P, DC, P], BF16))

        NW = 4
        d_w = [sems.enter_context(nc.semaphore(f"d_we{p}")) for p in (0, 1)]
        g_w = sems.enter_context(nc.semaphore("g_w"))
        d_g, d_y = Loads(sems, nc, "d_g"), Loads(sems, nc, "d_y")
        p_gt = count("p_gt")
        a_gt = count("a_gt")
        p_up = count("p_up")
        a_sil = count("a_sil", per=2)
        v_h = count("v_h", per=2)
        p_ht = count("p_ht")
        v_ht = count("v_ht", per=2)
        p_dn = count("p_dn")
        a_y = count("a_y")
        v_y = count("v_y")

        with nc.Block() as block:
            @block.gpsimd
            def _(eng):
                for e in range(E):
                    if e >= 1:
                        eng.wait_ge(d_w[1 - e % 2], (e + 1) // 2 * 16 * NW)
                        eng.sem_inc(g_w, 1)
                    if e >= 2:
                        last = eng.value_load(kept["ends"][0:1, e - 2:e - 1], min_val=0, max_val=ET)
                        eng.wait_ge(p_dn.sem, last + p_dn.lead)
                        settled(eng, kept["spare"])
                    for c in (0, 1):
                        cs = slice(c * DC // 2, (c + 1) * DC // 2)
                        eng.dma_start(wu[:, e % 2, cs, :], w13[e][:, cs, :]).then_inc(d_w[e % 2], 16)
                    eng.dma_start(wd[:, e % 2, 0:HC - 1, :],
                                  w2[e][0:(HC - 1) * P, :].rearrange("(c p) n -> p c n", p=P)).then_inc(d_w[e % 2], 16)
                    eng.dma_start(wd[0:HTAIL, e % 2, HC - 1, :], w2[e][(HC - 1) * P:HID, :]).then_inc(d_w[e % 2], 16)
                eng.wait_ge(d_w[1 - E % 2], (E + 1) // 2 * 16 * NW)
                eng.sem_inc(g_w, 1)

            @block.sync
            def _(eng):
                for s in (d_g,):
                    s.prime(eng)

                def step(now, on):
                    if "g" in on:
                        t = now + 3
                        p_gt.wait(eng, t.at - 2)
                        settled(eng, kept["spare"])
                        row = eng.value_load(table[0:1, 0, bass.ds(t.at, 1)], min_val=0, max_val=GROWS - P)
                        d_g.inc(eng.dma_start(g[t.par][:], rows_d[bass.ds(row, P), :]), t)
                    if "y" in on:
                        t = now - 1
                        a_y.wait(eng, t.at)
                        v_y.wait(eng, t.at)
                        d_y.inc(eng.dma_start(y_d[bass.ts(t.at, P), :], y[t.par][:]), t)

                pipeline(eng, {"g": (3, 0, ET), "y": (-1, 0, ET)}, step)
                for t in (ET - 2, ET - 1):
                    d_y.wait(eng, Tile(t // 2, t % 2))

            @block.scalar
            def _(eng):
                for s in (a_gt, a_sil, a_y):
                    s.prime(eng)

                def step(now, on):
                    if "gt" in on:
                        t = now + 1
                        p_gt.wait(eng, t.at)
                        p_up.wait(eng, t.at - 2)
                        a_gt.inc(eng.copy(gt[t.par][:], gt_ps[:]))
                    if "up" in on:
                        t = now
                        p_up.wait(eng, t.at)
                        for i in (0, 1):
                            v_h.wait(eng, t.at - 1, i + 1)
                            a_sil.inc(eng.activation(sil[:, i * HALF:(i + 1) * HALF], up_ps[:, i, 0:HALF], ACT.Silu))
                    if "y" in on:
                        t = now - 1
                        p_dn.wait(eng, t.at)
                        d_y.wait(eng, t - 2)
                        a_y.inc(eng.copy(y[t.par][:, 0:512], down_ps[:, 0:512]))

                pipeline(eng, {"gt": (1, 0, ET), "up": (0, 0, ET), "y": (-1, 0, ET)}, step)

            @block.vector
            def _(eng):
                for s in (v_h, v_ht, v_y, d_y):
                    s.prime(eng)

                def step(now, on):
                    if "ht" in on:
                        t = now - 1
                        p_ht.wait(eng, t.at)
                        p_dn.wait(eng, t.at - 2)
                        v_ht.inc(eng.tensor_copy(ht[t.par][:, 0:HC - 1, :], ht_ps[:, 0:HC - 1, :]))
                        v_ht.inc(eng.tensor_copy(ht[t.par][0:HTAIL, HC - 1, :], ht_ps[0:HTAIL, HC - 1, :]))
                    if "up" in on:
                        t = now
                        p_ht.wait(eng, t.at - 2)
                        for i in (0, 1):
                            a_sil.wait(eng, t.at, i + 1)
                            v_h.inc(eng.tensor_tensor(h[t.par][:, i * HALF:(i + 1) * HALF],
                                                      sil[:, i * HALF:(i + 1) * HALF], up_ps[:, 2 + i, 0:HALF],
                                                      ALU.mult))
                    if "y" in on:
                        t = now - 1
                        p_dn.wait(eng, t.at)
                        d_y.wait(eng, t - 2)
                        v_y.inc(eng.tensor_copy(y[t.par][:, 512:], down_ps[:, 512:]))

                pipeline(eng, {"ht": (-1, 0, ET), "up": (0, 0, ET), "y": (-1, 0, ET)}, step)

            @block.tensor
            def _(eng):
                for s in (p_gt, p_up, p_ht, p_dn):
                    s.prime(eng)

                def step(now, on):
                    if "gt" in on:
                        t = now + 1
                        d_g.wait(eng, t)
                        a_gt.wait(eng, t.at - 1)
                        for c in range(DC):
                            ins = eng.transpose(gt_ps[:, c, :], g[t.par][:, c * P:(c + 1) * P], ident_b[:])
                        p_gt.inc(ins)
                    if "up" in on:
                        t = now
                        expert = eng.value_load(table[0:1, 1, bass.ds(t.at, 1)], min_val=0, max_val=E - 1)
                        buf = expert & 1
                        eng.wait_ge(g_w, expert + 1)
                        a_gt.wait(eng, t.at)
                        v_h.wait(eng, t.at - 1)
                        for c in range(DC):
                            for i in range(4):
                                ins = eng.matmul(up_ps[:, i, 0:HALF], gt[t.par][:, c, :],
                                                 wu[:, buf, c, i * HALF:(i + 1) * HALF], start=c == 0,
                                                 stop=c == DC - 1)
                        p_up.inc(ins)
                    if "dn" in on:
                        t = now - 1
                        expert = eng.value_load(table[0:1, 1, bass.ds(t.at, 1)], min_val=0, max_val=E - 1)
                        buf = expert & 1
                        v_ht.wait(eng, t.at)
                        a_y.wait(eng, t.at - 1)
                        v_y.wait(eng, t.at - 1)
                        for c in range(HC):
                            k = P if c < HC - 1 else HTAIL
                            for i in (0, 1):
                                ins = eng.matmul(down_ps[:, i * 512:(i + 1) * 512], ht[t.par][0:k, c, :],
                                                 wd[0:k, buf, c, i * 512:(i + 1) * 512], start=c == 0,
                                                 stop=c == HC - 1)
                        p_dn.inc(ins)
                    if "up" in on:
                        t = now
                        v_h.wait(eng, t.at)
                        v_ht.wait(eng, t.at - 1)
                        for c in range(HC):
                            k = P if c < HC - 1 else HTAIL
                            ins = eng.transpose(ht_ps[0:k, c, :], h[t.par][:, c * P:c * P + k], ident_b[:])
                        p_ht.inc(ins)

                pipeline(eng, {"gt": (1, 0, ET), "up": (0, 0, ET), "dn": (-1, 0, ET)}, step)


def shared(nc, sems, kept, sw13, sw2, x1_d, xt_d, y_d, out):
    with ExitStack() as ctx:
        def sb(name, shape, dt):
            return ctx.enter_context(nc.sbuf_tensor(name, shape, dt))

        def pair(name, shape, dt):
            return [sb(f"{name}{p}", shape, dt) for p in (0, 1)]

        def count(name, **kw):
            return Count(sems, nc, name, **kw)

        ident_f, slot_all = kept["ident_f"], kept["slot_all"]
        wu_h, wu_l = sb("wu_h", [P, DC, 2 * HID], F32R), sb("wu_l", [P, DC, 2 * HID], F32R)
        wd_h, wd_l = sb("wd_h", [P, HC, D], F32R), sb("wd_l", [P, HC, D], F32R)
        raw = pair("raw", [P, 2 * HID], F32)
        x1 = pair("sx1", [P, D], F32)
        xt_f = pair("sxt_f", [P, D], F32)
        xt_h, xt_l = pair("xt_h", [P, DC, P], F32R), pair("xt_l", [P, DC, P], F32R)
        sil = sb("ssil", [P, HID], F32)
        h = sb("sh", [P, HC * P], F32)
        ht_h, ht_l = sb("ht_h", [P, HC, P], F32R), sb("ht_l", [P, HC - 1, P], F32R)
        idx = [pair("idx0_", [P, 1], I32), pair("idx1_", [P, 1], I32)]
        yr = [sb("yr0", [P, D], BF16), sb("yr1", [P, D], BF16)]
        o = sb("so", [P, D], F32)
        up_ps = ctx.enter_context(nc.psum_tensor("sup_ps", [P, 4, 512], F32))
        down_ps = ctx.enter_context(nc.psum_tensor("sdown_ps", [P, D], F32))
        t_ps = ctx.enter_context(nc.psum_tensor("st_ps", [P, D], F32))

        d_raw = Loads(sems, nc, "d_raw")
        d_x1 = Loads(sems, nc, "d_sx1")
        d_yr = Loads(sems, nc, "d_yr", n=TOPK, lead=0)
        d_o = Loads(sems, nc, "d_o")
        a_wh, v_wl = count("a_wh"), count("v_wl")
        v_idx = count("v_idx", per=2)
        d_xt = Loads(sems, nc, "d_sxt")
        a_xt, v_xt = count("a_sxt"), count("v_sxt")
        p_up = count("p_sup")
        a_sil = count("a_ssil", per=2)
        v_h = count("v_sh", per=3)
        p_ht = count("p_sht")
        a_ht, v_ht = count("a_sht", per=2), count("v_sht", per=2)
        p_dn = count("p_sdn")
        v_o = count("v_o", per=3)

        chunks = [(sw13[:, c, :], wu_h[:, c, :], wu_l[:, c, :], P, 2 * HID) for c in range(DC)]
        for c in range(HC):
            chunks.append((sw2[c], wd_h[:, c, :], wd_l[:, c, :], P, D))

        with nc.Block() as block:
            @block.sync
            def _(eng):
                for s in (d_raw, d_x1, d_xt):
                    s.prime(eng)
                for n, (src, _, _, k, width) in enumerate(chunks):
                    t = Tile(n // 2, n % 2)
                    a_wh.wait(eng, n - 2)
                    v_wl.wait(eng, n - 2)
                    d_raw.inc(eng.dma_start(raw[t.par][0:k, 0:width], src), t)

                def step(now, on):
                    if "xt" in on:
                        t = now + 3
                        v_xt.wait(eng, t.at - 2)
                        d_xt.inc(eng.dma_start(xt_f[t.par][:], xt_d[t.at]), t)
                    if "x1" in on:
                        t = now + 1
                        v_o.wait(eng, t.at - 2)
                        settled(eng, kept["spare"])
                        d_x1.inc(eng.dma_start(x1[t.par][:], x1_d[bass.ts(t.at, P), :]), t)
                    if "o" in on:
                        t = now - 1
                        v_o.wait(eng, t.at)
                        d_o.inc(eng.dma_start(out[t.at], o[:]), t)

                pipeline(eng, {"xt": (3, 0, NT), "x1": (1, 0, NT), "o": (-1, 0, NT)}, step)
                for t in (NT - 2, NT - 1):
                    d_o.wait(eng, Tile(t // 2, t % 2))

            @block.gpsimd
            def _(eng):
                def step(now, on):
                    t = now
                    v_idx.wait(eng, t.at)
                    v_o.wait(eng, t.at - 1)
                    for k in range(TOPK):
                        settled(eng, kept["spare"])
                        d_yr.inc(eng.indirect_dma_start(
                            yr[k][:], None, y_d, bass.IndirectOffsetOnAxis(ap=idx[k][t.par][:, 0:1], axis=0)), t)

                pipeline(eng, {"y": (0, 0, NT)}, step)

            @block.scalar
            def _(eng):
                for s in (a_wh, a_xt, a_sil, a_ht):
                    s.prime(eng)
                for n, (_, hi, _, k, width) in enumerate(chunks):
                    d_raw.wait(eng, Tile(n // 2, n % 2))
                    a_wh.inc(eng.copy(hi, raw[n % 2][0:k, 0:width]))

                def step(now, on):
                    if "xt" in on:
                        t = now + 1
                        d_xt.wait(eng, t)
                        p_up.wait(eng, t.at - 2)
                        a_xt.inc(eng.copy(xt_h[t.par][:], xt_f[t.par][:]))
                    if "up" in on:
                        t = now
                        p_up.wait(eng, t.at)
                        for i in (0, 1):
                            v_h.wait(eng, t.at - 1, 1 + 2 * i)
                            a_sil.inc(eng.activation(sil[:, i * HALF:(i + 1) * HALF], up_ps[:, i, 0:HALF], ACT.Silu))
                        p_ht.wait(eng, t.at)
                        p_dn.wait(eng, t.at - 1)
                        a_ht.inc(eng.copy(ht_h[:, 0:HC - 1, :], t_ps[:, 0:(HC - 1) * P]))
                        a_ht.inc(eng.copy(ht_h[:, HC - 1, :], t_ps[:, (HC - 1) * P:HC * P]))

                pipeline(eng, {"xt": (1, 0, NT), "up": (0, 0, NT)}, step)

            @block.vector
            def _(eng):
                for s in (v_wl, v_idx, v_xt, v_h, v_ht, v_o, d_o):
                    s.prime(eng)
                for n, (_, hi, lo, k, width) in enumerate(chunks):
                    a_wh.wait(eng, n)
                    v_wl.inc(eng.tensor_tensor(lo, raw[n % 2][0:k, 0:width], hi.bitcast(F32), ALU.subtract))

                def step(now, on):
                    if "idx" in on:
                        t = now
                        if "sent" in on:
                            d_yr.wait(eng, t - 2)
                        for k in range(TOPK):
                            v_idx.inc(eng.tensor_copy(idx[k][t.par][:], slot_all[:, bass.ds(t.at, 1), k]))
                    if "xt" in on:
                        t = now + 1
                        a_xt.wait(eng, t.at)
                        v_xt.inc(eng.tensor_tensor(xt_l[t.par][:].rearrange("p c n -> p (c n)"),
                                                   xt_f[t.par][:],
                                                   xt_h[t.par][:].rearrange("p c n -> p (c n)").bitcast(F32),
                                                   ALU.subtract))
                    if "up" in on:
                        t = now
                        p_ht.wait(eng, t.at - 1)
                        for i in (0, 1):
                            a_sil.wait(eng, t.at, i + 1)
                            v_h.inc(eng.tensor_tensor(h[:, i * HALF:(i + 1) * HALF],
                                                      sil[:, i * HALF:(i + 1) * HALF], up_ps[:, 2 + i, 0:HALF],
                                                      ALU.mult))
                        v_h.inc(eng.tensor_tensor(h[:, HID:HC * P], sil[:, HID - HTAIL:HID],
                                                  up_ps[:, 3, HALF - HTAIL:HALF], ALU.mult))
                        a_ht.wait(eng, t.at)
                        v_ht.inc(eng.tensor_tensor(
                            ht_l[:, 0:HC - 1, :].rearrange("p c n -> p (c n)"), t_ps[:, 0:(HC - 1) * P],
                            ht_h[:, 0:HC - 1, :].rearrange("p c n -> p (c n)").bitcast(F32), ALU.subtract))
                        v_ht.inc(eng.tensor_tensor(ht_h[HTAIL:P, HC - 1, :], t_ps[HTAIL:P, (HC - 1) * P:HC * P],
                                                   ht_h[HTAIL:P, HC - 1, :].bitcast(F32), ALU.subtract))
                    if "o" in on:
                        t = now - 1
                        p_dn.wait(eng, t.at)
                        d_yr.wait(eng, t)
                        d_o.wait(eng, t - 1)
                        v_o.inc(eng.tensor_tensor(o[:], down_ps[:], yr[0][:], ALU.add))
                        v_o.wait(eng, t.at, 1)
                        v_o.inc(eng.tensor_tensor(o[:], o[:], yr[1][:], ALU.add))
                        v_o.wait(eng, t.at, 2)
                        d_x1.wait(eng, t)
                        v_o.inc(eng.tensor_tensor(o[:], o[:], x1[t.par][:], ALU.add))

                pipeline(eng, {"idx": (0, 0, NT), "sent": (-2, 0, NT), "xt": (1, 0, NT),
                               "o": (-1, 0, NT), "up": (0, 0, NT)}, step)

            @block.tensor
            def _(eng):
                for s in (p_up, p_ht, p_dn):
                    s.prime(eng)

                def up(t):
                    for c in range(DC):
                        if isinstance(t.at, int) and t.at == 0:
                            v_wl.wait(eng, c)
                        for x, w in ((xt_h, wu_h), (xt_h, wu_l), (xt_l, wu_h)):
                            for i in range(4):
                                ins = eng.matmul(up_ps[:, i, 0:HALF], x[t.par][:, c, :],
                                                 w[:, c, i * HALF:(i + 1) * HALF],
                                                 start=c == 0 and x is xt_h and w is wu_h,
                                                 stop=c == DC - 1 and x is xt_l)
                    return ins

                def step(now, on):
                    if "up" in on:
                        t = now
                        v_xt.wait(eng, t.at)
                        v_h.wait(eng, t.at - 1)
                        p_up.inc(up(t))
                    if "dn" in on:
                        t = now - 1
                        if isinstance(t.at, int) and t.at == 0:
                            v_wl.wait(eng, DC + HC - 1)
                        v_ht.wait(eng, t.at)
                        v_o.wait(eng, t.at - 1, 1)
                        passes = [(x, w, c, P) for c in range(HC - 1)
                                  for x, w in ((ht_h, wd_h), (ht_h, wd_l), (ht_l, wd_h))]
                        passes += [(ht_h, wd_h, HC - 1, P), (ht_h, wd_l, HC - 1, HTAIL)]
                        for n, (x, w, c, k) in enumerate(passes):
                            for i in (0, 1):
                                ins = eng.matmul(down_ps[:, i * 512:(i + 1) * 512], x[0:k, c, :],
                                                 w[0:k, c, i * 512:(i + 1) * 512],
                                                 start=n == 0, stop=n == len(passes) - 1)
                        p_dn.inc(ins)
                    if "up" in on:
                        t = now
                        v_h.wait(eng, t.at)
                        v_ht.wait(eng, t.at - 1)
                        for c in range(HC):
                            ins = eng.transpose(t_ps[:, c * P:(c + 1) * P], h[:, c * P:(c + 1) * P], ident_f[:])
                        p_ht.inc(ins)

                pipeline(eng, {"up": (0, 0, NT), "dn": (-1, 0, NT)}, step)


def layout(a, chunk=P):
    return np.ascontiguousarray(a.reshape(-1, chunk, a.shape[-1]).transpose(1, 0, 2))


def kernel(x, ctx_1024, L0_xattn_Wq, L0_xattn_bq, L0_xattn_Wk, L0_xattn_bk, L0_ffn_gate_w, L0_ffn_w1, L0_ffn_w2,
           L0_ffn_w3, L0_ffn_sw1, L0_ffn_sw2, L0_ffn_sw3, L0_ffn_expert_bias):
    import concourse.bacc as bacc
    from concourse.bass_utils import run_bass_kernel_spmd

    up = np.concatenate([L0_ffn_w1, L0_ffn_w3], axis=1)
    sup = np.concatenate([L0_ffn_sw1, L0_ffn_sw3], axis=0)
    inputs = {
        "x": np.ascontiguousarray(x.reshape(NT, P, D)),
        "ctxt": np.ascontiguousarray(ctx_1024.reshape(TOK // GROUP, GROUP, CC, P).transpose(0, 3, 2, 1)),
        "wq": layout(L0_xattn_Wq.T), "wk": layout(L0_xattn_Wk.T),
        "bq": L0_xattn_bq.reshape(DH, 1), "bk": L0_xattn_bk.reshape(DH, 1),
        "gate_w": layout(L0_ffn_gate_w.T), "ebias": L0_ffn_expert_bias.reshape(1, E),
        "w13": np.ascontiguousarray(up.reshape(E, 2 * HID, DC, P).transpose(0, 3, 2, 1)),
        "w2": np.ascontiguousarray(L0_ffn_w2.transpose(0, 2, 1)),
        "sw13": np.ascontiguousarray(sup.reshape(2 * HID, DC, P).transpose(2, 1, 0)),
        "sw2": np.concatenate([L0_ffn_sw2.T, L0_ffn_sw2.T[HID - HTAIL:]]).reshape(HC, P, D),
    }
    nc = bacc.Bacc("TRN2", target_bir_lowering=False, num_devices=1, dynamic_dma_scratch_size=DMA_RING)
    args = []
    for name, a in inputs.items():
        args.append(nc.dram_tensor(f"in_{name}", a.shape, mybir.dt.from_np(a.dtype), kind="ExternalInput").ap())
    out = nc.dram_tensor("out", [NT, P, D], F32, kind="ExternalOutput").ap()
    build(nc, *args, out)
    r = run_bass_kernel_spmd(nc, [{f"in_{n}": a for n, a in inputs.items()}], core_ids=[0])
    return r.results[0]["out"].reshape(B, L, D)
```

```python
from contextlib import ExitStack

import numpy as np

import concourse.bass as bass
import concourse.mybir as mybir
from concourse.alu_op_type import AluOpType as ALU

F32 = mybir.dt.float32
F32R = mybir.dt.float32r
BF16 = mybir.dt.bfloat16
I32 = mybir.dt.int32
U32 = mybir.dt.uint32
ACT = mybir.ActivationFunctionType
AX = mybir.AxisListType.X

P = 128
B, L, D = 4, 1024, 1024
TOK = B * L
NT = TOK // P
C, DH = 512, 128
CC = C // P
DC = D // P
BT = L // P
E, HID = 8, 704
HALF = HID // 2
HC = -(-HID // P)
HTAIL = HID - (HC - 1) * P
TOPK = 2
REG = TOK + P
ET = TOPK * TOK // P + E - 1
IDLE = E - 1
GROWS = E * REG + IDLE * P
EPS = 1e-5
DMA_RING = 8192
GROUP = 512


class Count:

    def __init__(self, ctx, nc, name, per=1, first=0, lead=24):
        self.sem = ctx.enter_context(nc.semaphore(name))
        self.per, self.first, self.lead = per, first, lead

    def prime(self, eng):
        eng.sem_inc(self.sem, self.per * self.lead)

    def wait(self, eng, tile, k=None):
        k = self.per if k is None else k
        eng.wait_ge(self.sem, (tile - self.first + self.lead) * self.per + k)

    def inc(self, ins):
        ins.then_inc(self.sem, 1)


class Loads:

    def __init__(self, ctx, nc, name, n=1, first=0, lead=4):
        self.sems = [ctx.enter_context(nc.semaphore(f"{name}{p}")) for p in (0, 1)]
        self.n, self.first, self.lead = n, first // 2, lead

    def prime(self, eng):
        for s in self.sems:
            eng.sem_inc(s, 16 * self.n * self.lead)

    def wait(self, eng, tile):
        eng.wait_ge(self.sems[tile.par], (tile.half - self.first + 1 + self.lead) * 16 * self.n)

    def inc(self, ins, tile):
        ins.then_inc(self.sems[tile.par], 16)


class Tile:

    def __init__(self, half, par):
        self.half, self.par = half, par
        self.at = half * 2 + par

    def __add__(self, n):
        q, par = divmod(self.par + n, 2)
        return Tile(self.half + q, par)

    def __sub__(self, n):
        return self + (-n)


def settled(eng, spare):
    eng.sem_inc(spare, 1)


def pipeline(eng, stages, body, unroll=1):
    lo = min(a - o for o, a, b in stages.values())
    hi = max(b - o for o, a, b in stages.values())
    lo -= lo % 2
    shift = -lo // 2

    def on(s):
        return frozenset(n for n, (o, a, b) in stages.items() if a <= s + o < b)

    pairs = [(on(s), on(s + 1)) for s in range(lo, hi, 2)]
    at = 0
    while at < len(pairs):
        end = at
        while end < len(pairs) and pairs[end] == pairs[at]:
            end += 1

        def both(half):
            for par in (0, 1):
                if pairs[at][par]:
                    body(Tile(half - shift, par), pairs[at][par])

        if end - at < 2 * unroll:
            both(at)
            at += 1
        else:
            turns = (end - at) // unroll
            with eng.Fori(0, turns) as turn:
                for n in range(unroll):
                    both(turn * unroll + (at + n))
            at += turns * unroll


def build(nc, x, ctxt, wq, wk, bq, bk, gate_w, ebias, w13, w2, sw13, sw2, out):
    xt_d = nc.dram_tensor("xt_d", [NT, P, D], F32, kind="Internal").ap()
    x1_d = nc.dram_tensor("x1_d", [TOK, D], F32, kind="Internal").ap()
    rows_d = nc.dram_tensor("rows_d", [GROWS, D], BF16, kind="Internal").ap()
    y_d = nc.dram_tensor("y_d", [ET * P, D], BF16, kind="Internal").ap()
    q_d, k_d = (nc.dram_tensor(n, [NT, P, P], F32, kind="Internal").ap() for n in ("q_d", "k_d"))
    with ExitStack() as ctx:
        def keep(name, shape, dt):
            return ctx.enter_context(nc.sbuf_tensor(name, shape, dt))

        kept = {
            "ident_f": keep("ident_f", [P, P], F32),
            "ident_b": keep("ident_b", [P, P], BF16),
            "ones_b": keep("ones_b", [P, P], BF16),
            "dest_all": keep("dest_all", [P, NT, TOPK], F32),
            "before": keep("before", [P, P], BF16),
            "gw": keep("gw", [P, DC, E], F32),
            "eb": keep("eb", [P, E], F32),
            "index8": keep("index8", [P, E], F32),
            "region": keep("region", [P, E], F32),
            "eps": keep("eps", [P, 1], F32),
            "half_neg": keep("half_neg", [P, 1], F32),
            "ends": keep("ends_i", [1, E], I32),
            "spare": ctx.enter_context(nc.semaphore("spare")),
            "seen": [keep(f"seen{p}", [P, E], BF16) for p in (0, 1)],
        }
        place = -(-nc.sbuf_base // 32) * 32
        att_l = keep("att_l", [P, 2 * BT, L], F32R)
        weights = ExpertWeights(nc, ctx, place, w13, w2)
        with ExitStack() as first:
            keys = [first.enter_context(nc.sbuf_tensor(n, [P, 2 * L], F32R)) for n in ("k_h", "k_l")]
            expd = first.enter_context(nc.sbuf_tensor("expd", [P, L], F32))
            qf = [first.enter_context(nc.sbuf_tensor(f"qf{p}", [P, P], F32)) for p in (0, 1)]
            d_q = Loads(ctx, nc, "d_q")
            project(nc, ctx, kept, keys, qf, d_q, expd, ctxt, (wq, wk), (bq, bk), (q_d, k_d), gate_w, ebias, rows_d)
            attention(nc, ctx, kept, keys, qf, d_q, expd, att_l, weights, x, q_d, k_d, x1_d, xt_d, rows_d)
        kept["slot_all"] = keep("slot_all", [P, NT, TOPK], I32)
        ahead = SharedWeights(nc, ctx, place, sw13, sw2, xt_d)
        routed(nc, ctx, kept, weights, ahead, rows_d, y_d)
        shared(nc, ctx, kept, ahead, x1_d, y_d, out)


class ExpertWeights:

    def __init__(self, nc, ctx, place, w13, w2):
        self.w13, self.w2 = w13, w2
        up, down = DC * 2 * HID, (HC - 1) * D
        assert 2 * (up + down) <= 4 * BT * L
        both = nc.alloc_sbuf_tensor_at("we", [P, 2, up + down], BF16, offset=place)
        self.up = both[:, :, 0:up].rearrange("p e (c n) -> p e c n", n=2 * HID)
        self.down = both[:, :, up:up + down].rearrange("p e (c n) -> p e c n", n=D)
        self.tail = ctx.enter_context(nc.sbuf_tensor("wd_tail", [HTAIL, 2, D], BF16))
        self.d_up, self.d_down = ([ctx.enter_context(nc.semaphore(f"d_we_{n}{p}")) for p in (0, 1)]
                                  for n in ("up", "down"))


    def load_up(self, eng, e):
        for cs in (slice(0, DC // 2), slice(DC // 2, DC)):
            eng.dma_start(self.up[:, e % 2, cs, :], self.w13[e][:, cs, :]).then_inc(self.d_up[e % 2], 16)

    def load_down(self, eng, e):
        done = self.d_down[e % 2]
        eng.dma_start(self.down[:, e % 2],
                      self.w2[e][0:(HC - 1) * P, :].rearrange("(c p) n -> p c n", p=P)).then_inc(done, 16)
        eng.dma_start(self.tail[:, e % 2, :], self.w2[e][(HC - 1) * P:HID, :]).then_inc(done, 16)

    def wait(self, eng, part, e):
        eng.wait_ge(part[e % 2], (e // 2 + 1) * 16 * 2)


class SharedWeights:

    def __init__(self, nc, ctx, place, sw13, sw2, xt_d):
        def sb(name, shape, dt):
            return ctx.enter_context(nc.sbuf_tensor(name, shape, dt))

        self.up_h, self.up_l = sb("wu_h", [P, DC, 2 * HID], F32R), sb("wu_l", [P, DC, 2 * HID], F32R)
        offset = place

        def at_place(name, shape):
            nonlocal offset
            t = nc.alloc_sbuf_tensor_at(name, shape, F32R, offset=offset)
            offset += int(np.prod(shape[1:])) * 4
            assert offset <= place + 4 * 2 * BT * L
            return t

        self.down_h, self.down_l = at_place("wd_h", [P, HC, D]), at_place("wd_l", [P, HC, D])
        self.xt_h, self.xt_l = ([at_place(f"xt_{n}{p}", [P, DC, P]) for p in (0, 1)] for n in "hl")
        self.raw = [sb(f"sraw{p}", [P, 2 * HID], F32) for p in (0, 1)]
        self.xt = [sb(f"sxt_f{p}", [P, D], F32) for p in (0, 1)]
        self.sw13, self.sw2, self.xt_d = sw13, sw2, xt_d
        self.d_raw, self.d_xt = Loads(ctx, nc, "d_raw"), Loads(ctx, nc, "d_sxt")
        self.a_hi, self.v_lo = Count(ctx, nc, "a_wh"), Count(ctx, nc, "v_wl")

    def parts(self, n):
        if not isinstance(n.at, int) or n.at < DC:
            return self.sw13[:, n.at, :], self.up_h[:, n.at, :], self.up_l[:, n.at, :], 2 * HID
        c = n.at - DC
        return self.sw2[c], self.down_h[:, c, :], self.down_l[:, c, :], D

    def load(self, eng, n):
        src, _, _, width = self.parts(n)
        self.a_hi.wait(eng, n.at - 2)
        self.v_lo.wait(eng, n.at - 2)
        self.d_raw.inc(eng.dma_start(self.raw[n.par][:, 0:width], src), n)

    def high(self, eng, n):
        _, hi, _, width = self.parts(n)
        self.d_raw.wait(eng, n)
        self.a_hi.inc(eng.copy(hi, self.raw[n.par][:, 0:width]))

    def low(self, eng, n):
        _, hi, lo, width = self.parts(n)
        self.a_hi.wait(eng, n.at)
        self.v_lo.inc(eng.tensor_tensor(lo, self.raw[n.par][:, 0:width], hi.bitcast(F32), ALU.subtract))

    def load_rows(self, eng, t):
        self.d_xt.inc(eng.dma_start(self.xt[t.par][:], self.xt_d[t.at]), t)


def project(nc, sems, kept, keys, qf, d_q, expd, ctxt, weights, biases, outs, gate_w, ebias, rows_d):
    with ExitStack() as ctx:
        def sb(name, shape, dt):
            return ctx.enter_context(nc.sbuf_tensor(name, shape, dt))

        def pair(name, shape, dt):
            return [sb(f"{name}{p}", shape, dt) for p in (0, 1)]

        NG = TOK // GROUP
        raw = sb("raw", [P, 2, CC, DH], F32)
        w_h, w_l = sb("w_h", [P, 2, CC, DH], F32R), sb("w_l", [P, 2, CC, DH], F32R)
        bias = sb("bias", [P, 2], F32)
        cf = pair("cf", [P, CC, GROUP], F32)
        ch, cl = pair("ch", [P, CC, GROUP], F32R), pair("cl", [P, CC, GROUP], F32R)
        res = pair("res", [P, 2, GROUP], F32)
        acc = [ctx.enter_context(nc.psum_tensor(f"acc{p}", [P, 2, GROUP], F32)) for p in (0, 1)]

        zeros = sb("idle_zeros", [P, D], BF16)

        d_const = sems.enter_context(nc.semaphore("d_const"))
        d_idle = sems.enter_context(nc.semaphore("d_idle"))
        c_const = sems.enter_context(nc.semaphore("c_const"))
        d_first = sems.enter_context(nc.semaphore("d_first"))
        c_first = sems.enter_context(nc.semaphore("c_first"))
        d_w = sems.enter_context(nc.semaphore("d_w"))
        c_w = sems.enter_context(nc.semaphore("c_w"))
        d_c = Loads(sems, nc, "d_c")
        d_res = Loads(sems, nc, "d_res", n=2)
        a_hi = Count(sems, nc, "a_hi")
        v_lo = Count(sems, nc, "v_lo")
        p_acc = Count(sems, nc, "p_acc")
        a_res = Count(sems, nc, "a_res")

        with nc.Block() as block:
            @block.gpsimd
            def _(eng):
                def const(ins):
                    ins.then_inc(c_const, 1)

                ident_f, ones_b = kept["ident_f"], kept["ones_b"]
                const(eng.memset(zeros[:], 0.0))
                const(eng.memset(ident_f[:], 0.0))
                const(eng.memset(ones_b[:], 1.0))
                eng.wait_ge(c_const, 3)
                const(eng.affine_select(out=ident_f[:], in_=ident_f[:], compare_op=ALU.not_equal, fill=1.0, base=0,
                                        pattern=[[-1, P]], channel_multiplier=1))
                const(eng.affine_select(out=kept["before"][:], in_=ones_b[:], compare_op=ALU.is_gt, fill=0.0,
                                        base=0, pattern=[[1, P]], channel_multiplier=-1))
                eng.wait_ge(c_const, 4)
                const(eng.tensor_copy(kept["ident_b"][:], ident_f[:]))
                const(eng.iota(kept["index8"][:], pattern=[[1, E]], base=0, channel_multiplier=0,
                               allow_small_or_imprecise_dtypes=True))
                const(eng.iota(kept["region"][:], pattern=[[REG, E]], base=0, channel_multiplier=0,
                               allow_small_or_imprecise_dtypes=True))
                const(eng.memset(kept["half_neg"][:], -0.5))
                const(eng.memset(kept["eps"][:], EPS))
                for p in (0, 1):
                    const(eng.memset(kept["seen"][p][:], 0.0))

            @block.sync
            def _(eng):
                d_c.prime(eng)
                d_q.prime(eng)
                for i in (0, 1):
                    eng.dma_start(raw[:, i], weights[i]).then_inc(d_w, 16)
                    eng.dma_start(bias[:, i:i + 1], biases[i]).then_inc(d_w, 16)

                def step(now, on):
                    if "load" in on:
                        t = now + 3
                        a_hi.wait(eng, t.at - 2)
                        v_lo.wait(eng, t.at - 2)
                        d_c.inc(eng.dma_start(cf[t.par][:], ctxt[t.at]), t)
                    if "idle" in on:
                        eng.dma_start(kept["gw"][:], gate_w).then_inc(d_const, 16)
                        eng.dma_start(kept["eb"][:], ebias.broadcast_to([P, E])).then_inc(d_const, 16)
                        eng.wait_ge(c_const, 1)
                        for i in range(IDLE):
                            r = E * REG + i * P
                            eng.dma_start(rows_d[r:r + P, :], zeros[:]).then_inc(d_idle, 16)

                    if "first" in on:
                        for t in (0, 1):
                            d_res.wait(eng, Tile(0, t))
                        eng.dma_start(expd[:].rearrange("p (t n) -> p t n", n=P),
                                      outs[1][0:BT].rearrange("t p n -> p t n")).then_inc(d_first, 16)
                        for t in (0, 1):
                            d_q.inc(eng.dma_start(qf[t][:], outs[0][t]), Tile(0, t))
                    if "out" in on:
                        a_res.wait(eng, now.at)
                        for i in (0, 1):
                            d_res.inc(eng.dma_start(
                                outs[i][bass.ts(now.at, GROUP // P)].rearrange("t p n -> p t n"),
                                res[now.par][:, i].rearrange("p (t n) -> p t n", n=P)), now)

                pipeline(eng, {"load": (3, 0, NG), "idle": (0, 0, 1), "first": (0, 2, 3), "out": (0, 0, NG)}, step)
                eng.wait_ge(d_const, 16 * 2)
                eng.wait_ge(d_idle, 16 * IDLE)
                for t in (NG - 2, NG - 1):
                    d_res.wait(eng, Tile(t // 2, t % 2))

            @block.scalar
            def _(eng):
                a_hi.prime(eng)
                a_res.prime(eng)
                d_res.prime(eng)
                eng.wait_ge(d_w, 16 * 4)
                eng.copy(w_h[:], raw[:]).then_inc(c_w, 1)

                def step(now, on):
                    if "hi" in on:
                        t = now + 2
                        d_c.wait(eng, t)
                        p_acc.wait(eng, t.at - 2)
                        a_hi.inc(eng.copy(ch[t.par][:], cf[t.par][:]))
                    if "res" in on:
                        p_acc.wait(eng, now.at)
                        d_res.wait(eng, now - 2)
                        eng.activation(res[now.par][:, 0], acc[now.par][:, 0], ACT.Identity, bias=bias[:, 0:1])
                        a_res.inc(eng.activation(res[now.par][:, 1], acc[now.par][:, 1], ACT.Identity,
                                                 bias=bias[:, 1:2]))
                    if "first" in on:
                        eng.wait_ge(d_first, 16)
                        eng.copy(keys[0][:, 0:L], expd[:]).then_inc(c_first, 1)

                pipeline(eng, {"hi": (2, 0, NG), "res": (0, 0, NG), "first": (0, 4, 5)}, step)

            @block.vector
            def _(eng):
                v_lo.prime(eng)
                eng.wait_ge(c_w, 1)
                eng.tensor_tensor(w_l[:], raw[:], w_h[:].bitcast(F32), ALU.subtract).then_inc(c_w, 1)

                def step(now, on):
                    if "first" in on:
                        eng.wait_ge(c_first, 1)
                        eng.tensor_tensor(keys[1][:, 0:L], expd[:], keys[0][:, 0:L].bitcast(F32),
                                          ALU.subtract).then_inc(c_first, 1)
                    a_hi.wait(eng, now.at)
                    v_lo.inc(eng.tensor_tensor(cl[now.par][:], cf[now.par][:], ch[now.par][:].bitcast(F32),
                                               ALU.subtract))

                pipeline(eng, {"lo": (0, 0, NG), "first": (0, 6, 7)}, step)

            @block.tensor
            def _(eng):
                p_acc.prime(eng)
                eng.wait_ge(c_w, 2)

                def products(now, pairs, first):
                    for i in (0, 1):
                        for c in range(CC):
                            for n, (w, v) in enumerate(pairs):
                                ins = eng.matmul(acc[now.par][:, i], w[:, i, c, :], v[now.par][:, c, :],
                                                 start=first and c == 0 and n == 0,
                                                 stop=not first and c == CC - 1)
                    return ins

                def step(now, on):
                    a_hi.wait(eng, now.at)
                    a_res.wait(eng, now.at - 2)
                    products(now, ((w_h, ch), (w_l, ch)), True)
                    v_lo.wait(eng, now.at)
                    ins = products(now, ((w_h, cl),), False)
                    p_acc.inc(ins)

                pipeline(eng, {"mm": (0, 0, NG)}, step)


def attention(nc, sems, kept, keys, qf, d_q, expd, att_l, weights, x, q_d, k_d, x1_d, xt_d, rows_d):
    with ExitStack() as ctx:
        def sb(name, shape, dt):
            return ctx.enter_context(nc.sbuf_tensor(name, shape, dt))

        def ps(name, shape, dt):
            return ctx.enter_context(nc.psum_tensor(name, shape, dt))

        def count(name, **kw):
            return Count(sems, nc, name, **kw)

        def pair(name, shape, dt):
            return [sb(f"{name}{p}", shape, dt) for p in (0, 1)]

        ident_f, ident_b, ones_b = kept["ident_f"], kept["ident_b"], kept["ones_b"]
        dest_all, seen = kept["dest_all"], kept["seen"]
        before, gw, eb, index8, region, eps, half_neg = (
            kept[n] for n in ("before", "gw", "eb", "index8", "region", "eps", "half_neg"))

        kf = pair("kf", [P, P], F32)
        q_h, q_l = pair("q_h", [P, P], F32R), pair("q_l", [P, P], F32R)
        k_h, k_l = keys
        att_h = sb("att_h", [P, 2 * BT, L], F32R)
        att = sb("att", [P, L], F32)
        nmax, rsum, rinv = (pair(n, [P, 1], F32) for n in ("nmax", "rsum", "rinv"))

        xs = pair("xs", [P, D], F32)
        xr = sb("xr", [P, D], F32)
        xn = sb("xn", [P, D], F32)
        xnt_h, xnt_l = pair("xnt_h", [P, DC, P], F32R), pair("xnt_l", [P, DC, P], F32R)
        x1 = sb("x1", [P, D], F32)
        x2 = pair("x2", [P, D], F32)
        x2t = sb("x2t", [P, DC, P], F32)
        bs = [pair("bs0", [P, 2, 6], F32), pair("bs1", [P, 2, 6], F32)]
        mv = [pair("mv0", [P, 2], F32), pair("mv1", [P, 2], F32)]
        ve = [pair("ve0", [P, 1], F32), pair("ve1", [P, 1], F32)]
        rstd = [pair("rstd0", [P, 1], F32), pair("rstd1", [P, 1], F32)]

        logit = pair("logit", [P, E], F32)
        rank = pair("rank", [P, E], F32)
        sig_e = pair("sig_e", [P, E], F32)
        score = pair("score", [P, E], F32)
        sel = pair("sel", [P, E], F32)
        top = pair("top", [P, E], F32)
        top_i = pair("top_i", [P, E], U32)
        top_e = pair("top_e", [P, TOPK], F32)
        one_hot = [pair("hot0_", [P, E], F32), pair("hot1_", [P, E], F32)]
        mask = pair("mask", [P, E], BF16)
        junk = pair("junk", [P, E], F32)
        wsc = pair("wsc", [P, TOPK], F32)
        destf = pair("destf", [P, TOPK], F32)
        dest = [pair("dest0_", [P, 1], I32), pair("dest1_", [P, 1], I32)]
        disp = [sb("disp0", [P, D], BF16), sb("disp1", [P, D], BF16)]

        o_ps = [ps(f"o_ps{p}", [P, L], F32) for p in (0, 1)]
        e_ps = ps("e_ps", [P, L], F32)
        t_ps = ps("t_ps", [P, L], F32)
        gate_ps, rank_ps = t_ps[:, 0:E], t_ps[:, E:2 * E]

        d_x, d_xr = Loads(sems, nc, "d_x"), Loads(sems, nc, "d_xr")
        d_k = Loads(sems, nc, "d_k", first=BT)
        d_x1, d_x2t = Loads(sems, nc, "d_x1"), Loads(sems, nc, "d_x2t")
        d_disp = Loads(sems, nc, "d_disp", n=TOPK, lead=0)
        spare = kept["spare"]
        v_xstat = count("v_xstat", per=3)
        g_rstd = [count("g_rstd0", per=2), count("g_rstd1", per=2)]
        v_xn = count("v_xn")
        p_xt = count("p_xt")
        a_xth = count("a_xth")
        v_xtl = count("v_xtl")
        p_mm = count("p_mm")
        v_x1 = count("v_x1", per=4)
        v_x2 = count("v_x2")
        p_x2t = count("p_x2t")
        a_x2t = count("a_x2t")
        p_gate = count("p_gate")
        v_gcopy = count("v_gcopy")
        a_sig = count("a_sig")
        v_route = count("v_route", per=11)
        p_rank = count("p_rank")
        v_rcopy = count("v_rcopy")
        v_dest = count("v_dest", per=6)
        a_disp = count("a_disp")
        a_qh, a_kh = count("a_qh"), count("a_kh", first=BT)
        g_ql, g_kl = count("g_ql"), count("g_kl", first=BT)
        p_en = count("p_en")
        v_max = count("v_max")
        a_exp = count("a_exp")
        v_inv = count("v_inv")
        a_att = count("a_att")
        p_att = count("p_att")
        a_atth = count("a_atth")
        v_attl = count("v_attl")

        K_LEAD = 2 * BT + 2
        E_LEAD = BT + 2

        def energies(t, sums):
            return e_ps if sums or t.par == 0 else o_ps[1]

        def columns(half, t):
            return half[:, bass.ds(t.at & BT, BT), bass.ds((t.at & (BT - 1)) * P, P)]

        with nc.Block() as block:
            @block.sync
            def _(eng):
                for s in (d_x, d_xr, d_k):
                    s.prime(eng)

                def step(now, on):
                    if "st" in on:
                        t = now - 1
                        v_x1.wait(eng, t.at, 1)
                        d_x1.inc(eng.dma_start(x1_d[bass.ts(t.at, P), :], x1[:]), t)
                    if "st2" in on:
                        t = now - 2
                        a_x2t.wait(eng, t.at)
                        d_x2t.inc(eng.dma_start(xt_d[t.at], x2t[:].rearrange("p c n -> p (c n)")), t)
                    if "xr" in on:
                        t = now
                        v_x1.wait(eng, t.at - 1, 1)
                        d_xr.inc(eng.dma_start(xr[:], x[t.at]), t)
                    if "x" in on:
                        t = now + 3
                        v_xn.wait(eng, t.at - 2)
                        d_x.inc(eng.dma_start(xs[t.par][:], x[t.at]), t)
                    for name, off, dst, src, sem, hi, lo in (("k", K_LEAD + 1, kf, k_d, d_k, a_kh, g_kl),
                                                             ("q", E_LEAD + 2, qf, q_d, d_q, a_qh, g_ql)):
                        if name in on:
                            t = now + off
                            hi.wait(eng, t.at - 2)
                            lo.wait(eng, t.at - 2)
                            sem.inc(eng.dma_start(dst[t.par][:], src[t.at]), t)

                pipeline(eng, {"k": (K_LEAD + 1, BT, NT), "q": (E_LEAD + 2, 2, NT), "x": (3, 0, NT),
                               "xr": (0, 0, NT), "st": (-1, 0, NT), "st2": (-2, 0, NT)}, step)
                for t in (NT - 2, NT - 1):
                    d_x1.wait(eng, Tile(t // 2, t % 2))
                    d_x2t.wait(eng, Tile(t // 2, t % 2))

            @block.gpsimd
            def _(eng):
                for s in (*g_rstd, g_ql, g_kl):
                    s.prime(eng)
                def deviation(t, i):
                    (v_x1 if i else v_xstat).wait(eng, t.at)
                    (v_x2 if i else v_xn).wait(eng, t.at - 2)
                    g_rstd[i].inc(eng.tensor_tensor(ve[i][t.par][:], mv[i][t.par][:, 1:2], eps[:], ALU.add))
                    g_rstd[i].wait(eng, t.at, 1)
                    g_rstd[i].inc(eng.tensor_tensor(rstd[i][t.par][:], ve[i][t.par][:], half_neg[:],
                                                    ALU.pow))

                def step(now, on):
                    if "r1" in on:
                        deviation(now - 1, 1)
                    if "disp" in on:
                        t = now - 3
                        a_disp.wait(eng, t.at)
                        v_dest.wait(eng, t.at)
                        for k in range(TOPK):
                            settled(eng, spare)
                            d_disp.inc(eng.indirect_dma_start(
                                rows_d, bass.IndirectOffsetOnAxis(ap=dest[k][t.par][:, 0:1], axis=0),
                                disp[k][:], None), t)
                    if "r0" in on:
                        deviation(now + 2, 0)
                    if "weights" in on:
                        p_mm.wait(eng, now.at - 2)
                        weights.load_up(eng, 0)
                        weights.load_down(eng, 0)
                    if "k" in on:
                        t = now + K_LEAD
                        at = bass.ts(t.at & (2 * BT - 1), P)
                        a_kh.wait(eng, t.at)
                        g_kl.inc(eng.tensor_tensor(k_l[:, at], kf[t.par][:], k_h[:, at].bitcast(F32), ALU.subtract))
                    if "q" in on:
                        t = now + E_LEAD + 1
                        a_qh.wait(eng, t.at)
                        g_ql.inc(eng.tensor_tensor(q_l[t.par][:], qf[t.par][:], q_h[t.par][:].bitcast(F32),
                                                   ALU.subtract))

                pipeline(eng, {"k": (K_LEAD, BT, NT), "q": (E_LEAD + 1, 0, NT), "r1": (-1, 0, NT),
                               "r0": (2, 0, NT), "weights": (0, NT - BT + 1, NT - BT + 2), "disp": (-3, 0, NT)}, step)
                for t in (NT - 2, NT - 1):
                    d_disp.wait(eng, Tile(t // 2, t % 2))

            @block.scalar
            def _(eng):
                for s in (a_xth, a_x2t, a_sig, a_disp, a_qh, a_kh, a_exp, a_att, a_atth):
                    s.prime(eng)

                def step(now, on):
                    if "sig" in on:
                        t = now - 2
                        v_gcopy.wait(eng, t.at)
                        v_route.wait(eng, t.at - 2)
                        a_sig.inc(eng.activation(sig_e[t.par][:], logit[t.par][:], ACT.Exp, scale=-1.0))
                    if "xt" in on:
                        t = now + 1
                        p_xt.wait(eng, t.at)
                        p_mm.wait(eng, t.at - 2)
                        a_xth.inc(eng.copy(xnt_h[t.par][:], t_ps[:]))
                    if "disp" in on:
                        t = now - 3
                        v_route.wait(eng, t.at)
                        if "sent" in on:
                            d_disp.wait(eng, t - 1)
                        for k in range(TOPK):
                            ins = eng.activation(disp[k][:], x2[t.par][:], ACT.Copy,
                                                 scale=wsc[t.par][:, k:k + 1])
                        a_disp.inc(ins)
                    if "sm" in on:
                        t = now + E_LEAD - 1
                        v_max.wait(eng, t.at)
                        v_inv.wait(eng, t.at - 2)
                        a_att.wait(eng, t.at - 1)
                        a_exp.inc(eng.activation(expd[:], energies(t, "mm_last" in on)[:], ACT.Exp, bias=nmax[t.par][:],
                                                 accum_out=rsum[t.par][:]))
                    if "ta" in on:
                        t = now + E_LEAD - 2
                        p_att.wait(eng, t.at)
                        p_mm.wait(eng, t.at - BT - 1)
                        a_atth.inc(eng.copy(columns(att_h, t), t_ps[:].rearrange("p (c n) -> p c n", n=P)))
                    if "x2t" in on:
                        t = now - 1
                        p_x2t.wait(eng, t.at)
                        p_gate.wait(eng, t.at - 1)
                        d_x2t.wait(eng, t - 1)
                        a_x2t.inc(eng.copy(x2t[:], t_ps[:]))
                    if "sm" in on:
                        t = now + E_LEAD - 1
                        v_inv.wait(eng, t.at)
                        p_att.wait(eng, t.at - 1)
                        a_att.inc(eng.activation(att[:], expd[:], ACT.Copy, scale=rinv[t.par][:]))
                    if "k" in on:
                        t = now + K_LEAD
                        d_k.wait(eng, t)
                        p_en.wait(eng, t.at - BT - 1)
                        a_kh.inc(eng.copy(k_h[:, bass.ts(t.at & (2 * BT - 1), P)], kf[t.par][:]))
                    if "q" in on:
                        t = now + E_LEAD + 1
                        d_q.wait(eng, t)
                        p_en.wait(eng, t.at - 2)
                        a_qh.inc(eng.copy(q_h[t.par][:], qf[t.par][:]))

                pipeline(eng, {"k": (K_LEAD, BT, NT), "q": (E_LEAD + 1, 0, NT), "xt": (1, 0, NT),
                               "ta": (E_LEAD - 2, 0, NT), "sm": (E_LEAD - 1, 0, NT), "mm_last": (-1, 0, NT),
                               "sig": (-2, 0, NT), "x2t": (-1, 0, NT), "disp": (-3, 0, NT), "sent": (-4, 0, NT)}, step)

            @block.vector
            def _(eng):
                for s in (v_xstat, v_xn, v_xtl, v_x1, v_x2, v_gcopy, v_route, v_rcopy, v_dest,
                          v_max, v_inv, v_attl, d_x1, d_x2t):
                    s.prime(eng)

                def stats(src, i, t, counts, k0):
                    for h in (0, 1):
                        counts.inc(eng.bn_stats(bs[i][t.par][:, h, :], src[:, h * 512:(h + 1) * 512]))
                    counts.wait(eng, t.at, k0 + 2)
                    settled(eng, spare)
                    counts.inc(eng.bn_aggr(mv[i][t.par][:], bs[i][t.par][:].rearrange("p a b -> p (a b)")))

                def normalize(dst, src, i, t, counts):
                    counts.inc(eng.tensor_scalar(dst, src, mv[i][t.par][:, 0:1], rstd[i][t.par][:, 0:1],
                                                 ALU.subtract, ALU.mult))

                def step(now, on):
                    if "x1" in on:
                        t = now - 1
                        p_mm.wait(eng, t.at)
                        d_x1.wait(eng, t - 1)
                        g_rstd[1].wait(eng, t.at - 2, 1)
                        d_xr.wait(eng, t)
                        v_x1.inc(eng.tensor_tensor(x1[:], o_ps[t.par][:], xr[:], ALU.add))
                    if "gcopy" in on:
                        t = now - 2
                        p_gate.wait(eng, t.at)
                        if "rcopy" in on:
                            p_rank.wait(eng, t.at - 1)
                        a_sig.wait(eng, t.at - 2)
                        v_gcopy.inc(eng.tensor_copy(logit[t.par][:], gate_ps))
                    if "rcopy" in on:
                        t = now - 3
                        p_rank.wait(eng, t.at)
                        v_rcopy.inc(eng.tensor_copy(rank[t.par][:], rank_ps))
                    if "x1" in on:
                        t = now - 1
                        v_x1.wait(eng, t.at, 1)
                        stats(x1, 1, t, v_x1, 1)
                    if "xt" in on:
                        t = now + 1
                        a_xth.wait(eng, t.at)
                        v_xtl.inc(eng.tensor_tensor(xnt_l[t.par][:].rearrange("p c n -> p (c n)"), t_ps[:],
                                                    xnt_h[t.par][:].rearrange("p c n -> p (c n)").bitcast(F32),
                                                    ALU.subtract))
                    if "sm" in on:
                        t = now + E_LEAD - 1
                        p_en.wait(eng, t.at)
                        a_exp.wait(eng, t.at - 2)
                        v_max.inc(eng.tensor_reduce(nmax[t.par][:], energies(t, "mm_last" in on)[:], AX, ALU.max, negate=True))
                    if "x1" in on:
                        t = now - 1
                        g_rstd[1].wait(eng, t.at)
                        p_x2t.wait(eng, t.at - 2)
                        a_disp.wait(eng, t.at - 2)
                        normalize(x2[t.par][:], x1[:], 1, t, v_x2)
                    if "dest" in on:
                        t = now - 3
                        p, n = t.par, 0

                        def dlink(ins):
                            nonlocal n
                            n += 1
                            v_dest.inc(ins)
                            v_dest.wait(eng, t.at, n)

                        v_rcopy.wait(eng, t.at)
                        if "sent" in on:
                            d_disp.wait(eng, t - 2)
                        dlink(eng.tensor_tensor(seen[1 - p][:], seen[p][:], mask[p][:], ALU.add))
                        dlink(eng.tensor_tensor(rank[p][:], rank[p][:], region[:], ALU.add))
                        for k in range(TOPK):
                            dlink(eng.tensor_tensor_reduce(junk[p][:, 0:E], one_hot[k][p][:], rank[p][:], 1.0,
                                                           0.0, ALU.mult, ALU.add, destf[p][:, k:k + 1]))
                        dlink(eng.tensor_copy(dest_all[:, t.at, :], destf[p][:]))
                        eng.tensor_copy(dest[0][p][:], destf[p][:, 0:1])
                        dlink(eng.tensor_copy(dest[1][p][:], destf[p][:, 1:2]))
                    if "sm" in on:
                        t = now + E_LEAD - 1
                        a_exp.wait(eng, t.at)
                        a_att.wait(eng, t.at - 2)
                        v_inv.inc(eng.reciprocal(rinv[t.par][:], rsum[t.par][:]))
                    if "ta" in on:
                        t = now + E_LEAD - 2
                        a_atth.wait(eng, t.at)
                        v_attl.inc(eng.tensor_tensor(columns(att_l, t), t_ps[:].rearrange("p (c n) -> p c n", n=P),
                                                     columns(att_h, t).bitcast(F32), ALU.subtract))
                    if "xs" in on:
                        t = now + 2
                        d_x.wait(eng, t)
                        g_rstd[0].wait(eng, t.at - 2, 1)
                        stats(xs[t.par], 0, t, v_xstat, 0)
                    if "route" in on:
                        t = now - 2
                        p, n = t.par, 0

                        def link(ins=None):
                            nonlocal n
                            if ins:
                                n += 1
                                v_route.inc(ins)
                            v_route.wait(eng, t.at, n)

                        a_sig.wait(eng, t.at)
                        a_disp.wait(eng, t.at - 2)
                        link(eng.tensor_scalar(score[p][:], sig_e[p][:], 1.0, None, ALU.add))
                        link(eng.reciprocal(score[p][:], score[p][:]))
                        link(eng.tensor_tensor(sel[p][:], score[p][:], eb[:], ALU.add))
                        settled(eng, spare)
                        link(eng.max(top[p][:], sel[p][:]))
                        settled(eng, spare)
                        link(eng.max_index(top_i[p][:], top[p][:], sel[p][:]))
                        link(eng.tensor_copy(top_e[p][:], top_i[p][:, 0:TOPK]))
                        for k in range(TOPK):
                            link(eng.tensor_scalar(one_hot[k][p][:], index8[:], top_e[p][:, k:k + 1], None,
                                                   ALU.is_equal))
                        p_rank.wait(eng, t.at - 2)
                        link(eng.tensor_tensor(mask[p][:], one_hot[0][p][:], one_hot[1][p][:], ALU.add))
                        for k in range(TOPK):
                            link(eng.tensor_tensor_reduce(junk[p][:, 0:E], one_hot[k][p][:], score[p][:], 1.0,
                                                          0.0, ALU.mult, ALU.add, wsc[p][:, k:k + 1]))
                    if "xn" in on:
                        t = now + 2
                        g_rstd[0].wait(eng, t.at)
                        p_xt.wait(eng, t.at - 1)
                        normalize(xn[:], xs[t.par][:], 0, t, v_xn)

                pipeline(eng, {"x1": (-1, 0, NT), "gcopy": (-2, 0, NT), "rcopy": (-3, 0, NT),
                               "xt": (1, 0, NT), "ta": (E_LEAD - 2, 0, NT),
                               "sm": (E_LEAD - 1, 0, NT), "mm_last": (-1, 0, NT), "xs": (2, 0, NT), "route": (-2, 0, NT),
                               "dest": (-3, 0, NT), "sent": (-5, 0, NT), "xn": (2, 0, NT)}, step)

            @block.tensor
            def _(eng):
                for s in (p_xt, p_mm, p_x2t, p_gate, p_rank, p_en, p_att):
                    s.prime(eng)

                def transposes(src):
                    for c in range(DC):
                        ins = eng.transpose(t_ps[:, c * P:(c + 1) * P], src[:, c * P:(c + 1) * P], ident_f[:])
                    return ins

                def sums(t, chunks):
                    parity = t.at & BT
                    for c in chunks:
                        for xt, at in ((xnt_h, att_h), (xnt_h, att_l), (xnt_l, att_h)):
                            for h in (0, 1):
                                ins = eng.matmul(o_ps[t.par][:, h * 512:(h + 1) * 512], xt[t.par][:, c, :],
                                                 at[:, parity + c, h * 512:(h + 1) * 512],
                                                 start=(c == 0 and xt is xnt_h and at is att_h),
                                                 stop=(c == DC - 1 and xt is xnt_l))
                    return ins

                def copied(now, on):
                    if "ta_last" in on:
                        v_attl.wait(eng, now.at + E_LEAD - 3)
                    if "x2t_last" in on:
                        v_gcopy.wait(eng, now.at - 2)
                    if "rank_last" in on:
                        v_rcopy.wait(eng, now.at - 3)

                def step(now, on):
                    if "xt" in on:
                        t = now + 1
                        v_xn.wait(eng, t.at)
                        copied(now, on)
                        p_xt.inc(transposes(xn))
                    if "mm" in on:
                        t = now
                        v_xtl.wait(eng, t.at)
                        v_attl.wait(eng, t.at | (BT - 1))
                        v_x1.wait(eng, t.at - 2, 1)
                        sums(t, range(0, 3))
                    if "ta" in on:
                        t = now + E_LEAD - 2
                        a_att.wait(eng, t.at)
                        if "xt" in on:
                            v_xtl.wait(eng, now.at + 1)
                        else:
                            copied(now, on)
                        p_att.inc(transposes(att))
                    if "mm" in on:
                        sums(now, range(3, 6))
                    if "x2t" in on:
                        t = now - 1
                        v_x2.wait(eng, t.at)
                        if "ta" in on:
                            v_attl.wait(eng, now.at + E_LEAD - 2)
                        elif "xt" in on:
                            v_xtl.wait(eng, now.at + 1)
                        else:
                            copied(now, on)
                        p_x2t.inc(transposes(x2[t.par]))
                    if "mm" in on:
                        p_mm.inc(sums(now, range(6, DC)))
                    if "x2t" in on:
                        t = now - 1
                        a_x2t.wait(eng, t.at)
                        for c in range(DC):
                            ins = eng.matmul(gate_ps, x2t[:, c, :], gw[:, c, :], start=(c == 0),
                                             stop=(c == DC - 1))
                        p_gate.inc(ins)
                    if "rank" in on:
                        t = now - 2
                        v_route.wait(eng, t.at)
                        v_dest.wait(eng, t.at - 1, 1)
                        if "x2t" in on:
                            a_x2t.wait(eng, t.at + 1)
                        else:
                            copied(now, on)
                        eng.matmul(rank_ps, before[:], mask[t.par][:], start=True, stop=False)
                        p_rank.inc(eng.matmul(rank_ps, ones_b[:], seen[t.par][:], start=False, stop=True))
                    if "en" in on:
                        t = now + E_LEAD
                        g_ql.wait(eng, t.at)
                        g_kl.wait(eng, t.at | (BT - 1))
                        a_exp.wait(eng, t.at - 1 if "mm" in on else t.at - 2)
                        to = energies(t, "mm" in on)
                        base = (t.at & BT) * P
                        for q, k in ((q_h, k_h), (q_h, k_l), (q_l, k_h)):
                            for h in (0, 1):
                                ins = eng.matmul(to[:, h * 512:(h + 1) * 512], q[t.par][:],
                                                 k[:, bass.ds(base + h * 512, 512)],
                                                 start=(q is q_h and k is k_h), stop=(q is q_l))
                        p_en.inc(ins)

                pipeline(eng, {"xt": (1, 0, NT), "mm": (0, 0, NT), "ta": (E_LEAD - 2, 0, NT),
                               "ta_last": (E_LEAD - 3, 0, NT), "x2t": (-1, 0, NT), "x2t_last": (-2, 0, NT),
                               "rank": (-2, 0, NT), "rank_last": (-3, 0, NT),
                               "en": (E_LEAD, 0, NT)}, step)


def plan(nc, sems, ctx, kept, cnt, table, rows_d):
    def sb(name, shape, dt):
        return ctx.enter_context(nc.sbuf_tensor(name, shape, dt))

    zeros = sb("zeros", [P, D], BF16)
    cnt_i = sb("cnt_i", [P, E], I32)
    rows_i = sb("rows_i", [P, 2, E], I32)
    tiles = sb("tiles", [P, E], F32)
    ends = sb("ends", [P, E], F32)
    base = sb("base", [P, E], F32)
    moved = sb("moved", [P, E], F32)
    step = sb("step", [P, E], F32)
    part = sb("part", [P, NT * TOPK], F32)
    slot = [sb(f"slot{p}", [P, NT * TOPK], F32) for p in (0, 1)]
    index = sb("index", [1, ET], F32)
    past = sb("past", [1, ET, E], F32)
    past_tiles = sb("past_tiles", [1, ET, E], F32)
    expert, first, offset, start = (sb(n, [1, ET], F32) for n in ("expert", "first", "offset", "start"))
    s_pool = sems.enter_context(nc.semaphore("s_pool"))
    s_cnt = sems.enter_context(nc.semaphore("s_cnt"))
    s_v = sems.enter_context(nc.semaphore("s_v"))
    s_tail = sems.enter_context(nc.semaphore("s_tail"))

    def pool(eng):
        eng.iota(index[:], pattern=[[1, ET]], base=0, channel_multiplier=0,
                 allow_small_or_imprecise_dtypes=True).then_inc(s_pool, 1)
        eng.iota(base[:], pattern=[[REG, E]], base=0, channel_multiplier=0,
                 allow_small_or_imprecise_dtypes=True).then_inc(s_pool, 1)
        eng.memset(zeros[:], 0.0).then_inc(s_pool, 1)

    def tensor(eng):
        eng.matmul(cnt, kept["ones_b"][:], kept["seen"][NT % 2][:], start=True, stop=True).then_inc(s_cnt, 1)

    def vector(eng):
        n = 0

        def link(ins):
            nonlocal n
            n += 1
            ins.then_inc(s_v, 1)
            eng.wait_ge(s_v, n)

        eng.wait_ge(s_cnt, 1)
        eng.wait_ge(s_pool, 2)
        link(eng.tensor_scalar(cnt_i[:], cnt, 1.0, float(P - 1), ALU.max, ALU.add))
        link(eng.tensor_tensor(rows_i[:, 1, :], cnt, base[:], ALU.add))
        link(eng.tensor_scalar(rows_i[:, 0, :], cnt_i[:], P.bit_length() - 1, None, ALU.arith_shift_right))
        link(eng.tensor_copy(tiles[:], rows_i[:, 0, :]))
        link(eng.tensor_copy(ends[:, 0:1], tiles[:, 0:1]))
        for e in range(1, E):
            link(eng.tensor_tensor(ends[:, e:e + 1], ends[:, e - 1:e], tiles[:, e:e + 1], ALU.add))
        of_tiles = index[:].unsqueeze(2).broadcast_to([1, ET, E])
        link(eng.tensor_tensor(past[:], of_tiles, ends[0:1, :].unsqueeze(1).broadcast_to([1, ET, E]), ALU.is_ge))
        link(eng.tensor_reduce(expert[:], past[:], AX, ALU.add))
        link(eng.tensor_tensor(past_tiles[:], past[:], tiles[0:1, :].unsqueeze(1).broadcast_to([1, ET, E]),
                               ALU.mult))
        link(eng.tensor_reduce(first[:], past_tiles[:], AX, ALU.add))
        link(eng.tensor_tensor(offset[:], index[:], first[:], ALU.subtract))
        link(eng.tensor_scalar(start[:], expert[:], float(REG), None, ALU.mult))
        link(eng.scalar_tensor_tensor(table[:, 0, :], offset[:], float(P), start[:], ALU.mult, ALU.add))
        link(eng.tensor_scalar(table[:, 1, :], expert[:], float(E - 1), None, ALU.min))
        link(eng.tensor_copy(kept["ends"][:], ends[0:1, :]))
        assert n == TABLE
        link(eng.tensor_tensor(moved[:], ends[:], tiles[:], ALU.subtract))
        link(eng.scalar_tensor_tensor(moved[:], moved[:], float(P), base[:], ALU.mult, ALU.subtract))
        link(eng.tensor_copy(step[:, 0:1], moved[:, 0:1]))
        link(eng.tensor_tensor(step[:, 1:E], moved[:, 1:E], moved[:, 0:E - 1], ALU.subtract))
        dest = kept["dest_all"][:].rearrange("p t k -> p (t k)")
        link(eng.tensor_copy(slot[0][:], dest))
        for e in range(E):
            a, b = e % 2, 1 - e % 2
            link(eng.tensor_scalar(part[:], dest, float(e * REG), step[:, e:e + 1], ALU.is_ge, ALU.mult))
            link(eng.tensor_tensor(slot[b][:], slot[a][:], part[:], ALU.add))
        link(eng.tensor_copy(kept["slot_all"][:].rearrange("p t k -> p (t k)"), slot[E % 2][:]))

    def sync(eng):
        eng.wait_ge(s_pool, 3)
        eng.wait_ge(s_v, 2)
        for e in range(E):
            row = eng.value_load(rows_i[0:1, 1, e:e + 1], min_val=e * REG, max_val=e * REG + TOK)
            eng.dma_start(rows_d[bass.ds(row, P), :], zeros[:]).then_inc(s_tail, 16)
        eng.wait_ge(s_tail, 16 * E)

    TABLE = 5 + E - 1 + 9

    def planned(eng):
        eng.wait_ge(s_v, TABLE)

    return {"pool": pool, "tensor": tensor, "vector": vector, "sync": sync, "planned": planned}


def routed(nc, sems, kept, weights, ahead, rows_d, y_d):
    with ExitStack() as ctx:
        def sb(name, shape, dt):
            return ctx.enter_context(nc.sbuf_tensor(name, shape, dt))

        def pair(name, shape, dt):
            return [sb(f"{name}{p}", shape, dt) for p in (0, 1)]

        def count(name, **kw):
            return Count(sems, nc, name, **kw)

        ident_b = kept["ident_b"]
        wu, wd, wd_tail = weights.up, weights.down, weights.tail
        table = sb("table", [1, 2, ET], I32)
        g = pair("g", [P, D], BF16)
        gt = pair("gt", [P, DC, P], BF16)
        sil = sb("sil", [P, HID], F32)
        h = pair("h", [P, HID], BF16)
        ht = pair("ht", [P, HC, P], BF16)
        y = pair("y", [P, D], BF16)
        up_ps = ctx.enter_context(nc.psum_tensor("up_ps", [P, 4, 512], F32))
        down_ps = ctx.enter_context(nc.psum_tensor("down_ps", [P, D], F32))
        gt_ps = ctx.enter_context(nc.psum_tensor("gt_ps", [P, DC, P], BF16))
        ht_ps = ctx.enter_context(nc.psum_tensor("ht_ps", [P, DC, P], BF16))
        steps = plan(nc, sems, ctx, kept, down_ps[:, 0:E], table, rows_d)

        g_w = sems.enter_context(nc.semaphore("g_w"))
        d_g, d_y = Loads(sems, nc, "d_g"), Loads(sems, nc, "d_y")
        p_gt = count("p_gt")
        a_gt = count("a_gt")
        p_up = count("p_up")
        a_sil = count("a_sil", per=2)
        v_h = count("v_h", per=2)
        p_ht = count("p_ht")
        v_ht = count("v_ht", per=2)
        p_dn = count("p_dn")
        a_y = count("a_y")
        v_y = count("v_y")

        with nc.Block() as block:
            @block.gpsimd
            def _(eng):
                steps["pool"](eng)
                p_gt.wait(eng, 1)
                weights.load_up(eng, 1)
                weights.load_down(eng, 1)
                steps["planned"](eng)
                for e in range(E):
                    if e >= 2:
                        last = eng.value_load(kept["ends"][0:1, e - 2:e - 1], min_val=0, max_val=ET)
                        for used, load in ((p_up, weights.load_up), (p_dn, weights.load_down)):
                            eng.wait_ge(used.sem, last + used.lead)
                            settled(eng, kept["spare"])
                            load(eng, e)
                    for part in (weights.d_up, weights.d_down):
                        weights.wait(eng, part, e)
                        eng.sem_inc(g_w, 1)

            @block.sync
            def _(eng):
                for s in (d_g, ahead.d_raw, ahead.d_xt):
                    s.prime(eng)
                steps["sync"](eng)
                steps["planned"](eng)

                def step(now, on):
                    if "g" in on:
                        t = now + 3
                        p_gt.wait(eng, t.at - 2)
                        settled(eng, kept["spare"])
                        row = eng.value_load(table[0:1, 0, bass.ds(t.at, 1)], min_val=0, max_val=GROWS - P)
                        d_g.inc(eng.dma_start(g[t.par][:], rows_d[bass.ds(row, P), :]), t)
                    if "y" in on:
                        t = now - 1
                        a_y.wait(eng, t.at)
                        v_y.wait(eng, t.at)
                        d_y.inc(eng.dma_start(y_d[bass.ts(t.at, P), :], y[t.par][:]), t)

                    if "raw" in on:
                        ahead.load(eng, now - 6)

                pipeline(eng, {"g": (3, 0, ET), "y": (-1, 0, ET), "raw": (-6, 0, DC)}, step)
                for t in (0, 1):
                    ahead.load_rows(eng, Tile(0, t))
                    ahead.load(eng, Tile(DC // 2, t))
                for t in (ET - 2, ET - 1):
                    d_y.wait(eng, Tile(t // 2, t % 2))

            @block.scalar
            def _(eng):
                for s in (a_gt, a_sil, a_y, ahead.a_hi):
                    s.prime(eng)

                def step(now, on):
                    if "gt" in on:
                        t = now + 1
                        p_gt.wait(eng, t.at)
                        p_up.wait(eng, t.at - 2)
                        a_gt.inc(eng.copy(gt[t.par][:], gt_ps[:]))
                    if "up" in on:
                        t = now
                        p_up.wait(eng, t.at)
                        for i in (0, 1):
                            v_h.wait(eng, t.at - 1, i + 1)
                            a_sil.inc(eng.activation(sil[:, i * HALF:(i + 1) * HALF], up_ps[:, i, 0:HALF], ACT.Silu))
                    if "y" in on:
                        t = now - 1
                        p_dn.wait(eng, t.at)
                        d_y.wait(eng, t - 2)
                        a_y.inc(eng.copy(y[t.par][:, 0:512], down_ps[:, 0:512]))

                    if "wh" in on:
                        ahead.high(eng, now - 8)

                pipeline(eng, {"gt": (1, 0, ET), "up": (0, 0, ET), "y": (-1, 0, ET), "wh": (-8, 0, DC)}, step)

            @block.vector
            def _(eng):
                for s in (v_h, v_ht, v_y, d_y, ahead.v_lo):
                    s.prime(eng)
                steps["vector"](eng)

                def step(now, on):
                    if "ht" in on:
                        t = now - 1
                        p_ht.wait(eng, t.at)
                        p_dn.wait(eng, t.at - 2)
                        v_ht.inc(eng.tensor_copy(ht[t.par][:, 0:HC - 1, :], ht_ps[:, 0:HC - 1, :]))
                        v_ht.inc(eng.tensor_copy(ht[t.par][0:HTAIL, HC - 1, :], ht_ps[0:HTAIL, HC - 1, :]))
                    if "up" in on:
                        t = now
                        p_ht.wait(eng, t.at - 2)
                        for i in (0, 1):
                            a_sil.wait(eng, t.at, i + 1)
                            v_h.inc(eng.tensor_tensor(h[t.par][:, i * HALF:(i + 1) * HALF],
                                                      sil[:, i * HALF:(i + 1) * HALF], up_ps[:, 2 + i, 0:HALF],
                                                      ALU.mult))
                    if "y" in on:
                        t = now - 1
                        p_dn.wait(eng, t.at)
                        d_y.wait(eng, t - 2)
                        v_y.inc(eng.tensor_copy(y[t.par][:, 512:], down_ps[:, 512:]))

                    if "wl" in on:
                        ahead.low(eng, now - 8)

                pipeline(eng, {"ht": (-1, 0, ET), "up": (0, 0, ET), "y": (-1, 0, ET), "wl": (-8, 0, DC)}, step)

            @block.tensor
            def _(eng):
                for s in (p_gt, p_up, p_ht, p_dn):
                    s.prime(eng)
                steps["tensor"](eng)
                steps["planned"](eng)

                def step(now, on):
                    if "gt" in on:
                        t = now + 1
                        d_g.wait(eng, t)
                        a_gt.wait(eng, t.at - 1)
                        for c in range(DC):
                            ins = eng.transpose(gt_ps[:, c, :], g[t.par][:, c * P:(c + 1) * P], ident_b[:])
                        p_gt.inc(ins)
                    if "up" in on:
                        t = now
                        expert = eng.value_load(table[0:1, 1, bass.ds(t.at, 1)], min_val=0, max_val=E - 1)
                        buf = expert & 1
                        eng.wait_ge(g_w, expert * 2 + 1)
                        a_gt.wait(eng, t.at)
                        v_h.wait(eng, t.at - 1)
                        for c in range(DC):
                            for i in range(4):
                                ins = eng.matmul(up_ps[:, i, 0:HALF], gt[t.par][:, c, :],
                                                 wu[:, buf, c, i * HALF:(i + 1) * HALF], start=c == 0,
                                                 stop=c == DC - 1)
                        p_up.inc(ins)
                    if "dn" in on:
                        t = now - 1
                        expert = eng.value_load(table[0:1, 1, bass.ds(t.at, 1)], min_val=0, max_val=E - 1)
                        buf = expert & 1
                        eng.wait_ge(g_w, expert * 2 + 2)
                        v_ht.wait(eng, t.at)
                        a_y.wait(eng, t.at - 1)
                        v_y.wait(eng, t.at - 1)
                        for c in range(HC):
                            k = P if c < HC - 1 else HTAIL
                            for i in (0, 1):
                                w = wd[:, buf, c] if c < HC - 1 else wd_tail[:, buf]
                                ins = eng.matmul(down_ps[:, i * 512:(i + 1) * 512], ht[t.par][0:k, c, :],
                                                 w[:, i * 512:(i + 1) * 512], start=c == 0, stop=c == HC - 1)
                        p_dn.inc(ins)
                    if "up" in on:
                        t = now
                        v_h.wait(eng, t.at)
                        v_ht.wait(eng, t.at - 1)
                        for c in range(HC):
                            k = P if c < HC - 1 else HTAIL
                            ins = eng.transpose(ht_ps[0:k, c, :], h[t.par][:, c * P:c * P + k], ident_b[:])
                        p_ht.inc(ins)

                pipeline(eng, {"gt": (1, 0, ET), "up": (0, 0, ET), "dn": (-1, 0, ET)}, step, unroll=4)


def shared(nc, sems, kept, ahead, x1_d, y_d, out):
    with ExitStack() as ctx:
        def sb(name, shape, dt):
            return ctx.enter_context(nc.sbuf_tensor(name, shape, dt))

        def pair(name, shape, dt):
            return [sb(f"{name}{p}", shape, dt) for p in (0, 1)]

        def count(name, **kw):
            return Count(sems, nc, name, **kw)

        ident_f, slot_all = kept["ident_f"], kept["slot_all"]
        wu_h, wu_l, xt_f, d_xt = ahead.up_h, ahead.up_l, ahead.xt, ahead.d_xt
        wd_h, wd_l = ahead.down_h, ahead.down_l
        x1 = pair("sx1", [P, D], F32)
        xt_h, xt_l = ahead.xt_h, ahead.xt_l
        sil = sb("ssil", [P, HID], F32)
        h = sb("sh", [P, HC * P], F32)
        ht_h, ht_l = sb("ht_h", [P, HC, P], F32R), sb("ht_l", [P, HC - 1, P], F32R)
        idx = [pair("idx0_", [P, 1], I32), pair("idx1_", [P, 1], I32)]
        yr = [sb("yr0", [P, D], BF16), sb("yr1", [P, D], BF16)]
        o = sb("so", [P, D], F32)
        up_ps = ctx.enter_context(nc.psum_tensor("sup_ps", [P, 4, 512], F32))
        down_ps = ctx.enter_context(nc.psum_tensor("sdown_ps", [P, D], F32))
        t_ps = ctx.enter_context(nc.psum_tensor("st_ps", [P, D], F32))

        d_x1 = Loads(sems, nc, "d_sx1")
        d_yr = Loads(sems, nc, "d_yr", n=TOPK, lead=0)
        d_o = Loads(sems, nc, "d_o")
        v_idx = count("v_idx", per=2)
        a_xt, v_xt = count("a_sxt"), count("v_sxt")
        p_up = count("p_sup")
        a_sil = count("a_ssil", per=2)
        v_h = count("v_sh", per=3)
        p_ht = count("p_sht")
        a_ht, v_ht = count("a_sht", per=2), count("v_sht", per=2)
        p_dn = count("p_sdn")
        v_o = count("v_o", per=3)

        down_chunks = [Tile(n // 2, n % 2) for n in range(DC, DC + HC)]

        with nc.Block() as block:
            @block.sync
            def _(eng):
                d_x1.prime(eng)

                def step(now, on):
                    if "xt" in on:
                        t = now + 3
                        v_xt.wait(eng, t.at - 2)
                        ahead.load_rows(eng, t)
                    if "x1" in on:
                        t = now + 1
                        v_o.wait(eng, t.at - 2)
                        settled(eng, kept["spare"])
                        d_x1.inc(eng.dma_start(x1[t.par][:], x1_d[bass.ts(t.at, P), :]), t)
                    if "wd" in on:
                        for n in down_chunks[2:]:
                            ahead.load(eng, n)
                    if "o" in on:
                        t = now - 1
                        v_o.wait(eng, t.at)
                        d_o.inc(eng.dma_start(out[t.at], o[:]), t)

                pipeline(eng, {"xt": (3, 2, NT), "x1": (1, 0, NT), "wd": (1, 0, 1), "o": (-1, 0, NT)}, step)
                for t in (NT - 2, NT - 1):
                    d_o.wait(eng, Tile(t // 2, t % 2))

            @block.gpsimd
            def _(eng):
                def step(now, on):
                    t = now
                    v_idx.wait(eng, t.at)
                    v_o.wait(eng, t.at - 1)
                    for k in range(TOPK):
                        settled(eng, kept["spare"])
                        d_yr.inc(eng.indirect_dma_start(
                            yr[k][:], None, y_d, bass.IndirectOffsetOnAxis(ap=idx[k][t.par][:, 0:1], axis=0)), t)

                pipeline(eng, {"y": (0, 0, NT)}, step)

            @block.scalar
            def _(eng):
                for s in (a_xt, a_sil, a_ht):
                    s.prime(eng)

                def step(now, on):
                    if "xt" in on:
                        t = now + 1
                        d_xt.wait(eng, t)
                        p_up.wait(eng, t.at - 2)
                        a_xt.inc(eng.copy(xt_h[t.par][:], xt_f[t.par][:]))
                    if "wd" in on:
                        for n in down_chunks:
                            ahead.high(eng, n)
                    if "up" in on:
                        t = now
                        p_up.wait(eng, t.at)
                        for i in (0, 1):
                            v_h.wait(eng, t.at - 1, 1 + 2 * i)
                            a_sil.inc(eng.activation(sil[:, i * HALF:(i + 1) * HALF], up_ps[:, i, 0:HALF], ACT.Silu))
                        p_ht.wait(eng, t.at)
                        p_dn.wait(eng, t.at - 1)
                        a_ht.inc(eng.copy(ht_h[:, 0:HC - 1, :], t_ps[:, 0:(HC - 1) * P]))
                        a_ht.inc(eng.copy(ht_h[:, HC - 1, :], t_ps[:, (HC - 1) * P:HC * P]))

                pipeline(eng, {"xt": (1, 0, NT), "wd": (0, 0, 1), "up": (0, 0, NT)}, step)

            @block.vector
            def _(eng):
                for s in (v_idx, v_xt, v_h, v_ht, v_o, d_o):
                    s.prime(eng)

                def step(now, on):
                    if "idx" in on:
                        t = now
                        if "sent" in on:
                            d_yr.wait(eng, t - 2)
                        for k in range(TOPK):
                            v_idx.inc(eng.tensor_copy(idx[k][t.par][:], slot_all[:, bass.ds(t.at, 1), k]))
                    if "xt" in on:
                        t = now + 1
                        a_xt.wait(eng, t.at)
                        v_xt.inc(eng.tensor_tensor(xt_l[t.par][:].rearrange("p c n -> p (c n)"),
                                                   xt_f[t.par][:],
                                                   xt_h[t.par][:].rearrange("p c n -> p (c n)").bitcast(F32),
                                                   ALU.subtract))
                    if "wd" in on:
                        for n in down_chunks:
                            ahead.low(eng, n)
                    if "up" in on:
                        t = now
                        p_ht.wait(eng, t.at - 1)
                        for i in (0, 1):
                            a_sil.wait(eng, t.at, i + 1)
                            v_h.inc(eng.tensor_tensor(h[:, i * HALF:(i + 1) * HALF],
                                                      sil[:, i * HALF:(i + 1) * HALF], up_ps[:, 2 + i, 0:HALF],
                                                      ALU.mult))
                        v_h.inc(eng.tensor_tensor(h[:, HID:HC * P], sil[:, HID - HTAIL:HID],
                                                  up_ps[:, 3, HALF - HTAIL:HALF], ALU.mult))
                        a_ht.wait(eng, t.at)
                        v_ht.inc(eng.tensor_tensor(
                            ht_l[:, 0:HC - 1, :].rearrange("p c n -> p (c n)"), t_ps[:, 0:(HC - 1) * P],
                            ht_h[:, 0:HC - 1, :].rearrange("p c n -> p (c n)").bitcast(F32), ALU.subtract))
                        v_ht.inc(eng.tensor_tensor(ht_h[HTAIL:P, HC - 1, :], t_ps[HTAIL:P, (HC - 1) * P:HC * P],
                                                   ht_h[HTAIL:P, HC - 1, :].bitcast(F32), ALU.subtract))
                    if "o" in on:
                        t = now - 1
                        p_dn.wait(eng, t.at)
                        d_yr.wait(eng, t)
                        d_o.wait(eng, t - 1)
                        v_o.inc(eng.tensor_tensor(o[:], down_ps[:], yr[0][:], ALU.add))
                        v_o.wait(eng, t.at, 1)
                        v_o.inc(eng.tensor_tensor(o[:], o[:], yr[1][:], ALU.add))
                        v_o.wait(eng, t.at, 2)
                        d_x1.wait(eng, t)
                        v_o.inc(eng.tensor_tensor(o[:], o[:], x1[t.par][:], ALU.add))

                pipeline(eng, {"idx": (0, 0, NT), "sent": (-2, 0, NT), "xt": (1, 0, NT),
                               "wd": (0, 0, 1), "o": (-1, 0, NT), "up": (0, 0, NT)}, step)

            @block.tensor
            def _(eng):
                for s in (p_up, p_ht, p_dn):
                    s.prime(eng)

                def up(t):
                    for c in range(DC):
                        for x, w in ((xt_h, wu_h), (xt_h, wu_l), (xt_l, wu_h)):
                            for i in range(4):
                                ins = eng.matmul(up_ps[:, i, 0:HALF], x[t.par][:, c, :],
                                                 w[:, c, i * HALF:(i + 1) * HALF],
                                                 start=c == 0 and x is xt_h and w is wu_h,
                                                 stop=c == DC - 1 and x is xt_l)
                    return ins

                def step(now, on):
                    if "up" in on:
                        t = now
                        v_xt.wait(eng, t.at)
                        v_h.wait(eng, t.at - 1)
                        p_up.inc(up(t))
                    if "dn" in on:
                        t = now - 1
                        if isinstance(t.at, int) and t.at == 0:
                            ahead.v_lo.wait(eng, DC + HC - 1)
                        v_ht.wait(eng, t.at)
                        v_o.wait(eng, t.at - 1, 1)
                        passes = [(x, w, c, P) for c in range(HC - 1)
                                  for x, w in ((ht_h, wd_h), (ht_h, wd_l), (ht_l, wd_h))]
                        passes += [(ht_h, wd_h, HC - 1, P), (ht_h, wd_l, HC - 1, HTAIL)]
                        for n, (x, w, c, k) in enumerate(passes):
                            for i in (0, 1):
                                ins = eng.matmul(down_ps[:, i * 512:(i + 1) * 512], x[0:k, c, :],
                                                 w[0:k, c, i * 512:(i + 1) * 512],
                                                 start=n == 0, stop=n == len(passes) - 1)
                        p_dn.inc(ins)
                    if "up" in on:
                        t = now
                        v_h.wait(eng, t.at)
                        v_ht.wait(eng, t.at - 1)
                        for c in range(HC):
                            ins = eng.transpose(t_ps[:, c * P:(c + 1) * P], h[:, c * P:(c + 1) * P], ident_f[:])
                        p_ht.inc(ins)

                pipeline(eng, {"up": (0, 0, NT), "dn": (-1, 0, NT)}, step)


def layout(a, chunk=P):
    return np.ascontiguousarray(a.reshape(-1, chunk, a.shape[-1]).transpose(1, 0, 2))


def kernel(x, ctx_1024, L0_xattn_Wq, L0_xattn_bq, L0_xattn_Wk, L0_xattn_bk, L0_ffn_gate_w, L0_ffn_w1, L0_ffn_w2,
           L0_ffn_w3, L0_ffn_sw1, L0_ffn_sw2, L0_ffn_sw3, L0_ffn_expert_bias):
    import concourse.bacc as bacc
    from concourse.bass_utils import run_bass_kernel_spmd

    up = np.concatenate([L0_ffn_w1, L0_ffn_w3], axis=1)
    sup = np.concatenate([L0_ffn_sw1, L0_ffn_sw3], axis=0)
    inputs = {
        "x": np.ascontiguousarray(x.reshape(NT, P, D)),
        "ctxt": np.ascontiguousarray(ctx_1024.reshape(TOK // GROUP, GROUP, CC, P).transpose(0, 3, 2, 1)),
        "wq": layout(L0_xattn_Wq.T), "wk": layout(L0_xattn_Wk.T),
        "bq": L0_xattn_bq.reshape(DH, 1), "bk": L0_xattn_bk.reshape(DH, 1),
        "gate_w": layout(L0_ffn_gate_w.T), "ebias": L0_ffn_expert_bias.reshape(1, E),
        "w13": np.ascontiguousarray(up.reshape(E, 2 * HID, DC, P).transpose(0, 3, 2, 1)),
        "w2": np.ascontiguousarray(L0_ffn_w2.transpose(0, 2, 1)),
        "sw13": np.ascontiguousarray(sup.reshape(2 * HID, DC, P).transpose(2, 1, 0)),
        "sw2": np.concatenate([L0_ffn_sw2.T, L0_ffn_sw2.T[HID - HTAIL:]]).reshape(HC, P, D),
    }
    nc = bacc.Bacc("TRN2", target_bir_lowering=False, num_devices=1, dynamic_dma_scratch_size=DMA_RING)
    args = []
    for name, a in inputs.items():
        args.append(nc.dram_tensor(f"in_{name}", a.shape, mybir.dt.from_np(a.dtype), kind="ExternalInput").ap())
    out = nc.dram_tensor("out", [NT, P, D], F32, kind="ExternalOutput").ap()
    build(nc, *args, out)
    r = run_bass_kernel_spmd(nc, [{f"in_{n}": a for n, a in inputs.items()}], core_ids=[0])
    return r.results[0]["out"].reshape(B, L, D)
```
